# Optimizing a Trainium2 kernel written in Bass

```python
import numpy as np
import jax
import jax.numpy as jnp

def _softmax(x, axis=-1):
    return jax.nn.softmax(x, axis=axis)

def _gelu(x):
    return jax.nn.gelu(x, approximate=True)

def _silu(x):
    return jax.nn.silu(x)

def _sigmoid(x):
    return jax.nn.sigmoid(x)

def _layernorm(x, axis=-1, eps=1e-05):
    m = jnp.mean(x, axis=axis, keepdims=True)
    v = jnp.var(x, axis=axis, keepdims=True)
    return (x - m) / jnp.sqrt(v + eps)

def _scatter_add(tgt, idx, src, axis=0):
    return tgt.at[idx].add(src)

def _segment_sum(src, seg, n):
    return jax.ops.segment_sum(src, seg, n)
kernel_name = 'mk_adaln_d1_jaxref_r4_4af3e9'

def setup_inputs(seed: int=0):
    np.random.seed(seed)
    _w = jnp.asarray

    def _L0_attn_setup():
        import jax, jax.numpy as jnp
        import numpy as np
        B, S, E = (4, 512, 256)
        H, KVH = (16, 4)
        D = E // H
        QL, KVL = (64, 32)
        ROPE_BASE = 10000.0

        def _rope(x):
            d = x.shape[-1]
            inv_freq = 1.0 / ROPE_BASE ** (jnp.arange(0, d, 2, dtype=jnp.float32) / d)
            t = jnp.arange(x.shape[1], dtype=jnp.float32)
            freqs = jnp.outer(t, inv_freq)
            cos = jnp.cos(freqs)[None, :, None, :].astype(x.dtype)
            sin = jnp.sin(freqs)[None, :, None, :].astype(x.dtype)
            x1, x2 = (x[..., ::2], x[..., 1::2])
            r1 = x1 * cos - x2 * sin
            r2 = x1 * sin + x2 * cos
            return jnp.stack([r1, r2], axis=-1).reshape(x.shape)
        key = jax.random.key(seed)
        ks = jax.random.split(key, 7)
        s = 0.02
        return {'x': jax.random.normal(ks[0], (B, S, E), dtype=jnp.float32), 'Wqa': jax.random.normal(ks[1], (E, QL), dtype=jnp.float32) * s, 'Wqb': jax.random.normal(ks[2], (QL, E), dtype=jnp.float32) * s, 'Wkva': jax.random.normal(ks[3], (E, KVL), dtype=jnp.float32) * s, 'Wkvb': jax.random.normal(ks[4], (KVL, KVH * D * 2), dtype=jnp.float32) * s, 'Wout': jax.random.normal(ks[5], (E, E), dtype=jnp.float32) * s, 'bout': jax.random.normal(ks[6], (E,), dtype=jnp.float32) * s}
    _L0_attn_in = _L0_attn_setup()

    def _L0_ffn_setup():
        import jax, jax.numpy as jnp
        import numpy as np
        import math
        D = 256
        H = 16
        E = 8
        TOPK = 2
        LAT = D // 2
        KPH = LAT // H
        HD = D // H

        def _forward(hs, q_w, q_b, k_w, k_b, v_w, v_b, o_w, o_b, router_w, router_b, w1, b1, w2, b2):
            B, S, _ = hs.shape
            Q = (hs @ q_w + q_b).reshape(B, S, H, HD).transpose(0, 2, 1, 3)
            K = (hs @ k_w + k_b).reshape(B, S, H, KPH).transpose(0, 2, 1, 3)
            V = (hs @ v_w + v_b).reshape(B, S, H, KPH).transpose(0, 2, 1, 3)
            scores = jnp.einsum('bhsk,bhtk->bhst', Q[..., :KPH], K) / math.sqrt(KPH)
            attn = jax.nn.softmax(scores, axis=-1)
            ao = jnp.einsum('bhst,bhtv->bhsv', attn, V)
            ao = ao.transpose(0, 2, 1, 3).reshape(B, S, H * KPH)
            ao = jnp.concatenate([ao, jnp.zeros((B, S, D - LAT), ao.dtype)], axis=-1)
            mla_out = ao @ o_w + o_b
            probs = jax.nn.softmax(mla_out @ router_w + router_b, axis=-1)
            topw, topi = jax.lax.top_k(probs, TOPK)
            topw = topw / (topw.sum(-1, keepdims=True) + 1e-08)
            combine = jnp.sum(jax.nn.one_hot(topi, E, dtype=probs.dtype) * topw[..., None], axis=-2)
            h1 = jnp.einsum('bsd,edf->ebsf', mla_out, w1) + b1[:, None, None, :]
            h1 = jax.nn.gelu(h1, approximate=False)
            h2 = jnp.einsum('ebsf,efd->ebsd', h1, w2) + b2[:, None, None, :]
            moe_out = jnp.einsum('bse,ebsd->bsd', combine, h2)
            return hs + 0.3 * moe_out
        key = jax.random.key(seed)
        ks = jax.random.split(key, 16)
        s = 0.02
        inp = {'hidden_states': jax.random.normal(ks[0], (2, 512, D), jnp.float32), 'q_w': jax.random.normal(ks[1], (D, D), jnp.float32) * s, 'q_b': jnp.zeros((D,), jnp.float32), 'k_w': jax.random.normal(ks[2], (D, LAT), jnp.float32) * s, 'k_b': jnp.zeros((LAT,), jnp.float32), 'v_w': jax.random.normal(ks[3], (D, LAT), jnp.float32) * s, 'v_b': jnp.zeros((LAT,), jnp.float32), 'o_w': jax.random.normal(ks[4], (D, D), jnp.float32) * s, 'o_b': jnp.zeros((D,), jnp.float32), 'router_w': jax.random.normal(ks[5], (D, E), jnp.float32) * s, 'router_b': jnp.zeros((E,), jnp.float32), 'w1': jax.random.normal(ks[6], (E, D, 2 * D), jnp.float32) * s, 'b1': jnp.zeros((E, 2 * D), jnp.float32), 'w2': jax.random.normal(ks[7], (E, 2 * D, D), jnp.float32) * s, 'b2': jnp.zeros((E, D), jnp.float32)}
        return inp
    _L0_ffn_in = _L0_ffn_setup()
    _L0_c = _w((lambda *s: np.random.randn(*s).astype(np.float32) * 0.05)(4, 256))
    _L0_wmod = _w((lambda *s: np.random.randn(*s).astype(np.float32) * 0.05)(256, 6 * 256) * 256 ** (-0.5))
    _d = {'L0_attn_x': _L0_attn_in['x'], 'L0_attn_Wqa': _L0_attn_in['Wqa'], 'L0_attn_Wqb': _L0_attn_in['Wqb'], 'L0_attn_Wkva': _L0_attn_in['Wkva'], 'L0_attn_Wkvb': _L0_attn_in['Wkvb'], 'L0_attn_Wout': _L0_attn_in['Wout'], 'L0_attn_bout': _L0_attn_in['bout'], 'L0_ffn_q_w': _L0_ffn_in['q_w'], 'L0_ffn_q_b': _L0_ffn_in['q_b'], 'L0_ffn_k_w': _L0_ffn_in['k_w'], 'L0_ffn_k_b': _L0_ffn_in['k_b'], 'L0_ffn_v_w': _L0_ffn_in['v_w'], 'L0_ffn_v_b': _L0_ffn_in['v_b'], 'L0_ffn_o_w': _L0_ffn_in['o_w'], 'L0_ffn_o_b': _L0_ffn_in['o_b'], 'L0_ffn_router_w': _L0_ffn_in['router_w'], 'L0_ffn_router_b': _L0_ffn_in['router_b'], 'L0_ffn_w1': _L0_ffn_in['w1'], 'L0_ffn_b1': _L0_ffn_in['b1'], 'L0_ffn_w2': _L0_ffn_in['w2'], 'L0_ffn_b2': _L0_ffn_in['b2'], 'L0_c': _L0_c, 'L0_wmod': _L0_wmod}
    _x0 = _d['L0_attn_x']
    _d['L0_attn_x'] = jax.random.normal(jax.random.fold_in(jax.random.key(seed), 1), (4, 1024, 256), dtype=_x0.dtype)
    del _x0
    return _d

def reference(L0_attn_x, L0_attn_Wqa, L0_attn_Wqb, L0_attn_Wkva, L0_attn_Wkvb, L0_attn_Wout, L0_attn_bout, L0_ffn_q_w, L0_ffn_q_b, L0_ffn_k_w, L0_ffn_k_b, L0_ffn_v_w, L0_ffn_v_b, L0_ffn_o_w, L0_ffn_o_b, L0_ffn_router_w, L0_ffn_router_b, L0_ffn_w1, L0_ffn_b1, L0_ffn_w2, L0_ffn_b2, L0_c, L0_wmod):

    def _L0_attn_ref(x, Wqa, Wqb, Wkva, Wkvb, Wout, bout):
        import jax, jax.numpy as jnp
        import numpy as np
        B, S, E = (4, 512, 256)
        H, KVH = (16, 4)
        D = E // H
        QL, KVL = (64, 32)
        ROPE_BASE = 10000.0

        def _rope(x):
            d = x.shape[-1]
            inv_freq = 1.0 / ROPE_BASE ** (jnp.arange(0, d, 2, dtype=jnp.float32) / d)
            t = jnp.arange(x.shape[1], dtype=jnp.float32)
            freqs = jnp.outer(t, inv_freq)
            cos = jnp.cos(freqs)[None, :, None, :].astype(x.dtype)
            sin = jnp.sin(freqs)[None, :, None, :].astype(x.dtype)
            x1, x2 = (x[..., ::2], x[..., 1::2])
            r1 = x1 * cos - x2 * sin
            r2 = x1 * sin + x2 * cos
            return jnp.stack([r1, r2], axis=-1).reshape(x.shape)
        b, s, _ = x.shape
        scale = D ** (-0.5)
        q = (x @ Wqa @ Wqb).reshape(b, s, H, D)
        kv = (x @ Wkva @ Wkvb).reshape(b, s, KVH, D, 2)
        k, v = (kv[..., 0], kv[..., 1])
        q = _rope(q)
        k = _rope(k)
        g = H // KVH
        k = jnp.repeat(k, g, axis=2)
        v = jnp.repeat(v, g, axis=2)
        scores = jnp.einsum('bqhd,bkhd->bhqk', q, k) * scale
        causal = jnp.triu(jnp.ones((s, s), dtype=bool), k=1)
        scores = jnp.where(causal[None, None], -jnp.inf, scores)
        w = jax.nn.softmax(scores, axis=-1)
        out = jnp.einsum('bhqk,bkhd->bqhd', w, v).reshape(b, s, E)
        return out @ Wout + bout

    def _L0_ffn_ref(hidden_states, q_w, q_b, k_w, k_b, v_w, v_b, o_w, o_b, router_w, router_b, w1, b1, w2, b2):
        import jax, jax.numpy as jnp
        import numpy as np
        import math
        D = 256
        H = 16
        E = 8
        TOPK = 2
        LAT = D // 2
        KPH = LAT // H
        HD = D // H

        def _forward(hs, q_w, q_b, k_w, k_b, v_w, v_b, o_w, o_b, router_w, router_b, w1, b1, w2, b2):
            B, S, _ = hs.shape
            Q = (hs @ q_w + q_b).reshape(B, S, H, HD).transpose(0, 2, 1, 3)
            K = (hs @ k_w + k_b).reshape(B, S, H, KPH).transpose(0, 2, 1, 3)
            V = (hs @ v_w + v_b).reshape(B, S, H, KPH).transpose(0, 2, 1, 3)
            scores = jnp.einsum('bhsk,bhtk->bhst', Q[..., :KPH], K) / math.sqrt(KPH)
            attn = jax.nn.softmax(scores, axis=-1)
            ao = jnp.einsum('bhst,bhtv->bhsv', attn, V)
            ao = ao.transpose(0, 2, 1, 3).reshape(B, S, H * KPH)
            ao = jnp.concatenate([ao, jnp.zeros((B, S, D - LAT), ao.dtype)], axis=-1)
            mla_out = ao @ o_w + o_b
            probs = jax.nn.softmax(mla_out @ router_w + router_b, axis=-1)
            topw, topi = jax.lax.top_k(probs, TOPK)
            topw = topw / (topw.sum(-1, keepdims=True) + 1e-08)
            combine = jnp.sum(jax.nn.one_hot(topi, E, dtype=probs.dtype) * topw[..., None], axis=-2)
            h1 = jnp.einsum('bsd,edf->ebsf', mla_out, w1) + b1[:, None, None, :]
            h1 = jax.nn.gelu(h1, approximate=False)
            h2 = jnp.einsum('ebsf,efd->ebsd', h1, w2) + b2[:, None, None, :]
            moe_out = jnp.einsum('bse,ebsd->bsd', combine, h2)
            return hs + 0.3 * moe_out
        return _forward(hidden_states, q_w, q_b, k_w, k_b, v_w, v_b, o_w, o_b, router_w, router_b, w1, b1, w2, b2)
    x = L0_attn_x
    mod = (_silu(L0_c) @ L0_wmod).reshape(L0_c.shape[0], 6, 1, -1)
    sa, ca, ga, sb, cb, gb = (mod[:, 0], mod[:, 1], mod[:, 2], mod[:, 3], mod[:, 4], mod[:, 5])
    ga = (2 * (ga >= 0) - 1) * jnp.maximum(jnp.abs(ga), 0.25)
    gb = (2 * (gb >= 0) - 1) * jnp.maximum(jnp.abs(gb), 0.25)
    h = _layernorm(x, axis=-1) * (1 + ca) + sa
    x = x + ga * _L0_attn_ref(h, L0_attn_Wqa, L0_attn_Wqb, L0_attn_Wkva, L0_attn_Wkvb, L0_attn_Wout, L0_attn_bout)
    h = _layernorm(x, axis=-1) * (1 + cb) + sb
    x = x + gb * _L0_ffn_ref(h, L0_ffn_q_w, L0_ffn_q_b, L0_ffn_k_w, L0_ffn_k_b, L0_ffn_v_w, L0_ffn_v_b, L0_ffn_o_w, L0_ffn_o_b, L0_ffn_router_w, L0_ffn_router_b, L0_ffn_w1, L0_ffn_b1, L0_ffn_w2, L0_ffn_b2)
    return x

_drawn_inputs = setup_inputs


def setup_inputs(seed=0):
    import zlib

    import numpy as np

    out = dict(_drawn_inputs(seed))
    spreads = {'L0_ffn_q_b': (0.0, 0.8),
     'L0_ffn_k_b': (0.0, 2.0),
     'L0_ffn_v_b': (0.0, 0.8),
     'L0_ffn_o_b': (0.0, 0.8),
     'L0_ffn_router_b': (0.0, 0.8),
     'L0_ffn_b1': (0.0, 0.8),
     'L0_ffn_b2': (0.0, 2.0)}
    factors = {'L0_attn_Wqa': 8.0,
     'L0_attn_Wqb': 8.0,
     'L0_attn_Wkva': 8.0,
     'L0_attn_Wkvb': 8.0,
     'L0_attn_Wout': 8.0,
     'L0_attn_bout': 8.0,
     'L0_ffn_q_w': 8.0,
     'L0_ffn_k_w': 8.0,
     'L0_ffn_v_w': 8.0,
     'L0_ffn_o_w': 8.0,
     'L0_ffn_router_w': 8.0,
     'L0_ffn_w1': 8.0,
     'L0_ffn_w2': 8.0}
    for name, (base, spread) in spreads.items():
        noise = np.random.default_rng([zlib.crc32(name.encode()), seed]).standard_normal(out[name].shape)
        drawn = base * np.exp(spread * noise) if base else spread * noise
        out[name] = jnp.asarray(drawn.astype(out[name].dtype))
    for name, factor in factors.items():
        out[name] = (out[name] * factor).astype(out[name].dtype)
    return out
```

```python
from contextlib import ExitStack

import numpy as np

import concourse.bass as bass
from concourse import mybir

F32 = mybir.dt.float32
F32R = mybir.dt.float32r
BF16 = mybir.dt.bfloat16
ALU = mybir.AluOpType
ACT = mybir.ActivationFunctionType
AX = mybir.AxisListType

P = 128
B, S, E = 4, 1024, 256
TOK = B * S
TILE = 512
TILES = TOK // TILE
TPB = S // TILE
BLK = TILE // P
EC = E // P
H, KVH = 16, 4
D1 = E // H
QL, KVL = 64, 32
D2 = 8
HQ = 4
UPB = H // HQ
NX, FF = 8, 512
FC = FF // P
EPS = 1e-5
FLOOR = 0.25
MASK = -1.0e30
LOW = -3.0e38
SA, CA, GA, SB, CB, GB, GB3 = range(7)
NMOD = 7


SIX = ((0, 0), (0, 1), (1, 0), (1, 1), (0, 2), (2, 0))
NINE = SIX + ((1, 2), (2, 1), (2, 2))


class Signal:

    def __init__(self, sem, per, credit=0):
        self.sem, self.per, self.credit = sem, per, credit

    def at(self, unit, steps):
        return (unit + self.credit) * self.per + steps

    def open(self, engine):
        engine.sem_inc(self.sem, self.credit * self.per)


def in_pairs(engine, units, body):
    with engine.Fori(0, units // 2 - 1) as i:
        body(i, False)
    body(units // 2 - 1, True)


class Program:

    def __init__(self, nc, ctx, a):
        self.nc, self.ctx, self.a = nc, ctx, a
        self.sems = 0
        self.bank = ctx.enter_context(nc.psum_tensor("bank", [P, 8, 512], F32))
        self.ident = ctx.enter_context(nc.sbuf_tensor("ident", [P, P], F32))
        self.ident16 = ctx.enter_context(nc.sbuf_tensor("ident16", [P, P], BF16))
        self.mask_kq = ctx.enter_context(nc.sbuf_tensor("mask_kq", [P, P], BF16))
        self.mask_qk = ctx.enter_context(nc.sbuf_tensor("mask_qk", [P, P], BF16))

        def dram(name, shape, dt):
            return nc.dram_tensor(name, shape, dt, kind="Internal").ap()

        self.mod_row = dram("mod_row", [B, NMOD, E], F32)
        self.mod_col = dram("mod_col", [B, P, NMOD * EC], F32)
        self.bias_col = dram("bias_col", [P, NX * (FC + EC)], F32)
        self.q1 = dram("q1", [3, E, TOK], BF16)
        self.k1 = dram("k1", [3, KVH * D1, TOK], BF16)
        self.q2 = dram("q2", [3, H * D2, TOK], BF16)
        self.k2 = dram("k2", [3, H * D2, TOK], BF16)
        self.v1 = dram("v1", [B, KVH, P, S // P, D1 + 1], F32)
        self.v2 = dram("v2", [B, UPB, P, S // P, HQ, D2 + 1], F32)
        self.o1 = dram("o1", [H * D1, TOK], F32)
        self.o2 = dram("o2", [H * D2, TOK], F32)
        self.den = [dram(f"den{n}", [H, TOK], F32) for n in (1, 2)]
        self.rden1 = dram("rden1", [H, D1, TOK], F32)
        self.rden2 = dram("rden2", [H, D2, TOK], F32)
        self.x1 = dram("x1", [TOK, E], F32)
        self.gh = dram("gh", [E, TOK], F32)
        self.mla = dram("mla", [2, E, TOK], F32)
        self.comb = dram("comb", [TILES, NX, TILE], F32)

    def sem(self, name):
        self.sems += 1
        return self.ctx.enter_context(self.nc.semaphore(name))

    def counter(self, name, per, credit=0):
        return Signal(self.sem(name), per, credit)


def modulation(pr):
    nc, a = pr.nc, pr.a
    with ExitStack() as ctx:
        def sb(name, shape, dt=F32):
            return ctx.enter_context(nc.sbuf_tensor(name, shape, dt))

        cT = sb("cT", [P, EC, B])
        sig = sb("sig", [P, EC, B])
        siluT = sb("siluT", [P, EC, B])
        wmod = sb("wmod", [P, EC, 6 * E])
        row = sb("row", [B, NMOD, E])
        sign = sb("sign", [B, 2, E])
        col = sb("col", [P, B, NMOD * EC])
        brow = sb("brow", [NX * (FC + EC), P])
        bcol = sb("bcol", [P, NX * (FC + EC)])

        loaded = pr.sem("m_loaded")
        made = pr.sem("m_made")
        neg_exp = pr.sem("m_neg_exp")
        silu = pr.sem("m_silu")
        summed = pr.sem("m_summed")
        rows = pr.sem("m_rows")
        turned = pr.sem("m_turned")
        cols = pr.sem("m_cols")
        stored = pr.sem("m_stored")
        raw = pr.bank[0:B, 0:3, :].rearrange("b n c -> b (n c)").rearrange("b (j e) -> b j e", e=E)

        with nc.Block() as block:
            @block.sync
            def _(sp):
                sp.dma_start(cT[:, 0, :], a["L0_c"][:, 0:P].rearrange("b p -> p b"),
                             allow_slow_non_contiguous=True).then_inc(loaded, 16)
                sp.dma_start(cT[:, 1, :], a["L0_c"][:, P:E].rearrange("b p -> p b"),
                             allow_slow_non_contiguous=True).then_inc(loaded, 16)
                sp.dma_start(wmod[:], a["L0_wmod"].rearrange("(k p) n -> p k n", p=P)).then_inc(loaded, 16)
                sp.dma_start(brow[0:NX * FC, :],
                             a["L0_ffn_b1"].rearrange("x (f p) -> (x f) p", p=P)).then_inc(loaded, 16)
                sp.dma_start(brow[NX * FC:NX * (FC + EC), :],
                             a["L0_ffn_b2"].rearrange("x (f p) -> (x f) p", p=P)).then_inc(loaded, 16)
                sp.wait_ge(rows, 12)
                sp.dma_start(pr.mod_row, row[:]).then_inc(stored, 16)
                sp.wait_ge(cols, 2)
                sp.dma_start(pr.mod_col.rearrange("b p c -> p b c"), col[:]).then_inc(stored, 16)
                sp.dma_start(pr.bias_col, bcol[:]).then_inc(stored, 16)
                sp.wait_ge(stored, 48)

            @block.gpsimd
            def _(pool):
                for m in (pr.ident, pr.ident16, pr.mask_kq, pr.mask_qk):
                    pool.memset(m[:], 0.0).then_inc(made, 1)
                pool.wait_ge(made, 4)
                for m in (pr.ident, pr.ident16):
                    pool.affine_select(out=m[:], in_=m[:], compare_op=ALU.not_equal, fill=1.0, base=0,
                                       pattern=[[-1, P]], channel_multiplier=1).then_inc(made, 1)
                pool.affine_select(out=pr.mask_kq[:], in_=pr.mask_kq[:], compare_op=ALU.is_ge, fill=MASK,
                                   base=0, pattern=[[1, P]], channel_multiplier=-1).then_inc(made, 1)
                pool.affine_select(out=pr.mask_qk[:], in_=pr.mask_qk[:], compare_op=ALU.is_ge, fill=MASK,
                                   base=0, pattern=[[-1, P]], channel_multiplier=1).then_inc(made, 1)

            @block.scalar
            def _(act):
                act.wait_ge(loaded, 80)
                act.activation(sig[:], cT[:], ACT.Exp, scale=-1.0).then_inc(neg_exp, 1)

            @block.vector
            def _(dve):
                dve.wait_ge(neg_exp, 1)
                dve.tensor_scalar(sig[:], sig[:], 1.0, None, ALU.add).then_inc(silu, 1)
                dve.wait_ge(silu, 1)
                dve.reciprocal(sig[:], sig[:]).then_inc(silu, 1)
                dve.wait_ge(silu, 2)
                dve.tensor_tensor(siluT[:], cT[:], sig[:], ALU.mult).then_inc(silu, 1)
                dve.wait_ge(summed, 1)
                for j, f in ((SA, None), (SB, None), (CA, 1.0), (CB, 1.0)):
                    if f is None:
                        dve.tensor_copy(row[:, j, :], raw[:, j, :]).then_inc(rows, 1)
                    else:
                        dve.tensor_scalar(row[:, j, :], raw[:, j, :], f, None, ALU.add).then_inc(rows, 1)
                for n, j in enumerate((GA, GB)):
                    dve.tensor_scalar(sign[:, n, :], raw[:, j, :], 0.0, 2.0, ALU.is_ge, ALU.mult).then_inc(rows, 1)
                dve.wait_ge(rows, 6)
                dve.tensor_scalar(sign[:], sign[:], -1.0, None, ALU.add).then_inc(rows, 1)
                dve.wait_ge(rows, 7)
                for n, j in enumerate((GA, GB)):
                    dve.tensor_tensor(row[:, j, :], raw[:, j, :], sign[:, n, :], ALU.mult).then_inc(rows, 1)
                dve.wait_ge(rows, 9)
                for n, j in enumerate((GA, GB)):
                    dve.scalar_tensor_tensor(out=row[:, j, :], in0=row[:, j, :], scalar=FLOOR,
                                             in1=sign[:, n, :], op0=ALU.max, op1=ALU.mult).then_inc(rows, 1)
                dve.wait_ge(rows, 11)
                dve.tensor_scalar(row[:, GB3, :], row[:, GB, :], 0.3, None, ALU.mult).then_inc(rows, 1)
                dve.wait_ge(turned, 1)
                dve.tensor_copy(col[:], pr.bank[:, 4, 0:NMOD * EC * B].rearrange("p (c b) -> p b c", b=B)).then_inc(cols, 1)
                dve.tensor_copy(bcol[:], pr.bank[:, 5, 0:NX * (FC + EC)]).then_inc(cols, 1)

            @block.tensor
            def _(pe):
                pe.wait_ge(silu, 3)
                for n in range(3):
                    for k in range(EC):
                        mm = pe.matmul(pr.bank[0:B, n, :], siluT[:, k, :], wmod[:, k, n * 512:(n + 1) * 512],
                                       start=(k == 0), stop=(k == EC - 1))
                mm.then_inc(summed, 1)
                pe.wait_ge(made, 8)
                pe.wait_ge(rows, 12)
                flat = row[:].rearrange("b j e -> b (j e)")
                for c in range(NMOD * EC):
                    pe.transpose(pr.bank[:, 4, c * B:(c + 1) * B], flat[:, c * P:(c + 1) * P], pr.ident[0:B, 0:B])
                n = NX * (FC + EC)
                pe.transpose(pr.bank[:, 5, 0:n], brow[:], pr.ident[0:n, 0:n]).then_inc(turned, 1)


class Norm:

    def __init__(self, pr, sb, name, shift, scale):
        self.pr, self.shift, self.scale = pr, shift, scale
        self.stats = sb(name + "_stats", [P, BLK, 6])
        self.mean = sb(name + "_mean", [P, BLK])
        self.diff = sb(name + "_diff", [P, BLK])
        self.var = sb(name + "_var", [P, BLK])
        self.rstd = sb(name + "_rstd", [P, BLK])
        self.power = sb(name + "_power", [P, BLK])
        self.xn = sb(name + "_xn", [P, BLK, E])
        self.hT = sb(name + "_hT", [P, EC, TILE])
        self.stat = pr.counter(name + "_stat", BLK + 6)
        self.var_ready = pr.counter(name + "_var_ready", 1)
        self.rstd_ready = pr.counter(name + "_rstd_ready", 1)
        self.xn_ready = pr.counter(name + "_xn_ready", 1)
        self.turned = pr.counter(name + "_turned", 1, credit=1)
        self.h_ready = pr.counter(name + "_h_ready", EC, credit=1)

    def open(self, engine, which):
        {"pe": self.turned, "act": self.h_ready}[which].open(engine)

    def dve(self, dve, n, x):
        for b in range(BLK):
            dve.bn_stats(self.stats[:, b, :], x[:, b, :]).then_inc(self.stat.sem, 1)
        even, odd = (self.stats[:, :, 1], self.stats[:, :, 2]), (self.stats[:, :, 4], self.stats[:, :, 5])
        sem, at = self.stat.sem, self.stat.at
        dve.wait_ge(sem, at(n, BLK))
        dve.tensor_tensor(self.mean[:], even[0], odd[0], ALU.add).then_inc(sem, 1)
        dve.tensor_tensor(self.diff[:], even[0], odd[0], ALU.subtract).then_inc(sem, 1)
        dve.tensor_tensor(self.var[:], even[1], odd[1], ALU.add).then_inc(sem, 1)
        dve.wait_ge(sem, at(n, BLK + 3))
        dve.tensor_scalar(self.mean[:], self.mean[:], 0.5, None, ALU.mult).then_inc(sem, 1)
        dve.tensor_scalar(self.var[:], self.var[:], 1.0 / E, EPS, ALU.mult, ALU.add).then_inc(sem, 1)
        dve.scalar_tensor_tensor(out=self.diff[:], in0=self.diff[:], scalar=0.25, in1=self.diff[:],
                                 op0=ALU.mult, op1=ALU.mult).then_inc(sem, 1)
        dve.wait_ge(sem, at(n, BLK + 6))
        dve.tensor_tensor(self.var[:], self.var[:], self.diff[:], ALU.add).then_inc(self.var_ready.sem, 1)
        dve.wait_ge(self.turned.sem, self.turned.at(n - 1, 1))
        dve.wait_ge(self.rstd_ready.sem, self.rstd_ready.at(n, 1))
        for b in range(BLK):
            op = dve.tensor_scalar(self.xn[:, b, :], x[:, b, :], self.mean[:, b:b + 1], self.rstd[:, b:b + 1],
                                   ALU.subtract, ALU.mult)
        op.then_inc(self.xn_ready.sem, 1)

    def pool(self, pool, n):
        pool.wait_ge(self.var_ready.sem, self.var_ready.at(n, 1))
        pool.tensor_tensor(self.rstd[:], self.var[:], self.power[:], ALU.pow).then_inc(self.rstd_ready.sem, 1)

    def pe(self, pe, n):
        pe.wait_ge(self.xn_ready.sem, self.xn_ready.at(n, 1))
        for c in range(EC):
            for b in range(BLK):
                mm = pe.transpose(self.pr.bank[:, c, b * P:(b + 1) * P], self.xn[:, b, c * P:(c + 1) * P],
                                  self.pr.ident[:])
        mm.then_inc(self.turned.sem, 1)

    def act(self, act, n, mod):
        act.wait_ge(self.turned.sem, self.turned.at(n, 1))
        for c in range(EC):
            sc, sh = self.scale * EC + c, self.shift * EC + c
            act.activation(self.hT[:, c, :], self.pr.bank[:, c, :], ACT.Identity,
                           bias=mod[:, sh:sh + 1], scale=mod[:, sc:sc + 1]).then_inc(self.h_ready.sem, 1)


def split_in_three(dve, sig, n, base, f, parts, rest):
    k = len(f)
    for i in range(k):
        dve.wait_ge(sig.sem, sig.at(n, base + i + 1 - k))
        dve.tensor_copy(parts[i][:, 0, :], f[i]).then_inc(sig.sem, 1)
    for j in (1, 2):
        for i in range(k):
            dve.wait_ge(sig.sem, sig.at(n, base + (2 * j - 2) * k + i + 1))
            dve.tensor_tensor(rest[i], f[i] if j == 1 else rest[i], parts[i][:, j - 1, :],
                              ALU.subtract).then_inc(sig.sem, 1)
        for i in range(k):
            dve.wait_ge(sig.sem, sig.at(n, base + (2 * j - 1) * k + i + 1))
            dve.tensor_copy(parts[i][:, j, :], rest[i]).then_inc(sig.sem, 1)


def from_x(pr):
    nc, a = pr.nc, pr.a
    R = slice(QL, QL + KVL)
    NK = KVH * D1
    with ExitStack() as ctx:
        def sb(name, shape, dt=F32):
            return ctx.enter_context(nc.sbuf_tensor(name, shape, dt))

        x = sb("p1_x", [P, 2, BLK, E])
        mod = sb("p1_mod", [P, 2, NMOD * EC])
        norm = Norm(pr, sb, "p1", SA, CA)
        wa = sb("p1_wa", [P, EC, QL + KVL])
        wq = sb("p1_wq", [QL, E])
        wq_turn = sb("p1_wq_turn", [QL, E])
        wkv = sb("p1_wkv", [QL + KVL, 2 * NK])
        wk = sb("p1_wk", [QL + KVL, NK])
        wk_turn = sb("p1_wk_turn", [QL + KVL, NK])
        wv = sb("p1_wv", [QL + KVL, NK])
        cos = sb("p1_cos", [P, S])
        sin = sb("p1_sin", [P, S])
        lat = sb("p1_lat", [QL + KVL, TILE])
        with_cos = [sb(f"p1_cos{i}", [(P, P, NK)[i], TILE]) for i in range(3)]
        with_sin = [sb(f"p1_sin{i}", [(P, P, NK)[i], TILE]) for i in range(3)]
        parts = [[sb(f"p1_part{k}{i}", [(P, P, NK)[i], 3, TILE], BF16) for i in range(3)] for k in range(2)]
        v = [sb(f"p1_v{k}", [P, KVH, BLK, D1 + 1]) for k in range(2)]

        loaded = pr.sem("p1_loaded")
        filled = pr.sem("p1_filled")
        weights = pr.sem("p1_weights")
        x_in = [pr.counter(f"p1_x_in{k}", 32) for k in range(2)]
        lat_sum = pr.counter("p1_lat_sum", 1)
        lat_ready = pr.counter("p1_lat_ready", 1)
        qk_sum = pr.counter("p1_qk_sum", 3)
        v_sum = pr.counter("p1_v_sum", 1)
        v_ready = pr.counter("p1_v_ready", 1, credit=1)
        steps = pr.counter("p1_steps", 24, credit=1)
        stored = [pr.counter(f"p1_stored{k}", 64, credit=1) for k in range(2)]

        with nc.Block() as block:
            @block.sync
            def _(sp):
                stored[0].open(sp)
                stored[1].open(sp)
                sp.dma_start(wa[:, :, 0:QL], a["L0_attn_Wqa"].rearrange("(k p) n -> p k n", p=P)).then_inc(loaded, 16)
                sp.dma_start(wa[:, :, QL:QL + KVL], a["L0_attn_Wkva"].rearrange("(k p) n -> p k n", p=P)).then_inc(loaded, 16)
                sp.dma_start(wq[:], a["L0_attn_Wqb"]).then_inc(loaded, 16)
                sp.dma_start(wkv[R, :], a["L0_attn_Wkvb"]).then_inc(loaded, 16)
                sp.dma_start(cos[:], a["rope_cos"]).then_inc(loaded, 16)
                sp.dma_start(sin[:], a["rope_sin"]).then_inc(loaded, 16)

                def load(n, i, k):
                    b = n if isinstance(n, int) else None
                    sp.dma_start(x[:, k], a["L0_attn_x"][bass.ds(i, 1), k * TILE:(k + 1) * TILE, :]
                                 .rearrange("b (n p) e -> p (b n) e", p=P)).then_inc(x_in[k].sem, 16)
                    sp.dma_start(mod[:, k], pr.mod_col[bass.ds(i, 1)].rearrange("b p c -> p (b c)")).then_inc(x_in[k].sem, 16)

                load(0, 0, 0)

                def pair(i, last):
                    for k in range(TPB):
                        n = i * TPB + k
                        if k == 0 or not last:
                            sp.wait_ge(norm.h_ready.sem, norm.h_ready.at(n - 1, EC))
                            load(n + 1, i + k, 1 - k)
                        tok = bass.ds(n * TILE, TILE)
                        sp.wait_ge(steps.sem, steps.at(n, 24))
                        for c in range(2):
                            sp.dma_start(pr.q1[:, c * P:(c + 1) * P, tok].rearrange("s p t -> p s t"),
                                         parts[k][c][:]).then_inc(stored[k].sem, 16)
                        sp.dma_start(pr.k1[:, :, tok].rearrange("s p t -> p s t"), parts[k][2][:]).then_inc(stored[k].sem, 16)
                        sp.wait_ge(v_ready.sem, v_ready.at(n, 1))
                        sp.dma_start(pr.v1[bass.ds(i, 1), :, :, k * BLK:(k + 1) * BLK, :].rearrange("b g p n d -> p (b g) (n d)"),
                                     v[k][:].rearrange("p g n d -> p g (n d)")).then_inc(stored[k].sem, 16)

                in_pairs(sp, TILES, pair)
                for k in range(2):
                    sp.wait_ge(stored[k].sem, stored[k].at(B - 1, 64))

            @block.gpsimd
            def _(pool):
                pool.memset(norm.power[:], -0.5).then_inc(filled, 1)
                for k in range(2):
                    pool.memset(v[k][:], 1.0).then_inc(filled, 1)
                pool.wait_ge(filled, 3)

                def pair(i, last):
                    for k in range(TPB):
                        norm.pool(pool, i * TPB + k)

                in_pairs(pool, TILES, pair)

            @block.scalar
            def _(act):
                norm.open(act, "act")
                v_ready.open(act)
                act.wait_ge(filled, 3)

                def pair(i, last):
                    for k in range(TPB):
                        n = i * TPB + k
                        norm.act(act, n, mod[:, k])
                        act.wait_ge(lat_sum.sem, lat_sum.at(n, 1))
                        act.copy(lat[:], pr.bank[0:QL + KVL, 2, :]).then_inc(lat_ready.sem, 1)
                        act.wait_ge(v_sum.sem, v_sum.at(n, 1))
                        act.wait_ge(stored[k].sem, stored[k].at(i - 1, 64))
                        act.copy(v[k][:, :, :, 0:D1].rearrange("p g n d -> p n g d"),
                                 pr.bank[:, 2, 0:BLK * NK].rearrange("p (n g d) -> p n g d", n=BLK, g=KVH)).then_inc(v_ready.sem, 1)

                in_pairs(act, TILES, pair)

            @block.vector
            def _(dve):
                steps.open(dve)
                dve.wait_ge(loaded, 96)
                dve.tensor_copy(wk[R, :], wkv[R, 0::2])
                dve.tensor_copy(wv[R, :], wkv[R, 1::2])
                for to, of in ((wq_turn, wq), (wk_turn[R], wkv[R, 0::2])):
                    dve.tensor_scalar(to[:, 0::2], of[:, 1::2], -1.0, None, ALU.mult)
                    dve.tensor_copy(to[:, 1::2], of[:, 0::2]).then_inc(weights, 1)
                dve.wait_ge(x_in[0].sem, x_in[0].at(0, 32))
                norm.dve(dve, 0, x[:, 0])

                def rotate(n, i, k):
                    pos = slice(k * TILE, (k + 1) * TILE)
                    rows = (P, P, NK)
                    sums = (pr.bank[:, 3, :], pr.bank[:, 5, :], pr.bank[0:NK, 0, :])
                    turns = (pr.bank[:, 4, :], pr.bank[:, 6, :], pr.bank[0:NK, 1, :])
                    dve.wait_ge(stored[k].sem, stored[k].at(i - 1, 64))
                    dve.wait_ge(steps.sem, steps.at(n - 1, 24))
                    for c in range(3):
                        dve.wait_ge(qk_sum.sem, qk_sum.at(n, c + 1))
                        dve.tensor_tensor(with_cos[c][:], sums[c], cos[0:rows[c], pos], ALU.mult).then_inc(steps.sem, 1)
                        dve.tensor_tensor(with_sin[c][:], turns[c], sin[0:rows[c], pos], ALU.mult).then_inc(steps.sem, 1)
                    for c in range(3):
                        dve.wait_ge(steps.sem, steps.at(n, 2 * c + 2))
                        dve.tensor_tensor(with_cos[c][:], with_cos[c][:], with_sin[c][:], ALU.add).then_inc(steps.sem, 1)
                    split_in_three(dve, steps, n, 9, [t[:] for t in with_cos], parts[k], [t[:] for t in with_sin])

                def pair(i, last):
                    for k in range(TPB):
                        n = i * TPB + k
                        if k == 0 or not last:
                            dve.wait_ge(x_in[1 - k].sem, x_in[1 - k].at(i + k, 32))
                            norm.dve(dve, n + 1, x[:, 1 - k])
                        rotate(n, i, k)

                in_pairs(dve, TILES, pair)

            @block.tensor
            def _(pe):
                norm.open(pe, "pe")
                pe.wait_ge(weights, 2)
                pe.wait_ge(loaded, 96)

                def pair(i, last):
                    for k in range(TPB):
                        n = i * TPB + k
                        pe.wait_ge(steps.sem, steps.at(n - 1, 6))
                        norm.pe(pe, n)
                        pe.wait_ge(norm.h_ready.sem, norm.h_ready.at(n, EC))
                        pe.wait_ge(v_ready.sem, v_ready.at(n - 1, 1))
                        for c in range(EC):
                            mm = pe.matmul(pr.bank[0:QL + KVL, 2, :], wa[:, c, :], norm.hT[:, c, :],
                                           start=(c == 0), stop=(c == EC - 1))
                        mm.then_inc(lat_sum.sem, 1)
                        pe.wait_ge(lat_ready.sem, lat_ready.at(n, 1))
                        for c in range(2):
                            pe.matmul(pr.bank[:, 3 + 2 * c, :], wq[:, c * P:(c + 1) * P], lat[0:QL, :], start=True, stop=True)
                            pe.matmul(pr.bank[:, 4 + 2 * c, :], wq_turn[:, c * P:(c + 1) * P], lat[0:QL, :],
                                      start=True, stop=True).then_inc(qk_sum.sem, 1)
                        pe.matmul(pr.bank[0:NK, 0, :], wk[R, :], lat[R, :], start=True, stop=True)
                        pe.matmul(pr.bank[0:NK, 1, :], wk_turn[R, :], lat[R, :], start=True, stop=True).then_inc(qk_sum.sem, 1)
                        for b in range(BLK):
                            mm = pe.matmul(pr.bank[:, 2, b * NK:(b + 1) * NK], lat[R, b * P:(b + 1) * P], wv[R, :],
                                           start=True, stop=True, skip_group_check=True)
                        mm.then_inc(v_sum.sem, 1)

                in_pairs(pe, TILES, pair)


def attention(pr, name, q, k, v, o, sums, rden, width, pairs, causal, scale):
    nc = pr.nc
    R = len(pairs) * width
    JK = 1 if causal else HQ
    KB, QB = S // P, S // P
    steps = [(t, kb) for t in range(TPB) for kb in range(KB) if not causal or kb * P < (t + 1) * TILE]
    L = len(steps)
    ends = [max(s for s in range(L) if steps[s][0] == t) for t in range(TPB)]
    looks = [(j, i, c) for j in range(HQ) for i in range(QB) for c in range(TPB)
             if not causal or c * TILE < (i + 1) * P]
    NL = len(looks)
    look_at = [NL * s // (L - 2) for s in range(L - 1)] + [NL, NL]
    look_at[L - 2] = NL

    with ExitStack() as ctx:
        def sb(n, shape, dt=F32):
            return ctx.enter_context(nc.sbuf_tensor(f"{name}_{n}", shape, dt))

        Q = [sb(f"Q{g}", [R + 2, HQ, S], BF16) for g in range(UPB)]
        K = [sb(f"K{g}", [R + 2, JK, S], BF16) for g in range(UPB)]
        V = [sb(f"V{g}", [P, JK, KB, width + 1] if causal else [P, KB, JK, width + 1]) for g in range(UPB)]
        prob = [sb(f"prob{n}", [P, HQ, TILE]) for n in range(2)]
        out = [sb(f"out{t}", [P, TILE]) for t in range(TPB)]
        peak = sb("peak", [P, HQ * QB, TPB])
        top = sb("top", [P, HQ * QB])
        top_row = [sb(f"top_row{g}", [HQ * QB, P]) for g in range(UPB)]
        top_hi = [sb(f"top_hi{g}", [HQ * QB, P], BF16) for g in range(UPB)]
        top_lo = [sb(f"top_lo{g}", [HQ * QB, P], BF16) for g in range(UPB)]
        den = sb("den", [P, H * TOK // P])
        scores = pr.bank[:, 0:4, :]
        acc = pr.bank[:, 4:6, :]
        look = pr.bank[:, 6:8, :]

        nload = (2 * len(pairs) if causal else (1 + JK) * len(pairs)) + 1
        filled = pr.sem(name + "_filled")
        cleared = pr.sem(name + "_cleared")
        loaded = [pr.counter(f"{name}_loaded{g}", 16 * nload) for g in range(UPB)]
        shift_in = [pr.counter(f"{name}_shift_in{g}", 32, credit=1) for g in range(UPB)]
        qk_done = pr.counter(name + "_qk_done", 2 * L)
        exp_done = pr.counter(name + "_exp_done", 2 * L, credit=1)
        pv_done = pr.counter(name + "_pv_done", L, credit=1)
        taken = pr.counter(name + "_taken", TPB, credit=1)
        stored = [pr.counter(f"{name}_stored{t}", 16 * (HQ + 1), credit=1) for t in range(TPB)]
        look_done = pr.counter(name + "_look_done", NL + 2)
        look_read = pr.counter(name + "_look_read", NL + 2, credit=1)
        topped = pr.counter(name + "_topped", 1)
        rows_made = pr.counter(name + "_rows_made", 1)
        den_in = pr.sem(name + "_den_in")
        den_done = pr.sem(name + "_den_done")
        den_out = pr.sem(name + "_den_out")

        def units(engine, body):
            with engine.Fori(0, B - 1) as b:
                for g in range(UPB):
                    body(b, g, True)
            for g in range(UPB):
                body(B - 1, g, g < UPB - 1)

        def after(b, g):
            return (b, g + 1) if g < UPB - 1 else (b + 1, 0)

        with nc.Block() as block:
            @block.sync
            def _(sp):
                for s in shift_in + stored:
                    s.open(sp)

                def load(b, g):
                    tok = bass.ds(b * S, S)
                    sem = loaded[g].sem
                    for n, (qi, ki) in enumerate(pairs):
                        rows = slice(n * width, (n + 1) * width)
                        feats = q[qi, g * HQ * width:(g + 1) * HQ * width, tok]
                        sp.dma_start(Q[g][rows, :, :], feats.rearrange("(j d) t -> d j t", d=width)).then_inc(sem, 16)
                        feats = k[ki, g * JK * width:(g + 1) * JK * width, tok]
                        if causal:
                            sp.dma_start(K[g][rows, 0, :], feats).then_inc(sem, 16)
                        else:
                            for j in range(JK):
                                sp.dma_start(K[g][rows, j, :], feats[j * width:(j + 1) * width]).then_inc(sem, 16)
                    sp.dma_start(V[g][:].rearrange("p a b d -> p (a b d)"),
                                 v[bass.ds(b, 1), g].rearrange("b p n d -> (b p) (n d)" if causal
                                                               else "b p n j d -> (b p) (n j d)")).then_inc(sem, 16)

                def shift(b, g):
                    sp.wait_ge(rows_made.sem, rows_made.at(b * UPB + g, 1))
                    for r, part in ((R, top_hi[g]), (R + 1, top_lo[g])):
                        sp.dma_start(Q[g][r:r + 1, :, :].rearrange("o j (i q) -> o (j i) q", q=P),
                                     part[:]).then_inc(shift_in[g].sem, 16)

                sp.wait_ge(filled, UPB)
                for g in range(UPB):
                    load(0, g)
                shift(0, 0)

                def unit(b, g, more):
                    u = b * UPB + g
                    if more:
                        shift(*after(b, g))
                    for t in range(TPB):
                        sp.wait_ge(taken.sem, taken.at(u, t + 1))
                        tok = bass.ds(b * S + t * TILE, TILE)
                        for j in range(HQ):
                            f = (g * HQ + j) * width
                            sp.dma_start(o[f:f + width, tok], out[t][32 * j:32 * j + width, :]).then_inc(stored[t].sem, 16)
                        sp.dma_start(sums[g * HQ:(g + 1) * HQ, tok], out[t][width::32, :]).then_inc(stored[t].sem, 16)
                    if more and not isinstance(b, int):
                        load(b + 1, g)

                units(sp, unit)
                for t in range(TPB):
                    sp.wait_ge(stored[t].sem, stored[t].at(B * UPB - 1, 16 * (HQ + 1)))
                sp.dma_start(den[:], sums.rearrange("h (s t) -> (h s) t", t=TOK * H // P)).then_inc(den_in, 16)
                sp.wait_ge(den_done, 1)
                for h in range(H):
                    part = den[h * P // H:(h + 1) * P // H, :]
                    sp.dma_start(rden[h].rearrange("d (s t) -> s d t", s=P // H),
                                 part.unsqueeze(1).broadcast_to([P // H, width, TOK * H // P])).then_inc(den_out, 16)
                sp.wait_ge(den_out, 16 * H)

            @block.gpsimd
            def _(pool):
                for g in range(UPB):
                    pool.memset(K[g][:], -1.0).then_inc(filled, 1)

            @block.scalar
            def _(act):
                exp_done.open(act)

                def unit(b, g, more):
                    u = b * UPB + g
                    for s, (t, kb) in enumerate(steps):
                        off = max(0, kb * P - t * TILE) if causal else 0
                        act.wait_ge(pv_done.sem, pv_done.at(u, s - 1))
                        for n in range(2):
                            act.wait_ge(qk_done.sem, qk_done.at(u, 2 * s + n + 1))
                            act.activation(prob[s % 2][:, 2 * n:2 * n + 2, off:], scores[:, 2 * n:2 * n + 2, off:],
                                           ACT.Exp, scale=scale).then_inc(exp_done.sem, 1)

                units(act, unit)

            @block.vector
            def _(dve):
                look_read.open(dve)
                taken.open(dve)
                dve.memset(peak[:], LOW).then_inc(cleared, 1)
                dve.memset(acc, 0.0).then_inc(cleared, 1)
                dve.wait_ge(cleared, 2)

                def peaks(b, g, first, last):
                    u = b * UPB + g
                    for m in range(first, last):
                        j, i, c = looks[m]
                        n = min(TILE, (i + 1) * P - c * TILE) if causal else TILE
                        dve.wait_ge(look_done.sem, look_done.at(u, m + 1))
                        if m == 0:
                            dve.wait_ge(look_read.sem, look_read.at(u - 1, NL + 2))
                        dve.tensor_reduce(peak[:, j * QB + i, c:c + 1], look[:, m % 2, 0:n], AX.X,
                                          ALU.max).then_inc(look_read.sem, 1)
                    if last == NL and first < NL:
                        dve.wait_ge(look_read.sem, look_read.at(u, NL))
                        dve.tensor_reduce(top[:], peak[:], AX.X, ALU.max).then_inc(topped.sem, 1)
                        dve.wait_ge(look_done.sem, look_done.at(u, NL + 1))
                        dve.wait_ge(shift_in[g].sem, shift_in[g].at(b - 1, 32))
                        dve.tensor_copy(top_row[g][:], look[0:HQ * QB, 0, 0:P]).then_inc(look_read.sem, 1)
                        dve.wait_ge(look_read.sem, look_read.at(u, NL + 1))
                        dve.tensor_copy(top_hi[g][:], top_row[g][:]).then_inc(look_read.sem, 1)
                        dve.wait_ge(look_read.sem, look_read.at(u, NL + 2))
                        dve.tensor_tensor(top_lo[g][:], top_row[g][:], top_hi[g][:], ALU.subtract).then_inc(rows_made.sem, 1)

                peaks(0, 0, 0, NL)

                def unit(b, g, more):
                    u = b * UPB + g
                    for s in range(L):
                        if more:
                            peaks(*after(b, g), look_at[s], look_at[s + 1])
                        for t in range(TPB):
                            if s == min(ends[t] + 1, L - 1):
                                dve.wait_ge(pv_done.sem, pv_done.at(u, ends[t] + 1))
                                dve.wait_ge(stored[t].sem, stored[t].at(u - 1, 16 * (HQ + 1)))
                                dve.tensor_copy(out[t][:], acc[:, t, :]).then_inc(taken.sem, 1)

                units(dve, unit)
                dve.wait_ge(den_in, 16)
                dve.reciprocal(den[:], den[:]).then_inc(den_done, 1)

            @block.tensor
            def _(pe):
                pv_done.open(pe)
                pe.wait_ge(cleared, 2)

                def look_for(b, g, first, last):
                    u = b * UPB + g
                    if first == 0:
                        pe.wait_ge(loaded[g].sem, loaded[g].at(b + 1, 0))
                    for m in range(first, last):
                        j, i, c = looks[m]
                        n = min(TILE, (i + 1) * P - c * TILE) if causal else TILE
                        diag = causal and c == i * P // TILE
                        pe.wait_ge(look_read.sem, look_read.at(u, m - 1) if m >= 2 else look_read.at(u - 1, NL + 2))
                        mm = pe.matmul(look[:, m % 2, 0:n], Q[g][0:R, j, i * P:(i + 1) * P],
                                       K[g][0:R, j % JK, c * TILE:c * TILE + n], start=True, stop=not diag)
                        if diag:
                            mm = pe.matmul(look[:, m % 2, n - P:n], pr.ident16[:], pr.mask_qk[:], start=False, stop=True)
                        mm.then_inc(look_done.sem, 1)
                    if last == NL and first < NL:
                        pe.wait_ge(topped.sem, topped.at(u, 1))
                        pe.transpose(look[0:HQ * QB, 0, 0:P], top[:], pr.ident[:]).then_inc(look_done.sem, 2)

                def score(b, g, s, n):
                    u = b * UPB + g
                    t, kb = steps[s]
                    off = max(0, kb * P - t * TILE) if causal else 0
                    diag = causal and kb * P >= t * TILE
                    if s == 0 and n == 0:
                        pe.wait_ge(shift_in[g].sem, shift_in[g].at(b, 32))
                    pe.wait_ge(exp_done.sem, exp_done.at(u, 2 * s - 2 + n + 1))
                    for j in (2 * n, 2 * n + 1):
                        mm = pe.matmul(scores[:, j, off:], K[g][:, j % JK, kb * P:(kb + 1) * P],
                                       Q[g][:, j, t * TILE + off:(t + 1) * TILE], start=True, stop=not diag)
                        if diag:
                            mm = pe.matmul(scores[:, j, off:off + P], pr.ident16[:], pr.mask_kq[:], start=False, stop=True)
                    mm.then_inc(qk_done.sem, 1)

                look_for(0, 0, 0, NL)
                score(0, 0, 0, 0)
                score(0, 0, 0, 1)

                def unit(b, g, more):
                    u = b * UPB + g
                    for s, (t, kb) in enumerate(steps):
                        off = max(0, kb * P - t * TILE) if causal else 0
                        first, last = (look_at[s], look_at[s + 1]) if more else (0, 0)
                        middle = (first + last) // 2
                        ahead = (b, g, s + 1) if s < L - 1 else (*after(b, g), 0)
                        if s < L - 1 or more:
                            score(*ahead, 0)
                        if middle > first:
                            look_for(*after(b, g), first, middle)
                        if s < L - 1 or more:
                            score(*ahead, 1)
                        if last > middle:
                            look_for(*after(b, g), middle, last)
                        pe.wait_ge(exp_done.sem, exp_done.at(u, 2 * s + 2))
                        if s in (0, ends[0] + 1):
                            pe.wait_ge(taken.sem, taken.at(u - 1, t + 1))
                        for j in range(HQ):
                            w = V[g][:, 0, kb, :] if causal else V[g][:, kb, j, :]
                            mm = pe.matmul(acc[32 * j:32 * j + width + 1, t, off:], w, prob[s % 2][:, j, off:],
                                           start=(kb == 0), stop=(s == ends[t]), skip_group_check=True)
                        mm.then_inc(pv_done.sem, 1)

                units(pe, unit)


def between(pr):
    nc, a = pr.nc, pr.a
    with ExitStack() as ctx:
        def sb(name, shape, dt=F32):
            return ctx.enter_context(nc.sbuf_tensor(name, shape, dt))

        x = [sb(f"p3_x{k}", [P, BLK, E]) for k in range(2)]
        o = [sb(f"p3_o{k}", [P, EC, TILE]) for k in range(2)]
        rden = [sb(f"p3_rden{k}", [P, EC, TILE]) for k in range(2)]
        mod = [sb(f"p3_mod{k}", [P, NMOD * EC]) for k in range(2)]
        gate = [sb(f"p3_gate{k}", [P, E]) for k in range(2)]
        norm = Norm(pr, sb, "p3", SB, CB)
        wout = sb("p3_wout", [P, EC, E])
        bout = sb("p3_bout", [P, E])
        gbias = sb("p3_gbias", [P, E])
        wq = sb("p3_wq", [P, EC, H, D2])
        wq_all = sb("p3_wq_all", [P, EC, E])
        wk = sb("p3_wk", [P, EC, P])
        wv = sb("p3_wv", [P, EC, P])
        qb = sb("p3_qb", [P, 1])
        kb = sb("p3_kb", [P, 1])
        vb = sb("p3_vb", [P, P])
        on = sb("p3_on", [P, EC, TILE])
        xg = sb("p3_xg", [P, BLK, E])
        gated = sb("p3_gated", [P, BLK, E])
        x1 = [sb(f"p3_x1_{k}", [P, BLK, E]) for k in range(2)]
        gh = [sb(f"p3_gh{k}", [P, EC, TILE]) for k in range(2)]
        qk = [sb(f"p3_qk{c}", [P, TILE]) for c in range(2)]
        rest = [sb(f"p3_rest{c}", [P, TILE]) for c in range(2)]
        parts = [[sb(f"p3_part{k}{c}", [P, 3, TILE], BF16) for c in range(2)] for k in range(2)]
        v = [sb(f"p3_v{k}", [P, UPB, BLK, HQ, D2 + 1]) for k in range(2)]

        loaded = pr.sem("p3_loaded")
        filled = pr.sem("p3_filled")
        picked = pr.sem("p3_picked")
        tile_in = [pr.counter(f"p3_tile_in{k}", 96) for k in range(2)]
        pre = pr.counter("p3_pre", 3, credit=1)
        out_sum = pr.counter("p3_out_sum", 1)
        resid = pr.counter("p3_resid", 2, credit=1)
        qk_sum = pr.counter("p3_qk_sum", 2)
        qk_ready = pr.counter("p3_qk_ready", 2, credit=1)
        gh_ready = pr.counter("p3_gh_ready", EC, credit=1)
        v_sum = pr.counter("p3_v_sum", 1)
        v_ready = pr.counter("p3_v_ready", 1, credit=1)
        cut = pr.counter("p3_cut", 10, credit=1)
        x1_out = [pr.counter(f"p3_x1_out{k}", 16, credit=1) for k in range(2)]
        out = [pr.counter(f"p3_out{k}", 96, credit=1) for k in range(2)]

        with nc.Block() as block:
            @block.sync
            def _(sp):
                for s in x1_out + out:
                    s.open(sp)
                sp.dma_start(wout[:], a["L0_attn_Wout"].rearrange("(k p) n -> p k n", p=P)).then_inc(loaded, 16)
                sp.dma_start(bout[:], a["L0_attn_bout"].partition_broadcast(P)).then_inc(loaded, 16)
                sp.dma_start(wq_all[:], a["L0_ffn_q_w"].rearrange("(k p) n -> p k n", p=P)).then_inc(loaded, 16)
                sp.dma_start(wk[:], a["L0_ffn_k_w"].rearrange("(k p) n -> p k n", p=P)).then_inc(loaded, 16)
                sp.dma_start(wv[:], a["L0_ffn_v_w"].rearrange("(k p) n -> p k n", p=P)).then_inc(loaded, 16)
                for h in range(H):
                    sp.dma_start(qb[h * D2:(h + 1) * D2, :],
                                 a["L0_ffn_q_b"][h * D1:h * D1 + D2].unsqueeze(1)).then_inc(loaded, 16)
                sp.dma_start(kb[:], a["L0_ffn_k_b"].unsqueeze(1)).then_inc(loaded, 16)
                sp.dma_start(vb[:], a["L0_ffn_v_b"].partition_broadcast(P)).then_inc(loaded, 16)

                def load(b, k):
                    tok, sem = bass.ds(b * S + k * TILE, TILE), tile_in[k].sem
                    sp.dma_start(x[k][:], a["L0_attn_x"][bass.ds(b, 1), k * TILE:(k + 1) * TILE, :]
                                 .rearrange("b (n p) e -> p (b n) e", p=P)).then_inc(sem, 16)
                    sp.dma_start(o[k][:], pr.o1[:, tok].rearrange("(c p) t -> p c t", p=P)).then_inc(sem, 16)
                    flat = pr.rden1.rearrange("h d t -> (h d) t")
                    sp.dma_start(rden[k][:], flat[:, tok].rearrange("(c p) t -> p c t", p=P)).then_inc(sem, 16)
                    sp.dma_start(mod[k][:], pr.mod_col[bass.ds(b, 1)].rearrange("b p c -> p (b c)")).then_inc(sem, 16)
                    sp.dma_start(gate[k][:], pr.mod_row[bass.ds(b, 1), GA, :].broadcast_to([P, E])).then_inc(sem, 32)

                def store_x1(b, k):
                    sp.wait_ge(resid.sem, resid.at(b * TPB + k, 2))
                    sp.dma_start(pr.x1[bass.ds(b * S + k * TILE, TILE), :].rearrange("(n p) e -> p n e", p=P),
                                 x1[k][:]).then_inc(x1_out[k].sem, 16)

                load(0, 0)
                load(0, 1)
                store_x1(0, 0)

                def pair(b, last):
                    for k in range(TPB):
                        n = b * TPB + k
                        tok = bass.ds(b * S + k * TILE, TILE)
                        sem = out[k].sem
                        sp.wait_ge(v_ready.sem, v_ready.at(n, 1))
                        sp.wait_ge(gh_ready.sem, gh_ready.at(n, EC))
                        sp.wait_ge(cut.sem, cut.at(n, 10))
                        sp.dma_start(pr.v2[bass.ds(b, 1), :, :, k * BLK:(k + 1) * BLK].rearrange("b g p n j d -> p (b g) (n j d)"),
                                     v[k][:].rearrange("p g n j d -> p g (n j d)")).then_inc(sem, 48)
                        sp.dma_start(pr.gh[:, tok].rearrange("(c p) t -> p c t", p=P), gh[k][:]).then_inc(sem, 16)
                        sp.dma_start(pr.q2[:, :, tok].rearrange("s p t -> p s t"), parts[k][0][:]).then_inc(sem, 16)
                        sp.dma_start(pr.k2[:, :, tok].rearrange("s p t -> p s t"), parts[k][1][:]).then_inc(sem, 16)
                        if k == 0 or not last:
                            store_x1(b + k, 1 - k)
                        if not last:
                            load(b + 1, k)

                in_pairs(sp, TILES, pair)
                for k in range(2):
                    sp.wait_ge(x1_out[k].sem, x1_out[k].at(B - 1, 16))
                    sp.wait_ge(out[k].sem, out[k].at(B - 1, 96))

            @block.gpsimd
            def _(pool):
                pool.memset(norm.power[:], -0.5).then_inc(filled, 1)
                for k in range(2):
                    pool.memset(v[k][:], 1.0).then_inc(filled, 1)
                pool.wait_ge(filled, 3)
                norm.pool(pool, 0)

                def pair(b, last):
                    for k in range(TPB):
                        if k == 0 or not last:
                            norm.pool(pool, b * TPB + k + 1)

                in_pairs(pool, TILES, pair)

            @block.scalar
            def _(act):
                norm.open(act, "act")
                qk_ready.open(act)
                gh_ready.open(act)
                act.wait_ge(loaded, 16 * (7 + H))

                def pair(b, last):
                    for k in range(TPB):
                        n = b * TPB + k
                        act.wait_ge(tile_in[k].sem, tile_in[k].at(b + 1, 0))
                        act.wait_ge(gh_ready.sem, gh_ready.at(n - 1, EC))
                        norm.act(act, n, mod[k])
                        for c in range(2):
                            act.wait_ge(qk_sum.sem, qk_sum.at(n, c + 1))
                            if c == 0:
                                act.wait_ge(cut.sem, cut.at(n - 1, 10))
                            act.activation(qk[c][:], pr.bank[:, 4 + c, :], ACT.Identity,
                                           bias=(qb, kb)[c][:, 0:1]).then_inc(qk_ready.sem, 1)
                        act.wait_ge(out[k].sem, out[k].at(b - 1, 96))
                        act.wait_ge(norm.h_ready.sem, norm.h_ready.at(n, EC))
                        for c in range(EC):
                            act.activation(gh[k][:, c, :], norm.hT[:, c, :], ACT.Identity,
                                           scale=mod[k][:, GB * EC + c:GB * EC + c + 1]).then_inc(gh_ready.sem, 1)

                in_pairs(act, TILES, pair)

            @block.vector
            def _(dve):
                pre.open(dve)
                resid.open(dve)
                v_ready.open(dve)
                cut.open(dve)
                dve.wait_ge(loaded, 16 * (7 + H))
                dve.wait_ge(filled, 3)
                dve.tensor_copy(wq[:], wq_all[:].rearrange("p k (h d) -> p k h d", d=D1)[:, :, :, 0:D2]).then_inc(picked, 1)

                def prepare(b, k):
                    n = b * TPB + k
                    dve.wait_ge(tile_in[k].sem, tile_in[k].at(b, 96))
                    dve.wait_ge(out_sum.sem, out_sum.at(n, 0)) if not isinstance(b, int) or n else None
                    dve.tensor_tensor(on[:], o[k][:], rden[k][:], ALU.mult).then_inc(pre.sem, 1)
                    dve.wait_ge(pre.sem, pre.at(n - 1, 3))
                    dve.tensor_tensor(gbias[:], gate[k][:], bout[:], ALU.mult).then_inc(pre.sem, 1)
                    dve.wait_ge(resid.sem, resid.at(n - 1, 2))
                    dve.wait_ge(pre.sem, pre.at(n, 2))
                    dve.tensor_tensor(xg[:], x[k][:], gbias[:].unsqueeze(1).broadcast_to([P, BLK, E]),
                                      ALU.add).then_inc(pre.sem, 1)

                def residual(b, k):
                    n = b * TPB + k
                    dve.wait_ge(out_sum.sem, out_sum.at(n, 1))
                    y = pr.bank[:, 2:4, :].rearrange("p a (n e) -> p (a n) e", e=E)
                    dve.tensor_tensor(gated[:], y, gate[k][:].unsqueeze(1).broadcast_to([P, BLK, E]),
                                      ALU.mult).then_inc(resid.sem, 1)
                    dve.wait_ge(resid.sem, resid.at(n, 1))
                    dve.wait_ge(pre.sem, pre.at(n, 3))
                    dve.wait_ge(x1_out[k].sem, x1_out[k].at(b - 1, 16))
                    dve.tensor_tensor(x1[k][:], gated[:], xg[:], ALU.add).then_inc(resid.sem, 1)
                    dve.wait_ge(resid.sem, resid.at(n, 2))
                    norm.dve(dve, n, x1[k])

                def split(b, k):
                    n = b * TPB + k
                    dve.wait_ge(qk_ready.sem, qk_ready.at(n, 2))
                    dve.wait_ge(out[k].sem, out[k].at(b - 1, 96))
                    split_in_three(dve, cut, n, 0, [t[:] for t in qk], parts[k], [t[:] for t in rest])
                    dve.wait_ge(v_sum.sem, v_sum.at(n, 1))
                    for i in range(BLK):
                        op = dve.tensor_tensor(v[k][:, :, i, :, 0:D2],
                                               pr.bank[:, 6, i * P:(i + 1) * P].rearrange("p (g j d) -> p g j d", g=UPB, j=HQ),
                                               vb[:].rearrange("p (g j d) -> p g j d", g=UPB, j=HQ), ALU.add)
                    op.then_inc(v_ready.sem, 1)

                prepare(0, 0)
                residual(0, 0)

                def pair(b, last):
                    for k in range(TPB):
                        more = k == 0 or not last
                        if more:
                            prepare(b + k, 1 - k)
                        split(b, k)
                        if more:
                            residual(b + k, 1 - k)

                in_pairs(dve, TILES, pair)

            @block.tensor
            def _(pe):
                norm.open(pe, "pe")
                pe.wait_ge(loaded, 16 * (7 + H))
                pe.wait_ge(picked, 1)

                def project(n):
                    pe.wait_ge(pre.sem, pre.at(n, 1))
                    pe.wait_ge(resid.sem, resid.at(n - 1, 1))
                    for i in range(BLK):
                        to = pr.bank[:, 2 + i // 2, (i % 2) * E:(i % 2 + 1) * E]
                        for c in range(EC):
                            mm = pe.matmul(to, on[:, c, i * P:(i + 1) * P], wout[:, c, :],
                                           start=(c == 0), stop=(c == EC - 1), skip_group_check=True)
                    mm.then_inc(out_sum.sem, 1)

                project(0)

                def pair(b, last):
                    for k in range(TPB):
                        n = b * TPB + k
                        pe.wait_ge(norm.h_ready.sem, norm.h_ready.at(n - 1, EC))
                        norm.pe(pe, n)
                        if k == 0 or not last:
                            project(n + 1)
                        pe.wait_ge(norm.h_ready.sem, norm.h_ready.at(n, EC))
                        pe.wait_ge(qk_ready.sem, qk_ready.at(n - 1, 2))
                        for i, w in enumerate((wq[:].rearrange("p k h d -> p k (h d)"), wk[:])):
                            for c in range(EC):
                                mm = pe.matmul(pr.bank[:, 4 + i, :], w[:, c, :], norm.hT[:, c, :],
                                               start=(c == 0), stop=(c == EC - 1))
                            mm.then_inc(qk_sum.sem, 1)
                        pe.wait_ge(v_ready.sem, v_ready.at(n - 1, 1))
                        for i in range(BLK):
                            for c in range(EC):
                                mm = pe.matmul(pr.bank[:, 6, i * P:(i + 1) * P], norm.hT[:, c, i * P:(i + 1) * P], wv[:, c, :],
                                               start=(c == 0), stop=(c == EC - 1), skip_group_check=True)
                        mm.then_inc(v_sum.sem, 1)

                in_pairs(pe, TILES, pair)


def route(pr):
    nc, a = pr.nc, pr.a
    NB = TILES * BLK
    with ExitStack() as ctx:
        def sb(name, shape, dt=F32):
            return ctx.enter_context(nc.sbuf_tensor(name, shape, dt))

        o = [sb(f"p5_o{k}", [P, TILE]) for k in range(2)]
        rden = [sb(f"p5_rden{k}", [P, TILE]) for k in range(2)]
        on = [sb(f"p5_on{k}", [P, TILE]) for k in range(2)]
        wo = sb("p5_wo", [P, E])
        ob = sb("p5_ob", [P, EC])
        wr = sb("p5_wr", [P, EC, NX])
        rb = sb("p5_rb", [P, NX])
        mla = [sb(f"p5_mla{k}", [P, EC, TILE]) for k in range(2)]
        part = [sb(f"p5_part{k}", [P, 2, EC, TILE], F32R) for k in range(2)]
        logit = sb("p5_logit", [P, NB, NX])
        prob = sb("p5_prob", [P, NB, NX])
        rank = sb("p5_rank", [P, NX])
        tmp = sb("p5_tmp", [P, NB, NX])
        first = sb("p5_first", [P, NB, NX])
        second = sb("p5_second", [P, NB, NX])
        top1 = sb("p5_top1", [P, NB])
        top2 = sb("p5_top2", [P, NB])
        best = sb("p5_best", [P, NB])
        total = sb("p5_total", [P, NB])
        comb = sb("p5_comb", [P, TILES, NX, BLK])
        combT = sb("p5_combT", [BLK * NX, TILES, P])

        loaded = pr.sem("p5_loaded")
        ranked = pr.sem("p5_ranked")
        tile_in = [pr.counter(f"p5_tile_in{k}", 32) for k in range(2)]
        on_ready = pr.counter("p5_on_ready", 1)
        mla_sum = pr.counter("p5_mla_sum", EC)
        mla_ready = pr.counter("p5_mla_ready", EC, credit=1)
        cut = pr.counter("p5_cut", 2, credit=2)
        logit_sum = pr.counter("p5_logit_sum", 1, credit=1)
        logit_ready = pr.counter("p5_logit_ready", 1, credit=1)
        stored = [pr.counter(f"p5_stored{k}", 32, credit=1) for k in range(2)]
        step = pr.sem("p5_step")
        exps = pr.sem("p5_exps")
        weighted = pr.sem("p5_weighted")
        turned = pr.sem("p5_turned")
        comb_ready = pr.sem("p5_comb_ready")
        comb_out = pr.sem("p5_comb_out")

        with nc.Block() as block:
            @block.sync
            def _(sp):
                for s in stored:
                    s.open(sp)
                sp.dma_start(wo[:], a["L0_ffn_o_w"][0:P, :]).then_inc(loaded, 16)
                sp.dma_start(wr[:], a["L0_ffn_router_w"].rearrange("(k p) n -> p k n", p=P)).then_inc(loaded, 16)
                sp.dma_start(rb[:], a["L0_ffn_router_b"].partition_broadcast(P)).then_inc(loaded, 16)
                for c in range(EC):
                    sp.dma_start(ob[:, c:c + 1], a["L0_ffn_o_b"][c * P:(c + 1) * P].unsqueeze(1)).then_inc(loaded, 16)

                def load(b, k):
                    tok, sem = bass.ds(b * S + k * TILE, TILE), tile_in[k].sem
                    sp.dma_start(o[k][:], pr.o2[:, tok]).then_inc(sem, 16)
                    sp.dma_start(rden[k][:], pr.rden2.rearrange("h d t -> (h d) t")[:, tok]).then_inc(sem, 16)

                load(0, 0)
                load(0, 1)

                def pair(b, last):
                    for k in range(TPB):
                        n = b * TPB + k
                        sp.wait_ge(on_ready.sem, on_ready.at(n, 1))
                        if not last:
                            load(b + 1, k)
                        sp.wait_ge(cut.sem, cut.at(n, 2))
                        for h in range(2):
                            sp.dma_start(pr.mla[h, :, bass.ds(b * S + k * TILE, TILE)].rearrange("(c p) t -> p c t", p=P),
                                         part[k][:, h].bitcast(F32)).then_inc(stored[k].sem, 16)

                in_pairs(sp, TILES, pair)
                for k in range(2):
                    sp.wait_ge(stored[k].sem, stored[k].at(B - 1, 32))
                sp.wait_ge(comb_ready, 1)
                sp.dma_start(pr.comb.rearrange("n e (b t) -> (e b) n t", b=BLK), combT[:]).then_inc(comb_out, 16)
                sp.wait_ge(comb_out, 16)

            @block.gpsimd
            def _(pool):
                for e in range(NX):
                    op = pool.memset(rank[:, e:e + 1], float(NX - e))
                op.then_inc(ranked, 1)

            @block.scalar
            def _(act):
                mla_ready.open(act)
                act.wait_ge(loaded, 80)

                def pair(b, last):
                    for k in range(TPB):
                        n = b * TPB + k
                        act.wait_ge(cut.sem, cut.at(n - 2, 2))
                        act.wait_ge(logit_sum.sem, logit_sum.at(n - 1, 1))
                        for c in range(EC):
                            act.wait_ge(mla_sum.sem, mla_sum.at(n, c + 1))
                            act.activation(mla[k][:, c, :], pr.bank[:, c, :], ACT.Identity,
                                           bias=ob[:, c:c + 1]).then_inc(mla_ready.sem, 1)

                in_pairs(act, TILES, pair)
                act.wait_ge(step, 2)
                act.activation(prob[:], logit[:], ACT.Exp).then_inc(exps, 1)

            @block.vector
            def _(dve):
                cut.open(dve)
                logit_ready.open(dve)
                dve.wait_ge(loaded, 80)

                def normalise(b, k):
                    dve.wait_ge(tile_in[k].sem, tile_in[k].at(b, 32))
                    dve.wait_ge(mla_ready.sem, mla_ready.at(b * TPB + k - 1, EC)) if not isinstance(b, int) or b or k else None
                    dve.tensor_tensor(on[k][:], o[k][:], rden[k][:], ALU.mult).then_inc(on_ready.sem, 1)

                normalise(0, 0)

                def pair(b, last):
                    for k in range(TPB):
                        n = b * TPB + k
                        if k == 0 or not last:
                            normalise(b + k, 1 - k)
                        dve.wait_ge(mla_ready.sem, mla_ready.at(n, EC))
                        dve.wait_ge(stored[k].sem, stored[k].at(b - 1, 32))
                        dve.tensor_copy(part[k][:, 0], mla[k][:]).then_inc(cut.sem, 1)
                        dve.wait_ge(cut.sem, cut.at(n, 1))
                        dve.tensor_tensor(part[k][:, 1], mla[k][:], part[k][:, 0].bitcast(F32), ALU.subtract).then_inc(cut.sem, 1)
                        dve.wait_ge(logit_sum.sem, logit_sum.at(n, 1))
                        dve.tensor_tensor(logit[:, bass.ds(n * BLK, BLK), :],
                                          pr.bank[:, 2, 0:BLK * NX].rearrange("p (b e) -> p b e", e=NX),
                                          rb[:].unsqueeze(1).broadcast_to([P, BLK, NX]), ALU.add).then_inc(logit_ready.sem, 1)

                in_pairs(dve, TILES, pair)
                dve.wait_ge(logit_ready.sem, logit_ready.at(TILES - 1, 1))
                dve.wait_ge(ranked, 1)

                def wide(t):
                    return t[:].unsqueeze(2).broadcast_to([P, NB, NX])

                dve.tensor_reduce(best[:], logit[:], AX.X, ALU.max).then_inc(step, 1)
                dve.wait_ge(step, 1)
                dve.tensor_tensor(logit[:], logit[:], wide(best), ALU.subtract).then_inc(step, 1)
                dve.wait_ge(exps, 1)
                dve.tensor_reduce(total[:], prob[:], AX.X, ALU.add).then_inc(step, 1)
                dve.wait_ge(step, 3)
                dve.reciprocal(total[:], total[:]).then_inc(step, 1)
                dve.wait_ge(step, 4)
                dve.tensor_tensor(prob[:], prob[:], wide(total), ALU.mult).then_inc(step, 1)
                at = 5
                for value, choice in ((top1, first), (top2, second)):
                    dve.wait_ge(step, at)
                    dve.tensor_reduce(value[:], prob[:], AX.X, ALU.max).then_inc(step, 1)
                    dve.wait_ge(step, at + 1)
                    dve.tensor_tensor(tmp[:], prob[:], wide(value), ALU.is_equal).then_inc(step, 1)
                    dve.wait_ge(step, at + 2)
                    dve.tensor_tensor(tmp[:], tmp[:], rank[:].unsqueeze(1).broadcast_to([P, NB, NX]), ALU.mult).then_inc(step, 1)
                    dve.wait_ge(step, at + 3)
                    dve.tensor_reduce(best[:], tmp[:], AX.X, ALU.max).then_inc(step, 1)
                    dve.wait_ge(step, at + 4)
                    dve.tensor_tensor(choice[:], tmp[:], wide(best), ALU.is_equal).then_inc(step, 1)
                    dve.wait_ge(step, at + 5)
                    dve.scalar_tensor_tensor(out=prob[:], in0=choice[:], scalar=-2.0, in1=prob[:],
                                             op0=ALU.mult, op1=ALU.add).then_inc(step, 1)
                    at += 6
                dve.wait_ge(step, at)
                dve.scalar_tensor_tensor(out=total[:], in0=top1[:], scalar=1e-8, in1=top2[:],
                                         op0=ALU.add, op1=ALU.add).then_inc(step, 1)
                dve.wait_ge(step, at + 1)
                dve.reciprocal(total[:], total[:]).then_inc(step, 1)
                dve.wait_ge(step, at + 2)
                dve.tensor_tensor(top1[:], top1[:], total[:], ALU.mult).then_inc(step, 1)
                dve.tensor_tensor(top2[:], top2[:], total[:], ALU.mult).then_inc(step, 1)
                dve.wait_ge(step, at + 4)
                dve.tensor_tensor(first[:], first[:], wide(top1), ALU.mult).then_inc(step, 1)
                dve.tensor_tensor(second[:], second[:], wide(top2), ALU.mult).then_inc(step, 1)
                dve.wait_ge(step, at + 6)
                dve.tensor_tensor(comb[:].rearrange("p n e b -> p n b e"),
                                  first[:].rearrange("p (n b) e -> p n b e", b=BLK),
                                  second[:].rearrange("p (n b) e -> p n b e", b=BLK), ALU.add).then_inc(weighted, 1)
                dve.wait_ge(turned, 1)
                dve.tensor_copy(combT[:], pr.bank[0:BLK * NX, 3:5, :].rearrange("q a (n t) -> q (a n) t", t=P)).then_inc(comb_ready, 1)

            @block.tensor
            def _(pe):
                logit_sum.open(pe)
                pe.wait_ge(loaded, 80)

                def pair(b, last):
                    for k in range(TPB):
                        n = b * TPB + k
                        pe.wait_ge(on_ready.sem, on_ready.at(n, 1))
                        pe.wait_ge(mla_ready.sem, mla_ready.at(n - 1, EC))
                        for c in range(EC):
                            pe.matmul(pr.bank[:, c, :], wo[:, c * P:(c + 1) * P], on[k][:], start=True,
                                      stop=True).then_inc(mla_sum.sem, 1)
                        pe.wait_ge(mla_ready.sem, mla_ready.at(n, EC))
                        pe.wait_ge(logit_ready.sem, logit_ready.at(n - 1, 1))
                        for i in range(BLK):
                            for c in range(EC):
                                mm = pe.matmul(pr.bank[:, 2, i * NX:(i + 1) * NX], mla[k][:, c, i * P:(i + 1) * P], wr[:, c, :],
                                               start=(c == 0), stop=(c == EC - 1), skip_group_check=True)
                        mm.then_inc(logit_sum.sem, 1)

                in_pairs(pe, TILES, pair)
                pe.wait_ge(weighted, 1)
                for n in range(TILES):
                    mm = pe.transpose(pr.bank[0:BLK * NX, 3 + n // 4, (n % 4) * P:(n % 4 + 1) * P],
                                      comb[:, n].rearrange("p e b -> p (e b)"), pr.ident[:])
                mm.then_inc(turned, 1)


def experts(pr):
    nc, a = pr.nc, pr.a
    COLS = 2 * FC * FC
    with ExitStack() as ctx:
        def sb(name, shape, dt=F32):
            return ctx.enter_context(nc.sbuf_tensor(name, shape, dt))

        x = [sb(f"p6_x{t}", [P, 2, EC, S], F32R) for t in range(2)]
        w = [[sb(f"p6_w{j}{k}", [P, EC * FF]) for j in (1, 2)] for k in range(2)]
        wp = [[sb(f"p6_wp{j}{k}", [P, 2, EC * FF], F32R) for j in (1, 2)] for k in range(2)]
        bias = sb("p6_bias", [P, NX * (FC + EC)])
        b1 = [sb(f"p6_b1{k}", [P, FC]) for k in range(2)]
        b2 = [sb(f"p6_b2{k}", [P, EC]) for k in range(2)]
        comb = [sb(f"p6_comb{k}", [P, TPB, TILE]) for k in range(2)]
        g = [sb(f"p6_g{f}", [P, S]) for f in range(2)]
        hid = [sb(f"p6_hid{f}", [P, 2, S], F32R) for f in range(FC)]
        z = [sb(f"p6_z{c}", [P, S]) for c in range(EC)]
        acc = sb("p6_acc", [P, EC, S])
        gh = sb("p6_gh", [P, EC, S])
        mod = sb("p6_mod", [P, NMOD * EC])
        x1 = sb("p6_resid", [P, S // P, E])
        y = sb("p6_y", [P, S // P, E])

        bank1 = [pr.bank[:, 2 * q:2 * q + 2, :] for q in range(2)]
        bank2 = [pr.bank[:, 4 + 2 * c:6 + 2 * c, :] for c in range(EC)]

        x_in = [pr.counter(f"p6_x_in{t}", 32) for t in range(2)]
        w_in = [pr.counter(f"p6_w_in{k}", 64) for k in range(2)]
        comb_in = [pr.counter(f"p6_comb_in{k}", 16) for k in range(2)]
        end_in = pr.counter("p6_end_in", 48)
        w_hi = pr.counter("p6_w_hi", 2, credit=1)
        w_lo = pr.counter("p6_w_lo", 2, credit=1)
        sum1 = pr.counter("p6_sum1", FC)
        gelu = pr.counter("p6_gelu", FC, credit=1)
        hi = pr.counter("p6_hi", FC)
        lo = pr.counter("p6_lo", FC, credit=1)
        sum2 = pr.counter("p6_sum2", FC, credit=1)
        weigh = pr.counter("p6_weigh", 2 * EC, credit=2)
        final = pr.counter("p6_final", EC + 1)
        turned = pr.counter("p6_turned", 2)
        done = pr.counter("p6_done", 2, credit=1)
        stored = pr.counter("p6_stored", 16, credit=1)

        def batches(engine, before, visit, end):
            with engine.Fori(0, B // 2) as i:
                for t in range(2):
                    b = i * 2 + t
                    before(b, i, t)
                    with engine.Fori(0, NX // 2) as j:
                        for k in range(2):
                            visit(i, b, j, k, b * NX + j * 2 + k, b * (NX // 2) + j, t)
                    end(b)

        with nc.Block() as block:
            @block.sync
            def _(sp):
                def before(b, i, t):
                    sp.wait_ge(sum2.sem, sum2.at(b * NX - 1, FC))
                    tok = bass.ds(b * S, S)
                    for h in range(2):
                        sp.dma_start(x[t][:, h].bitcast(F32), pr.mla[h, :, tok].rearrange("(c p) t -> p c t", p=P)).then_inc(x_in[t].sem, 16)

                def visit(i, b, j, k, v, pair, t):
                    e = j * 2 + k
                    sp.wait_ge(weigh.sem, weigh.at(v - 1, 0))
                    sp.dma_start(w[k][0][:], a["L0_ffn_w1"][bass.ds(e, 1)].rearrange("x (k p) n -> p (x k) n", p=P)).then_inc(w_in[k].sem, 16)
                    sp.dma_start(w[k][1][:], a["L0_ffn_w2"][bass.ds(e, 1)].rearrange("x (k p) n -> p (x k) n", p=P)).then_inc(w_in[k].sem, 16)
                    sp.dma_start(b1[k][:], pr.bias_col[:, bass.ds(e * FC, FC)]).then_inc(w_in[k].sem, 16)
                    sp.dma_start(b2[k][:], pr.bias_col[:, bass.ds(NX * FC + e * EC, EC)]).then_inc(w_in[k].sem, 16)
                    sp.dma_start(comb[k][:], pr.comb[bass.ds(b * TPB, TPB), bass.ds(e, 1), :]
                                 .rearrange("n e t -> e n t").broadcast_to([P, TPB, TILE])).then_inc(comb_in[k].sem, 16)

                batches(sp, before, visit, lambda b: None)

            @block.gpsimd
            def _(pool):
                w_lo.open(pool)

                def visit(i, b, j, k, v, pair, t):
                    for n in range(2):
                        pool.wait_ge(w_hi.sem, w_hi.at(v, n + 1))
                        pool.tensor_tensor(wp[k][n][:, 1], w[k][n][:], wp[k][n][:, 0].bitcast(F32), ALU.subtract).then_inc(w_lo.sem, 1)

                batches(pool, lambda b, i, t: None, visit, lambda b: None)

            @block.scalar
            def _(act):
                stored.open(act)
                w_hi.open(act)
                gelu.open(act)

                def high(v, j, k, pair):
                    act.wait_ge(w_in[k].sem, w_in[k].at(pair, 64))
                    act.wait_ge(sum2.sem, sum2.at(v - 1, FC))
                    for n in range(2):
                        act.copy(wp[k][n][:, 0], w[k][n][:]).then_inc(w_hi.sem, 1)

                def visit(i, b, j, k, v, pair, t):
                    high(v, j, k, pair)
                    for f in range(FC):
                        act.wait_ge(sum1.sem, sum1.at(v, f + 1))
                        act.wait_ge(lo.sem, lo.at(v, f - 1))
                        act.activation(g[f % 2][:], bank1[f % 2].rearrange("p a t -> p (a t)"), ACT.Gelu,
                                       bias=b1[k][:, f:f + 1]).then_inc(gelu.sem, 1)
                        act.wait_ge(sum2.sem, sum2.at(v - 1, f + 1))
                        act.wait_ge(gelu.sem, gelu.at(v, f + 1))
                        act.copy(hid[f][:, 0], g[f % 2][:]).then_inc(hi.sem, 1)

                def before(b, i, t):
                    act.wait_ge(done.sem, done.at(b - 1, 2))
                    tok = bass.ds(b * S, S)
                    act.dma_start(gh[:], pr.gh[:, tok].rearrange("(c p) t -> p c t", p=P)).then_inc(end_in.sem, 16)
                    act.dma_start(x1[:], pr.x1[tok, :].rearrange("(n p) e -> p n e", p=P)).then_inc(end_in.sem, 16)
                    act.dma_start(mod[:], pr.mod_col[bass.ds(b, 1)].rearrange("b p c -> p (b c)")).then_inc(end_in.sem, 16)

                def end(b):
                    act.wait_ge(done.sem, done.at(b, 2))
                    act.dma_start(a["out"][bass.ds(b, 1)].rearrange("b (n p) e -> p (b n) e", p=P), y[:]).then_inc(stored.sem, 16)

                batches(act, before, visit, end)
                act.wait_ge(stored.sem, stored.at(B - 1, 16))

            @block.vector
            def _(dve):
                lo.open(dve)
                weigh.open(dve)
                done.open(dve)

                def visit(i, b, j, k, v, pair, t):
                    for f in range(FC):
                        dve.wait_ge(hi.sem, hi.at(v, f + 1))
                        dve.tensor_tensor(hid[f][:, 1], g[f % 2][:], hid[f][:, 0].bitcast(F32), ALU.subtract).then_inc(lo.sem, 1)
                    dve.wait_ge(sum2.sem, sum2.at(v, FC))
                    dve.wait_ge(comb_in[k].sem, comb_in[k].at(pair, 16))
                    dve.wait_ge(weigh.sem, weigh.at(v - 1, 2 * EC))
                    dve.wait_ge(final.sem, final.at(b, 1))
                    weight = comb[k][:].rearrange("p n t -> p (n t)")
                    for c in range(EC):
                        dve.scalar_tensor_tensor(out=z[c][:], in0=bank2[c].rearrange("p a t -> p (a t)"), scalar=b2[k][:, c:c + 1],
                                                 in1=weight, op0=ALU.add, op1=ALU.mult).then_inc(weigh.sem, 1)
                    for c in range(EC):
                        dve.wait_ge(weigh.sem, weigh.at(v, c + 1))
                        dve.tensor_tensor(acc[:, c, :], acc[:, c, :], z[c][:], ALU.add).then_inc(weigh.sem, 1)

                def before(b, i, t):
                    dve.wait_ge(done.sem, done.at(b - 1, 2))
                    dve.memset(acc[:], 0.0).then_inc(final.sem, 1)

                def end(b):
                    dve.wait_ge(end_in.sem, end_in.at(b, 48))
                    dve.wait_ge(weigh.sem, weigh.at(b * NX + NX - 1, 2 * EC))
                    for c in range(EC):
                        dve.scalar_tensor_tensor(out=acc[:, c, :], in0=acc[:, c, :],
                                                 scalar=mod[:, GB3 * EC + c:GB3 * EC + c + 1],
                                                 in1=gh[:, c, :], op0=ALU.mult, op1=ALU.add).then_inc(final.sem, 1)
                    dve.wait_ge(stored.sem, stored.at(b - 1, 16))
                    for q in range(2):
                        dve.wait_ge(turned.sem, turned.at(b, q + 1))
                        n = S // P // 2
                        dve.tensor_tensor(y[:, q * n:(q + 1) * n, :], bank1[q].rearrange("p a (n e) -> p (a n) e", e=E),
                                          x1[:, q * n:(q + 1) * n, :], ALU.add).then_inc(done.sem, 1)

                batches(dve, before, visit, end)

            @block.tensor
            def _(pe):
                sum2.open(pe)

                def visit(i, b, j, k, v, pair, t):
                    w1 = wp[k][0][:].rearrange("p h (c f m) -> p h c f m", c=EC, f=FC)
                    w2 = wp[k][1][:].rearrange("p h (f c m) -> p h f c m", f=FC, c=EC)
                    products = ((0, 0), (0, 1), (1, 0))

                    def layer1(f):
                        pe.wait_ge(gelu.sem, gelu.at(v, f - 1))
                        for h in range(TPB):
                            for n, (pw, px) in enumerate(products):
                                for c in range(EC):
                                    mm = pe.matmul(bank1[f % 2][:, h, :], w1[:, pw, c, f, :],
                                                   x[t][:, px, c, h * TILE:(h + 1) * TILE],
                                                   start=(n == 0 and c == 0), stop=(n == 2 and c == EC - 1))
                        mm.then_inc(sum1.sem, 1)

                    def layer2(f):
                        pe.wait_ge(hi.sem, hi.at(v, f + 1))
                        pe.wait_ge(lo.sem, lo.at(v, f + 1))
                        if f == 0:
                            pe.wait_ge(weigh.sem, weigh.at(v - 1, EC))
                        for c in range(EC):
                            for h in range(TPB):
                                for n, (pw, px) in enumerate(products):
                                    mm = pe.matmul(bank2[c][:, h, :], w2[:, pw, f, c, :],
                                                   hid[f][:, px, h * TILE:(h + 1) * TILE],
                                                   start=(f == 0 and n == 0), stop=(f == FC - 1 and n == 2),
                                                   skip_group_check=True)
                        mm.then_inc(sum2.sem, 1)

                    pe.wait_ge(x_in[t].sem, x_in[t].at(i, 32))
                    pe.wait_ge(done.sem, done.at(b - 1, 2))
                    pe.wait_ge(w_hi.sem, w_hi.at(v, 2))
                    pe.wait_ge(w_lo.sem, w_lo.at(v, 2))
                    layer1(0)
                    layer1(1)
                    layer1(2)
                    layer2(0)
                    layer1(3)
                    layer2(1)
                    layer2(2)
                    layer2(3)

                def end(b):
                    pe.wait_ge(final.sem, final.at(b, EC + 1))
                    for q in range(2):
                        pe.wait_ge(gelu.sem, gelu.at(b * NX + NX - 1, FC))
                        for n in range(S // P // 2):
                            for c in range(EC):
                                s = (q * S // P // 2 + n) * P
                                mm = pe.transpose(bank1[q].rearrange("p a (n e) -> p (a n) e", e=E)[:, n, c * P:(c + 1) * P],
                                                  acc[:, c, s:s + P], pr.ident[:])
                        mm.then_inc(turned.sem, 1)

                batches(pe, lambda b, i, t: None, visit, end)


def build(nc, a):
    with ExitStack() as ctx:
        pr = Program(nc, ctx, a)
        modulation(pr)
        from_x(pr)
        attention(pr, "a1", pr.q1, pr.k1, pr.v1, pr.o1, pr.den[0], pr.rden1, D1, SIX, True, D1 ** -0.5)
        between(pr)
        attention(pr, "a2", pr.q2, pr.k2, pr.v2, pr.o2, pr.den[1], pr.rden2, D2, NINE, False, D2 ** -0.5)
        route(pr)
        experts(pr)


_INS = ['L0_attn_x', 'L0_attn_Wqa', 'L0_attn_Wqb', 'L0_attn_Wkva', 'L0_attn_Wkvb', 'L0_attn_Wout', 'L0_attn_bout',
        'L0_ffn_q_w', 'L0_ffn_q_b', 'L0_ffn_k_w', 'L0_ffn_k_b', 'L0_ffn_v_w', 'L0_ffn_v_b', 'L0_ffn_o_w',
        'L0_ffn_o_b', 'L0_ffn_router_w', 'L0_ffn_router_b', 'L0_ffn_w1', 'L0_ffn_b1', 'L0_ffn_w2', 'L0_ffn_b2',
        'L0_c', 'L0_wmod']


def rope_tables():
    inv_freq = 1.0 / np.float32(10000.0) ** (np.arange(0, D1, 2, dtype=np.float32) / np.float32(D1))
    angle = np.outer(np.arange(S, dtype=np.float32), inv_freq.astype(np.float32)).astype(np.float32)
    rows = (np.arange(P) % D1) // 2
    return (np.ascontiguousarray(np.cos(angle).T[rows]).astype(np.float32),
            np.ascontiguousarray(np.sin(angle).T[rows]).astype(np.float32))


def kernel(**inputs):
    import concourse.bacc as bacc
    from concourse.bass_utils import run_bass_kernel_spmd

    nc = bacc.Bacc("TRN2", target_bir_lowering=False, num_devices=1)
    arrays = {f"in_{name}": np.ascontiguousarray(inputs[name]) for name in _INS}
    arrays["in_rope_cos"], arrays["in_rope_sin"] = rope_tables()
    a = {name[3:]: nc.dram_tensor(name, v.shape, mybir.dt.from_np(v.dtype), kind="ExternalInput").ap()
         for name, v in arrays.items()}
    a["out"] = nc.dram_tensor("out_0", (B, S, E), F32, kind="ExternalOutput").ap()
    build(nc, a)
    r = run_bass_kernel_spmd(nc, [arrays], core_ids=[0])
    return r.results[0]["out_0"]
```

```python
from contextlib import ExitStack

import numpy as np

import concourse.bass as bass
from concourse import mybir

F32 = mybir.dt.float32
F32R = mybir.dt.float32r
BF16 = mybir.dt.bfloat16
ALU = mybir.AluOpType
ACT = mybir.ActivationFunctionType
AX = mybir.AxisListType

P = 128
B, S, E = 4, 1024, 256
TOK = B * S
TILE = 512
TILES = TOK // TILE
TPB = S // TILE
BLK = TILE // P
EC = E // P
H, KVH = 16, 4
D1 = E // H
QL, KVL = 64, 32
D2 = 8
HQ = 4
UPB = H // HQ
NX, FF = 8, 512
FC = FF // P
EPS = 1e-5
FLOOR = 0.25
MASK = -1.0e30
LOW = -3.0e38
SA, CA, GA, SB, CB, GB, GB3 = range(7)
NMOD = 7


SIX = ((0, 0), (0, 1), (1, 0), (1, 1), (0, 2), (2, 0))
NINE = SIX + ((1, 2), (2, 1), (2, 2))


class Signal:

    def __init__(self, sem, per, credit=0):
        self.sem, self.per, self.credit = sem, per, credit

    def at(self, unit, steps):
        return (unit + self.credit) * self.per + steps

    def open(self, engine):
        engine.sem_inc(self.sem, self.credit * self.per)


class Steps(Signal):

    def __init__(self, sem, names, credit=0):
        super().__init__(sem, len(names), credit)
        self.names = names

    def after(self, unit, name):
        return self.at(unit, self.names.index(name) + 1)


def in_pairs(engine, units, body):
    with engine.Fori(0, units // 2 - 1) as i:
        body(i, False)
    body(units // 2 - 1, True)


class Program:

    def __init__(self, nc, ctx, a):
        self.nc, self.ctx, self.a = nc, ctx, a
        self.sems = 0
        self.bank = ctx.enter_context(nc.psum_tensor("bank", [P, 8, 512], F32))
        self.ident = ctx.enter_context(nc.sbuf_tensor("ident", [P, P], F32))
        self.ident16 = ctx.enter_context(nc.sbuf_tensor("ident16", [P, P], BF16))
        self.mask_kq = ctx.enter_context(nc.sbuf_tensor("mask_kq", [P, P], BF16))
        self.mask_qk = ctx.enter_context(nc.sbuf_tensor("mask_qk", [P, P], BF16))

        def dram(name, shape, dt):
            return nc.dram_tensor(name, shape, dt, kind="Internal").ap()

        self.mod_row = dram("mod_row", [B, NMOD, E], F32)
        self.mod_col = dram("mod_col", [B, P, NMOD * EC], F32)
        self.bias_col = dram("bias_col", [P, NX * (FC + EC)], F32)
        self.q1 = dram("q1", [3, E, TOK], BF16)
        self.k1 = dram("k1", [3, KVH * D1, TOK], BF16)
        self.q2 = dram("q2", [3, H * D2, TOK], BF16)
        self.k2 = dram("k2", [3, H * D2, TOK], BF16)
        self.v1 = dram("v1", [B, KVH, P, S // P, D1 + 1], F32)
        self.v2 = dram("v2", [B, UPB, P, S // P, HQ, D2 + 1], F32)
        self.o1 = dram("o1", [H * D1, TOK], F32)
        self.o2 = dram("o2", [H * D2, TOK], F32)
        self.den = [dram(f"den{n}", [B, H, S], F32) for n in (1, 2)]
        self.rden1 = dram("rden1", [H, D1, TOK], F32)
        self.rden2 = dram("rden2", [H, D2, TOK], F32)
        self.x1 = dram("x1", [TOK, E], F32)
        self.gh = dram("gh", [E, TOK], F32)
        self.mla = dram("mla", [2, E, TOK], F32)
        self.comb = dram("comb", [TILES, NX, TILE], F32)

    def sem(self, name):
        self.sems += 1
        return self.ctx.enter_context(self.nc.semaphore(name))

    def counter(self, name, per, credit=0):
        return Signal(self.sem(name), per, credit)


    def steps(self, name, names, credit=0):
        return Steps(self.sem(name), names, credit)


def modulation(pr):
    nc, a = pr.nc, pr.a
    with ExitStack() as ctx:
        def sb(name, shape, dt=F32):
            return ctx.enter_context(nc.sbuf_tensor(name, shape, dt))

        cT = sb("cT", [P, EC, B])
        sig = sb("sig", [P, EC, B])
        siluT = sb("siluT", [P, EC, B])
        wmod = sb("wmod", [P, EC, 6 * E])
        row = sb("row", [B, NMOD, E])
        sign = sb("sign", [B, 2, E])
        col = sb("col", [P, B, NMOD * EC])
        brow = sb("brow", [NX * (FC + EC), P])
        bcol = sb("bcol", [P, NX * (FC + EC)])

        loaded = pr.sem("m_loaded")
        made = pr.sem("m_made")
        neg_exp = pr.sem("m_neg_exp")
        silu = pr.sem("m_silu")
        summed = pr.sem("m_summed")
        rows = pr.sem("m_rows")
        turned = pr.sem("m_turned")
        cols = pr.sem("m_cols")
        stored = pr.sem("m_stored")
        raw = pr.bank[0:B, 0:3, :].rearrange("b n c -> b (n c)").rearrange("b (j e) -> b j e", e=E)

        with nc.Block() as block:
            @block.sync
            def _(sp):
                sp.dma_start(cT[:, 0, :], a["L0_c"][:, 0:P].rearrange("b p -> p b"),
                             allow_slow_non_contiguous=True).then_inc(loaded, 16)
                sp.dma_start(cT[:, 1, :], a["L0_c"][:, P:E].rearrange("b p -> p b"),
                             allow_slow_non_contiguous=True).then_inc(loaded, 16)
                sp.dma_start(wmod[:], a["L0_wmod"].rearrange("(k p) n -> p k n", p=P)).then_inc(loaded, 16)
                sp.dma_start(brow[0:NX * FC, :],
                             a["L0_ffn_b1"].rearrange("x (f p) -> (x f) p", p=P)).then_inc(loaded, 16)
                sp.dma_start(brow[NX * FC:NX * (FC + EC), :],
                             a["L0_ffn_b2"].rearrange("x (f p) -> (x f) p", p=P)).then_inc(loaded, 16)
                sp.wait_ge(rows, 12)
                sp.dma_start(pr.mod_row, row[:]).then_inc(stored, 16)
                sp.wait_ge(cols, 2)
                sp.dma_start(pr.mod_col.rearrange("b p c -> p b c"), col[:]).then_inc(stored, 16)
                sp.dma_start(pr.bias_col, bcol[:]).then_inc(stored, 16)
                sp.wait_ge(stored, 48)

            @block.gpsimd
            def _(pool):
                for m in (pr.ident, pr.ident16, pr.mask_kq, pr.mask_qk):
                    pool.memset(m[:], 0.0).then_inc(made, 1)
                pool.wait_ge(made, 4)
                for m in (pr.ident, pr.ident16):
                    pool.affine_select(out=m[:], in_=m[:], compare_op=ALU.not_equal, fill=1.0, base=0,
                                       pattern=[[-1, P]], channel_multiplier=1).then_inc(made, 1)
                pool.affine_select(out=pr.mask_kq[:], in_=pr.mask_kq[:], compare_op=ALU.is_ge, fill=MASK,
                                   base=0, pattern=[[1, P]], channel_multiplier=-1).then_inc(made, 1)
                pool.affine_select(out=pr.mask_qk[:], in_=pr.mask_qk[:], compare_op=ALU.is_ge, fill=MASK,
                                   base=0, pattern=[[-1, P]], channel_multiplier=1).then_inc(made, 1)

            @block.scalar
            def _(act):
                act.wait_ge(loaded, 80)
                act.activation(sig[:], cT[:], ACT.Exp, scale=-1.0).then_inc(neg_exp, 1)

            @block.vector
            def _(dve):
                dve.wait_ge(neg_exp, 1)
                dve.tensor_scalar(sig[:], sig[:], 1.0, None, ALU.add).then_inc(silu, 1)
                dve.wait_ge(silu, 1)
                dve.reciprocal(sig[:], sig[:]).then_inc(silu, 1)
                dve.wait_ge(silu, 2)
                dve.tensor_tensor(siluT[:], cT[:], sig[:], ALU.mult).then_inc(silu, 1)
                dve.wait_ge(summed, 1)
                for j, f in ((SA, None), (SB, None), (CA, 1.0), (CB, 1.0)):
                    if f is None:
                        dve.tensor_copy(row[:, j, :], raw[:, j, :]).then_inc(rows, 1)
                    else:
                        dve.tensor_scalar(row[:, j, :], raw[:, j, :], f, None, ALU.add).then_inc(rows, 1)
                for n, j in enumerate((GA, GB)):
                    dve.tensor_scalar(sign[:, n, :], raw[:, j, :], 0.0, 2.0, ALU.is_ge, ALU.mult).then_inc(rows, 1)
                dve.wait_ge(rows, 6)
                dve.tensor_scalar(sign[:], sign[:], -1.0, None, ALU.add).then_inc(rows, 1)
                dve.wait_ge(rows, 7)
                for n, j in enumerate((GA, GB)):
                    dve.tensor_tensor(row[:, j, :], raw[:, j, :], sign[:, n, :], ALU.mult).then_inc(rows, 1)
                dve.wait_ge(rows, 9)
                for n, j in enumerate((GA, GB)):
                    dve.scalar_tensor_tensor(out=row[:, j, :], in0=row[:, j, :], scalar=FLOOR,
                                             in1=sign[:, n, :], op0=ALU.max, op1=ALU.mult).then_inc(rows, 1)
                dve.wait_ge(rows, 11)
                dve.tensor_scalar(row[:, GB3, :], row[:, GB, :], 0.3, None, ALU.mult).then_inc(rows, 1)
                dve.wait_ge(turned, 1)
                dve.tensor_copy(col[:], pr.bank[:, 4, 0:NMOD * EC * B].rearrange("p (c b) -> p b c", b=B)).then_inc(cols, 1)
                dve.tensor_copy(bcol[:], pr.bank[:, 5, 0:NX * (FC + EC)]).then_inc(cols, 1)

            @block.tensor
            def _(pe):
                pe.wait_ge(silu, 3)
                for n in range(3):
                    for k in range(EC):
                        mm = pe.matmul(pr.bank[0:B, n, :], siluT[:, k, :], wmod[:, k, n * 512:(n + 1) * 512],
                                       start=(k == 0), stop=(k == EC - 1))
                mm.then_inc(summed, 1)
                pe.wait_ge(made, 8)
                pe.wait_ge(rows, 12)
                flat = row[:].rearrange("b j e -> b (j e)")
                for c in range(NMOD * EC):
                    pe.transpose(pr.bank[:, 4, c * B:(c + 1) * B], flat[:, c * P:(c + 1) * P], pr.ident[0:B, 0:B])
                n = NX * (FC + EC)
                pe.transpose(pr.bank[:, 5, 0:n], brow[:], pr.ident[0:n, 0:n]).then_inc(turned, 1)


class Norm:

    def __init__(self, pr, sb, name, shift, scale):
        self.pr, self.shift, self.scale = pr, shift, scale
        self.stats = sb(name + "_stats", [P, BLK, 6])
        self.mean = sb(name + "_mean", [P, BLK])
        self.diff = sb(name + "_diff", [P, BLK])
        self.var = sb(name + "_var", [P, BLK])
        self.rstd = sb(name + "_rstd", [P, BLK])
        self.power = sb(name + "_power", [P, BLK])
        self.xn = sb(name + "_xn", [P, BLK, E])
        self.hT = sb(name + "_hT", [P, EC, TILE])
        self.stat = pr.counter(name + "_stat", BLK + 6)
        self.var_ready = pr.counter(name + "_var_ready", 1)
        self.rstd_ready = pr.counter(name + "_rstd_ready", 1)
        self.xn_ready = pr.counter(name + "_xn_ready", 1)
        self.turned = pr.counter(name + "_turned", 1, credit=1)
        self.h_ready = pr.counter(name + "_h_ready", EC, credit=1)

    def open(self, engine, which):
        {"pe": self.turned, "act": self.h_ready}[which].open(engine)

    def statistics(self, dve, n, x):
        for b in range(BLK):
            dve.bn_stats(self.stats[:, b, :], x[:, b, :]).then_inc(self.stat.sem, 1)
        even, odd = (self.stats[:, :, 1], self.stats[:, :, 2]), (self.stats[:, :, 4], self.stats[:, :, 5])
        sem, at = self.stat.sem, self.stat.at
        dve.wait_ge(sem, at(n, BLK))
        dve.tensor_tensor(self.mean[:], even[0], odd[0], ALU.add).then_inc(sem, 1)
        dve.tensor_tensor(self.diff[:], even[0], odd[0], ALU.subtract).then_inc(sem, 1)
        dve.tensor_tensor(self.var[:], even[1], odd[1], ALU.add).then_inc(sem, 1)
        dve.wait_ge(sem, at(n, BLK + 3))
        dve.tensor_scalar(self.mean[:], self.mean[:], 0.5, None, ALU.mult).then_inc(sem, 1)
        dve.tensor_scalar(self.var[:], self.var[:], 1.0 / E, EPS, ALU.mult, ALU.add).then_inc(sem, 1)
        dve.scalar_tensor_tensor(out=self.diff[:], in0=self.diff[:], scalar=0.25, in1=self.diff[:],
                                 op0=ALU.mult, op1=ALU.mult).then_inc(sem, 1)
        dve.wait_ge(sem, at(n, BLK + 6))
        dve.tensor_tensor(self.var[:], self.var[:], self.diff[:], ALU.add).then_inc(self.var_ready.sem, 1)

    def normalise(self, dve, n, x):
        dve.wait_ge(self.turned.sem, self.turned.at(n - 1, 1))
        dve.wait_ge(self.rstd_ready.sem, self.rstd_ready.at(n, 1))
        for b in range(BLK):
            op = dve.tensor_scalar(self.xn[:, b, :], x[:, b, :], self.mean[:, b:b + 1], self.rstd[:, b:b + 1],
                                   ALU.subtract, ALU.mult)
        op.then_inc(self.xn_ready.sem, 1)

    def pool(self, pool, n):
        pool.wait_ge(self.var_ready.sem, self.var_ready.at(n, 1))
        pool.tensor_tensor(self.rstd[:], self.var[:], self.power[:], ALU.pow).then_inc(self.rstd_ready.sem, 1)

    def pe(self, pe, n):
        pe.wait_ge(self.xn_ready.sem, self.xn_ready.at(n, 1))
        for c in range(EC):
            for b in range(BLK):
                mm = pe.transpose(self.pr.bank[:, c, b * P:(b + 1) * P], self.xn[:, b, c * P:(c + 1) * P],
                                  self.pr.ident[:])
        mm.then_inc(self.turned.sem, 1)

    def act(self, act, n, mod):
        act.wait_ge(self.turned.sem, self.turned.at(n, 1))
        for c in range(EC):
            sc, sh = self.scale * EC + c, self.shift * EC + c
            act.activation(self.hT[:, c, :], self.pr.bank[:, c, :], ACT.Identity,
                           bias=mod[:, sh:sh + 1], scale=mod[:, sc:sc + 1]).then_inc(self.h_ready.sem, 1)


def from_x(pr):
    nc, a = pr.nc, pr.a
    LAT = QL + KVL
    R = slice(QL, LAT)
    NK = KVH * D1
    ROWS = (P, P, NK)
    with ExitStack() as ctx:
        def sb(name, shape, dt=F32):
            return ctx.enter_context(nc.sbuf_tensor(name, shape, dt))

        x = sb("p1_x", [P, 2, BLK, E])
        mod = sb("p1_mod", [P, 2, NMOD * EC])
        norm = Norm(pr, sb, "p1", SA, CA)
        wa = sb("p1_wa", [P, EC, LAT])
        wq = sb("p1_wq", [LAT, E])
        wq_turn = sb("p1_wq_turn", [LAT, E])
        wkv = sb("p1_wkv", [LAT, 2 * NK])
        wk = sb("p1_wk", [LAT, NK])
        wk_turn = sb("p1_wk_turn", [LAT, NK])
        wv = sb("p1_wv", [LAT, NK])
        cos = sb("p1_cos", [P, S])
        sin = sb("p1_sin", [P, S])
        lat = sb("p1_lat", [LAT, TILE])
        rotated = [sb(f"p1_rotated{c}", [ROWS[c], TILE]) for c in range(3)]
        rest = [sb(f"p1_rest{c}", [ROWS[c], TILE]) for c in range(3)]
        parts = [[sb(f"p1_part{k}{c}", [ROWS[c], 3, TILE], BF16) for c in range(3)] for k in range(2)]
        v = [sb(f"p1_v{k}", [P, KVH, BLK, D1 + 1]) for k in range(2)]
        sums = [pr.bank[0:ROWS[c], (3, 5, 3)[c], :] for c in range(3)]
        turns = [pr.bank[0:ROWS[c], (4, 6, 4)[c], :] for c in range(3)]

        loaded = pr.sem("p1_loaded")
        filled = pr.sem("p1_filled")
        weights = pr.sem("p1_weights")
        x_in = [pr.counter(f"p1_x_in{k}", 32) for k in range(2)]
        lat_sum = pr.counter("p1_lat_sum", 1)
        lat_ready = pr.counter("p1_lat_ready", 1)
        qk_sum = pr.counter("p1_qk_sum", 3)
        v_sum = pr.counter("p1_v_sum", 1)
        v_ready = pr.counter("p1_v_ready", 1, credit=1)
        steps = pr.steps("p1_steps", ("cos0", "sin0", "add0", "cos1", "sin1", "add1", "less0_0", "cos2", "sin2",
                                      "less0_1", "less1_0", "less1_1"), credit=1)
        steps_k = pr.steps("p1_steps_k", ("add2", "less0_2", "less1_2"), credit=1)
        casts = pr.steps("p1_casts", ("cast0_0", "cast0_1", "cast1_0", "cast1_1", "cast2_0", "cast0_2",
                                      "cast2_1", "cast1_2", "cast2_2"), credit=1)
        stored = [pr.counter(f"p1_stored{k}", 64, credit=1) for k in range(2)]

        with nc.Block() as block:
            @block.sync
            def _(sp):
                stored[0].open(sp)
                stored[1].open(sp)

                def load(i, k):
                    sp.dma_start(x[:, k], a["L0_attn_x"][bass.ds(i, 1), k * TILE:(k + 1) * TILE, :]
                                 .rearrange("b (n p) e -> p (b n) e", p=P)).then_inc(x_in[k].sem, 16)
                    sp.dma_start(mod[:, k], pr.mod_col[bass.ds(i, 1)].rearrange("b p c -> p (b c)")).then_inc(x_in[k].sem, 16)

                load(0, 0)
                sp.dma_start(wkv[R, :], a["L0_attn_Wkvb"]).then_inc(loaded, 16)
                sp.dma_start(wa[:, :, 0:QL], a["L0_attn_Wqa"].rearrange("(k p) n -> p k n", p=P)).then_inc(loaded, 16)
                sp.dma_start(wa[:, :, QL:LAT], a["L0_attn_Wkva"].rearrange("(k p) n -> p k n", p=P)).then_inc(loaded, 16)
                sp.wait_ge(filled, 1)
                sp.dma_start(wq[0:QL, :], a["L0_attn_Wqb"]).then_inc(loaded, 16)
                sp.dma_start(cos[:], a["rope_cos"]).then_inc(loaded, 16)
                sp.dma_start(sin[:], a["rope_sin"]).then_inc(loaded, 16)
                load(0, 1)

                def pair(i, last):
                    for k in range(TPB):
                        n = i * TPB + k
                        if not last:
                            sp.wait_ge(norm.h_ready.sem, norm.h_ready.at(n, EC))
                            load(i + 1, k)
                        tok = bass.ds(n * TILE, TILE)
                        sp.wait_ge(v_ready.sem, v_ready.at(n, 1))
                        sp.dma_start(pr.v1[bass.ds(i, 1), :, :, k * BLK:(k + 1) * BLK, :].rearrange("b g p n d -> p (b g) (n d)"),
                                     v[k][:].rearrange("p g n d -> p g (n d)")).then_inc(stored[k].sem, 16)
                        sp.wait_ge(casts.sem, casts.after(n, "cast2_1"))
                        for c in range(2):
                            sp.dma_start(pr.q1[:, c * P:(c + 1) * P, tok].rearrange("s p t -> p s t"),
                                         parts[k][c][:]).then_inc(stored[k].sem, 16)
                        sp.wait_ge(casts.sem, casts.after(n, "cast2_2"))
                        sp.dma_start(pr.k1[:, :, tok].rearrange("s p t -> p s t"), parts[k][2][:]).then_inc(stored[k].sem, 16)

                in_pairs(sp, TILES, pair)
                for k in range(2):
                    sp.wait_ge(stored[k].sem, stored[k].at(B - 1, 64))

            @block.gpsimd
            def _(pool):
                steps_k.open(pool)
                pool.memset(wq[:], 0.0).then_inc(filled, 1)
                for t in (wq_turn, wk, wk_turn, wv):
                    pool.memset(t[:], 0.0).then_inc(filled, 1)
                pool.memset(norm.power[:], -0.5).then_inc(filled, 1)
                for k in range(2):
                    pool.memset(v[k][:], 1.0).then_inc(filled, 1)
                pool.wait_ge(filled, 8)
                norm.pool(pool, 0)

                def pair(i, last):
                    for k in range(TPB):
                        n = i * TPB + k
                        if k == 0 or not last:
                            norm.pool(pool, n + 1)
                        pool.wait_ge(steps.sem, steps.after(n, "sin2"))
                        pool.tensor_tensor(rotated[2][:], rotated[2][:], rest[2][:], ALU.add).then_inc(steps_k.sem, 1)
                        pool.wait_ge(casts.sem, casts.after(n, "cast0_2"))
                        pool.tensor_tensor(rest[2][:], rotated[2][:], parts[k][2][:, 0, :], ALU.subtract).then_inc(steps_k.sem, 1)
                        pool.wait_ge(casts.sem, casts.after(n, "cast1_2"))
                        pool.tensor_tensor(rest[2][:], rest[2][:], parts[k][2][:, 1, :], ALU.subtract).then_inc(steps_k.sem, 1)

                in_pairs(pool, TILES, pair)

            @block.scalar
            def _(act):
                norm.open(act, "act")
                v_ready.open(act)
                casts.open(act)
                act.wait_ge(filled, 8)

                def latents(n, k):
                    norm.act(act, n, mod[:, k])

                def copy_latents(n):
                    act.wait_ge(lat_sum.sem, lat_sum.at(n, 1))
                    act.copy(lat[:], pr.bank[0:LAT, 2, :]).then_inc(lat_ready.sem, 1)

                latents(0, 0)
                copy_latents(0)

                def pair(i, last):
                    for k in range(TPB):
                        n = i * TPB + k
                        more = k == 0 or not last

                        def cast(part, c):
                            sig = steps_k if c == 2 else steps
                            act.wait_ge(sig.sem, sig.after(n, f"less{part - 1}_{c}" if part else f"add{c}"))
                            act.copy(parts[k][c][:, part, :], (rest if part else rotated)[c][:]).then_inc(casts.sem, 1)

                        act.wait_ge(stored[k].sem, stored[k].at(i - 1, 64))
                        cast(0, 0)
                        act.wait_ge(v_sum.sem, v_sum.at(n, 1))
                        act.copy(v[k][:, :, :, 0:D1].rearrange("p g n d -> p n g d"),
                                 pr.bank[:, 7, 0:BLK * NK].rearrange("p (n g d) -> p n g d", n=BLK, g=KVH)).then_inc(v_ready.sem, 1)
                        cast(0, 1)
                        if more:
                            latents(n + 1, 1 - k)
                        cast(1, 0)
                        cast(1, 1)
                        if more:
                            copy_latents(n + 1)
                        cast(2, 0)
                        cast(0, 2)
                        cast(2, 1)
                        cast(1, 2)
                        cast(2, 2)

                in_pairs(act, TILES, pair)

            @block.vector
            def _(dve):
                steps.open(dve)
                dve.wait_ge(x_in[0].sem, x_in[0].at(0, 32))
                norm.statistics(dve, 0, x[:, 0])
                norm.normalise(dve, 0, x[:, 0])
                dve.wait_ge(loaded, 96)
                dve.wait_ge(filled, 5)
                dve.tensor_copy(wk[R, :], wkv[R, 0::2])
                dve.tensor_copy(wv[R, :], wkv[R, 1::2])
                for to, of in ((wq_turn[0:QL], wq[0:QL]), (wk_turn[R], wkv[R, 0::2])):
                    dve.tensor_scalar(to[:, 0::2], of[:, 1::2], -1.0, None, ALU.mult)
                    dve.tensor_copy(to[:, 1::2], of[:, 0::2]).then_inc(weights, 1)

                def pair(i, last):
                    for k in range(TPB):
                        n = i * TPB + k
                        more = k == 0 or not last
                        pos = slice(k * TILE, (k + 1) * TILE)

                        def rotate(c):
                            dve.wait_ge(casts.sem, casts.after(n - 1, f"cast2_{c}"))
                            dve.wait_ge(qk_sum.sem, qk_sum.at(n, c + 1))
                            dve.tensor_tensor(rotated[c][:], sums[c], cos[0:ROWS[c], pos], ALU.mult).then_inc(steps.sem, 1)
                            dve.tensor_tensor(rest[c][:], turns[c], sin[0:ROWS[c], pos], ALU.mult).then_inc(steps.sem, 1)

                        def add(c):
                            dve.wait_ge(steps.sem, steps.after(n, f"sin{c}"))
                            dve.tensor_tensor(rotated[c][:], rotated[c][:], rest[c][:], ALU.add).then_inc(steps.sem, 1)

                        def less(part, c):
                            dve.wait_ge(casts.sem, casts.after(n, f"cast{part}_{c}"))
                            dve.tensor_tensor(rest[c][:], (rest if part else rotated)[c][:], parts[k][c][:, part, :],
                                              ALU.subtract).then_inc(steps.sem, 1)

                        if more:
                            dve.wait_ge(x_in[1 - k].sem, x_in[1 - k].at(i + k, 32))
                            norm.statistics(dve, n + 1, x[:, 1 - k])
                        rotate(0)
                        add(0)
                        if more:
                            norm.normalise(dve, n + 1, x[:, 1 - k])
                        rotate(1)
                        add(1)
                        less(0, 0)
                        rotate(2)
                        less(0, 1)
                        less(1, 0)
                        less(1, 1)

                in_pairs(dve, TILES, pair)

            @block.tensor
            def _(pe):
                norm.open(pe, "pe")
                pe.wait_ge(weights, 2)
                pe.wait_ge(loaded, 96)

                def latents(n):
                    norm.pe(pe, n)
                    for c in range(EC):
                        pe.wait_ge(norm.h_ready.sem, norm.h_ready.at(n, c + 1))
                        mm = pe.matmul(pr.bank[0:LAT, 2, :], wa[:, c, :], norm.hT[:, c, :],
                                       start=(c == 0), stop=(c == EC - 1))
                    mm.then_inc(lat_sum.sem, 1)

                latents(0)

                def pair(i, last):
                    for k in range(TPB):
                        n = i * TPB + k
                        pe.wait_ge(lat_ready.sem, lat_ready.at(n, 1))
                        pe.wait_ge(steps.sem, steps.after(n - 1, "sin2"))
                        for c in range(3):
                            cols = slice(0, NK) if c == 2 else slice(c * P, (c + 1) * P)
                            if c == 2:
                                pe.wait_ge(steps.sem, steps.after(n, "sin0"))
                            pe.matmul(sums[c], (wq, wq, wk)[c][:, cols], lat[:], start=True, stop=True)
                            pe.matmul(turns[c], (wq_turn, wq_turn, wk_turn)[c][:, cols], lat[:],
                                      start=True, stop=True).then_inc(qk_sum.sem, 1)
                        pe.wait_ge(v_ready.sem, v_ready.at(n - 1, 1))
                        for b in range(BLK):
                            mm = pe.matmul(pr.bank[:, 7, b * NK:(b + 1) * NK], lat[:, b * P:(b + 1) * P], wv[:],
                                           start=True, stop=True, skip_group_check=True)
                        mm.then_inc(v_sum.sem, 1)
                        if k == 0 or not last:
                            latents(n + 1)

                in_pairs(pe, TILES, pair)


def attention(pr, name, q, k, v, o, sums, rden, width, pairs, causal, scale):
    nc = pr.nc
    R = len(pairs) * width
    JK = 1 if causal else HQ
    KB, QB = S // P, S // P
    steps = [(t, kb) for t in range(TPB) for kb in range(KB) if not causal or kb * P < (t + 1) * TILE]
    L = len(steps)
    ends = [max(s for s in range(L) if steps[s][0] == t) for t in range(TPB)]
    looks = [(j, i, c) for j in range(HQ) for i in range(QB) for c in range(TPB)
             if not causal or c * TILE < (i + 1) * P]
    NL = len(looks)
    LPS = NL // L
    assert NL == LPS * L
    AHEAD = 2 * LPS

    with ExitStack() as ctx:
        def sb(n, shape, dt=F32):
            return ctx.enter_context(nc.sbuf_tensor(f"{name}_{n}", shape, dt))

        Q = [sb(f"Q{g}", [R + 2, HQ, S], BF16) for g in range(UPB)]
        K = [sb(f"K{g}", [R + 2, JK, S], BF16) for g in range(UPB)]
        V = [sb(f"V{g}", [P, JK, KB, width + 1] if causal else [P, KB, JK, width + 1]) for g in range(UPB)]
        prob = [sb(f"prob{n}", [P, HQ, TILE]) for n in range(2)]
        out = [sb(f"out{t}", [P, TILE]) for t in range(TPB)]
        peak = sb("peak", [P, HQ * QB, TPB])
        top = sb("top", [P, HQ * QB])
        top_hi = [sb(f"top_hi{g}", [HQ * QB, P], BF16) for g in range(UPB)]
        top_lo = [sb(f"top_lo{g}", [HQ * QB, P], BF16) for g in range(UPB)]
        den = sb("den", [P, HQ * S // P])
        rden_sq = sb("rden_sq", [P, HQ * S // P])
        scores = pr.bank[:, 0:4, :]
        acc = pr.bank[:, 4:6, :]
        look = pr.bank[:, 6:8, :]

        nload = 2 * len(pairs) + 1
        filled = pr.sem(name + "_filled")
        cleared = pr.sem(name + "_cleared")
        loaded = [pr.counter(f"{name}_loaded{g}", 16 * nload) for g in range(UPB)]
        shift_in = [pr.counter(f"{name}_shift_in{g}", 32, credit=1) for g in range(UPB)]
        qk_done = pr.counter(name + "_qk_done", 2 * L)
        exp_done = pr.counter(name + "_exp_done", 2 * L, credit=1)
        pv_done = pr.counter(name + "_pv_done", L, credit=1)
        taken = [pr.counter(f"{name}_taken{t}", 1, credit=1) for t in range(TPB)]
        stored = [pr.counter(f"{name}_stored{t}", 16 * (HQ + 1), credit=1 + t) for t in range(TPB)]
        den_in = pr.counter(name + "_den_in", 16, credit=1)
        den_done = pr.counter(name + "_den_done", 1)
        den_out = pr.counter(name + "_den_out", 16 * HQ, credit=2)
        look_done = pr.counter(name + "_look_done", NL)
        look_read = pr.counter(name + "_look_read", NL, credit=1)
        topped = pr.counter(name + "_topped", 1, credit=1)
        turned = pr.counter(name + "_turned", 1)
        rows_made = pr.counter(name + "_rows_made", 2)

        def units(engine, body):
            with engine.Fori(0, B - 1) as b:
                for g in range(UPB):
                    body(b, g, 2)
            for g in range(UPB):
                body(B - 1, g, min(2, UPB - 1 - g))

        def after(b, g):
            return (b, g + 1) if g < UPB - 1 else (b + 1, 0)

        def looks_of(b, g, s, more):
            if s < L - 2:
                return (*after(b, g), AHEAD + s * LPS, AHEAD + (s + 1) * LPS) if more else None
            first = (s - (L - 2)) * LPS
            return (*after(*after(b, g)), first, first + LPS) if more == 2 else None

        with nc.Block() as block:
            @block.sync
            def _(sp):
                for s in shift_in + stored + [den_in, den_out]:
                    s.open(sp)

                def load(b, g):
                    tok = bass.ds(b * S, S)
                    sem = loaded[g].sem
                    for n, (qi, ki) in enumerate(pairs):
                        rows = slice(n * width, (n + 1) * width)
                        for slot, of, part, heads in ((Q[g], q, qi, HQ), (K[g], k, ki, JK)):
                            feats = of[part, g * heads * width:(g + 1) * heads * width, tok]
                            sp.dma_start(slot[rows, :, :], feats.rearrange("(j d) t -> d j t", d=width)).then_inc(sem, 16)
                    sp.dma_start(V[g][:].rearrange("p a b d -> p (a b d)"),
                                 v[bass.ds(b, 1), g].rearrange("b p n d -> (b p) (n d)" if causal
                                                               else "b p n j d -> (b p) (n j d)")).then_inc(sem, 16)

                def shift(b, g):
                    sp.wait_ge(rows_made.sem, rows_made.at(b * UPB + g, 2))
                    for r, part in ((R, top_hi[g]), (R + 1, top_lo[g])):
                        sp.dma_start(Q[g][r:r + 1, :, :].rearrange("o j (i q) -> o (j i) q", q=P),
                                     part[:]).then_inc(shift_in[g].sem, 16)

                sp.wait_ge(filled, UPB)
                for g in range(UPB):
                    load(0, g)
                shift(0, 0)

                def unit(b, g, more):
                    u = b * UPB + g
                    if more:
                        shift(*after(b, g))
                    for t in range(TPB):
                        sp.wait_ge(taken[t].sem, taken[t].at(u, 1))
                        tok = bass.ds(b * S + t * TILE, TILE)
                        for j in range(HQ):
                            f = (g * HQ + j) * width
                            sp.dma_start(o[f:f + width, tok], out[t][32 * j:32 * j + width, :]).then_inc(stored[t].sem, 16)
                        sp.dma_start(sums[bass.ds(b, 1), g * HQ:(g + 1) * HQ, t * TILE:(t + 1) * TILE]
                                     .rearrange("b h t -> (b h) t"), out[t][width::32, :]).then_inc(stored[t].sem, 16)
                    for t in range(TPB):
                        sp.wait_ge(stored[t].sem, stored[t].at(u, 16 * (HQ + 1)))
                    sp.wait_ge(den_done.sem, den_done.at(u, 1))
                    sp.dma_start(den[:], sums[bass.ds(b, 1), g * HQ:(g + 1) * HQ, :]
                                 .rearrange("b h (s t) -> (b h s) t", t=HQ * S // P)).then_inc(den_in.sem, 16)
                    if more and not isinstance(b, int):
                        load(b + 1, g)
                    sp.wait_ge(den_done.sem, den_done.at(u + 1, 1))
                    for j in range(HQ):
                        n = P // HQ
                        part = rden_sq[j * n:(j + 1) * n, :]
                        sp.dma_start(rden[g * HQ + j][:, bass.ds(b * S, S)].rearrange("d (s t) -> s d t", s=n),
                                     part.unsqueeze(1).broadcast_to([n, width, S // n])).then_inc(den_out.sem, 16)

                units(sp, unit)
                for t in range(TPB):
                    sp.wait_ge(stored[t].sem, stored[t].at(B * UPB - 1, 16 * (HQ + 1)))
                sp.wait_ge(den_out.sem, den_out.at(B * UPB - 1, 16 * HQ))

            @block.gpsimd
            def _(pool):
                for g in range(UPB):
                    pool.memset(K[g][:], -1.0).then_inc(filled, 1)

            @block.scalar
            def _(act):
                exp_done.open(act)
                taken[0].open(act)
                act.wait_ge(cleared, 3)

                def take(t, u):
                    act.wait_ge(pv_done.sem, pv_done.at(u, ends[t] + 1))
                    act.wait_ge(stored[t].sem, stored[t].at(u - 1, 16 * (HQ + 1)))
                    act.copy(out[t][:], acc[:, t, :]).then_inc(taken[t].sem, 1)

                def unit(b, g, more):
                    u = b * UPB + g
                    for s, (t, kb) in enumerate(steps):
                        off = max(0, kb * P - t * TILE) if causal else 0
                        act.wait_ge(pv_done.sem, pv_done.at(u, s - 1))
                        for n in range(2):
                            act.wait_ge(qk_done.sem, qk_done.at(u, 2 * s + n + 1))
                            act.activation(prob[s % 2][:, 2 * n:2 * n + 2, off:], scores[:, 2 * n:2 * n + 2, off:],
                                           ACT.Exp, scale=scale).then_inc(exp_done.sem, 1)
                        if s == 1:
                            take(1, u - 1)
                        if s == ends[0] + 2:
                            take(0, u)

                units(act, unit)
                take(1, B * UPB - 1)

            @block.vector
            def _(dve):
                look_read.open(dve)
                topped.open(dve)
                dve.memset(peak[:], LOW).then_inc(cleared, 1)
                dve.memset(den[:], 1.0).then_inc(cleared, 1)
                dve.memset(acc, 0.0).then_inc(cleared, 1)
                dve.wait_ge(cleared, 3)

                def peaks(b, g, first, last):
                    u = b * UPB + g
                    for m in range(first, last):
                        j, i, c = looks[m]
                        n = min(TILE, (i + 1) * P - c * TILE) if causal else TILE
                        dve.wait_ge(look_done.sem, look_done.at(u, m + 1))
                        if m == 0:
                            dve.wait_ge(topped.sem, topped.at(u - 1, 1))
                        dve.tensor_reduce(peak[:, j * QB + i, c:c + 1], look[:, m % 2, 0:n], AX.X,
                                          ALU.max).then_inc(look_read.sem, 1)

                def summits(b, g):
                    u = b * UPB + g
                    dve.wait_ge(look_read.sem, look_read.at(u, NL))
                    dve.tensor_reduce(top[:], peak[:], AX.X, ALU.max).then_inc(topped.sem, 1)

                def rows(b, g):
                    u = b * UPB + g
                    dve.wait_ge(turned.sem, turned.at(u, 1))
                    dve.wait_ge(shift_in[g].sem, shift_in[g].at(b - 1, 32))
                    dve.tensor_copy(top_hi[g][:], acc[0:HQ * QB, 0, 0:P]).then_inc(rows_made.sem, 1)
                    dve.wait_ge(rows_made.sem, rows_made.at(u, 1))
                    dve.tensor_tensor(top_lo[g][:], acc[0:HQ * QB, 0, 0:P], top_hi[g][:], ALU.subtract).then_inc(rows_made.sem, 1)

                peaks(0, 0, 0, NL)
                summits(0, 0)
                rows(0, 0)
                peaks(0, 1, 0, AHEAD)

                def invert(u):
                    dve.wait_ge(den_in.sem, den_in.at(u, 16))
                    dve.wait_ge(den_out.sem, den_out.at(u - 1, 16 * HQ))
                    dve.reciprocal(rden_sq[:], den[:]).then_inc(den_done.sem, 1)

                def unit(b, g, more):
                    for s in range(L):
                        at = looks_of(b, g, s, more)
                        if s == L - 5:
                            invert(b * UPB + g - 1)
                        if at:
                            peaks(*at[:3], at[2] + 2)
                        if s == L - 2 and more:
                            rows(*after(b, g))
                        if at:
                            peaks(*at[:2], at[2] + 2, at[3])
                        if s == L - 3 and more:
                            summits(*after(b, g))

                units(dve, unit)
                invert(B * UPB - 1)

            @block.tensor
            def _(pe):
                pv_done.open(pe)
                pe.wait_ge(cleared, 3)

                def look_for(b, g, first, last):
                    u = b * UPB + g
                    if first == 0:
                        pe.wait_ge(loaded[g].sem, loaded[g].at(b + 1, 0))
                    for m in range(first, last):
                        j, i, c = looks[m]
                        n = min(TILE, (i + 1) * P - c * TILE) if causal else TILE
                        diag = causal and c == i * P // TILE
                        pe.wait_ge(look_read.sem, look_read.at(u, m - 1))
                        mm = pe.matmul(look[:, m % 2, 0:n], Q[g][0:R, j, i * P:(i + 1) * P],
                                       K[g][0:R, j % JK, c * TILE:c * TILE + n], start=True, stop=not diag)
                        if diag:
                            mm = pe.matmul(look[:, m % 2, n - P:n], pr.ident16[:], pr.mask_qk[:], start=False, stop=True)
                        mm.then_inc(look_done.sem, 1)

                def turn(b, g):
                    pe.wait_ge(topped.sem, topped.at(b * UPB + g, 1))
                    pe.transpose(acc[0:HQ * QB, 0, 0:P], top[:], pr.ident[:]).then_inc(turned.sem, 1)

                def score(b, g, s, n):
                    u = b * UPB + g
                    t, kb = steps[s]
                    off = max(0, kb * P - t * TILE) if causal else 0
                    diag = causal and kb * P >= t * TILE
                    if s == 0 and n == 0:
                        pe.wait_ge(shift_in[g].sem, shift_in[g].at(b, 32))
                    pe.wait_ge(exp_done.sem, exp_done.at(u, 2 * s - 2 + n + 1))
                    for j in (2 * n, 2 * n + 1):
                        mm = pe.matmul(scores[:, j, off:], K[g][:, j % JK, kb * P:(kb + 1) * P],
                                       Q[g][:, j, t * TILE + off:(t + 1) * TILE], start=True, stop=not diag)
                        if diag:
                            mm = pe.matmul(scores[:, j, off:off + P], pr.ident16[:], pr.mask_kq[:], start=False, stop=True)
                    mm.then_inc(qk_done.sem, 1)

                look_for(0, 0, 0, NL)
                turn(0, 0)
                look_for(0, 1, 0, AHEAD)
                score(0, 0, 0, 0)
                score(0, 0, 0, 1)

                def unit(b, g, more):
                    u = b * UPB + g
                    for s, (t, kb) in enumerate(steps):
                        off = max(0, kb * P - t * TILE) if causal else 0
                        at = looks_of(b, g, s, more)
                        ahead = (b, g, s + 1) if s < L - 1 else (*after(b, g), 0)
                        if at:
                            look_for(*at[:3], at[2] + 2)
                        if s == L - 2 and more:
                            pe.wait_ge(taken[0].sem, taken[0].at(u, 1))
                            turn(*after(b, g))
                        if s < L - 1 or more:
                            score(*ahead, 0)
                            score(*ahead, 1)
                        if at:
                            look_for(*at[:2], at[2] + 2, at[3])
                        pe.wait_ge(exp_done.sem, exp_done.at(u, 2 * s + 2))
                        if s in (0, ends[0] + 1):
                            pe.wait_ge(taken[t].sem, taken[t].at(u - 1, 1))
                        for j in range(HQ):
                            w = V[g][:, 0, kb, :] if causal else V[g][:, kb, j, :]
                            mm = pe.matmul(acc[32 * j:32 * j + width + 1, t, off:], w, prob[s % 2][:, j, off:],
                                           start=(kb == 0), stop=(s == ends[t]), skip_group_check=True)
                        mm.then_inc(pv_done.sem, 1)

                units(pe, unit)


def between(pr):
    nc, a = pr.nc, pr.a
    with ExitStack() as ctx:
        def sb(name, shape, dt=F32):
            return ctx.enter_context(nc.sbuf_tensor(name, shape, dt))

        x = [sb(f"p3_x{k}", [P, BLK, E]) for k in range(2)]
        o = [sb(f"p3_o{k}", [P, EC, TILE]) for k in range(2)]
        rden = [sb(f"p3_rden{k}", [P, EC, TILE]) for k in range(2)]
        mod = [sb(f"p3_mod{k}", [P, NMOD * EC]) for k in range(2)]
        gate = sb("p3_gate", [P, E])
        norm = Norm(pr, sb, "p3", SB, CB)
        wout = sb("p3_wout", [P, EC, E])
        gwout = sb("p3_gwout", [P, EC, E])
        bout = sb("p3_bout", [P, E])
        gbias = sb("p3_gbias", [P, E])
        wq = sb("p3_wq", [P, EC, H, D2])
        wq_all = sb("p3_wq_all", [P, EC, E])
        wk = sb("p3_wk", [P, EC, P])
        wv = sb("p3_wv", [P, EC, P])
        qb = sb("p3_qb", [P, 1])
        kb = sb("p3_kb", [P, 1])
        vb = sb("p3_vb", [P, P])
        on = sb("p3_on", [P, EC, TILE])
        xg = sb("p3_xg", [P, BLK, E])
        x1 = [sb(f"p3_x1_{k}", [P, BLK, E]) for k in range(2)]
        gh = [sb(f"p3_gh{k}", [P, EC, TILE]) for k in range(2)]
        qk = [sb(f"p3_qk{c}", [P, TILE]) for c in range(2)]
        rest = [sb(f"p3_rest{c}", [P, TILE]) for c in range(2)]
        parts = [[sb(f"p3_part{k}{c}", [P, 3, TILE], BF16) for c in range(2)] for k in range(2)]
        v = [sb(f"p3_v{k}", [P, UPB, BLK, HQ, D2 + 1]) for k in range(2)]

        NLOAD = 16 * (5 + H)
        loaded_out = pr.sem("p3_loaded_out")
        loaded = pr.sem("p3_loaded")
        filled = pr.sem("p3_filled")
        picked = pr.sem("p3_picked")
        tile_in = [pr.counter(f"p3_tile_in{k}", 48) for k in range(2)]
        mod_in = [pr.counter(f"p3_mod_in{k}", 16) for k in range(2)]
        gate_in = pr.counter("p3_gate_in", 16)
        gated = pr.counter("p3_gated", 2)
        xg_ready = pr.counter("p3_xg_ready", 1)
        on_ready = pr.counter("p3_on_ready", 1)
        out_sum = pr.counter("p3_out_sum", 1)
        x1_ready = pr.counter("p3_x1_ready", 1)
        q_sum = pr.counter("p3_q_sum", 1)
        k_sum = pr.counter("p3_k_sum", 1)
        v_sum = pr.counter("p3_v_sum", 1)
        v_ready = pr.counter("p3_v_ready", 1, credit=1)
        gh_ready = pr.counter("p3_gh_ready", EC, credit=1)
        casts = pr.steps("p3_casts", ("q", "cast0_q", "k", "cast0_k", "cast1_q", "cast1_k", "cast2_q", "cast2_k"), credit=1)
        less = pr.steps("p3_less", ("less0_q", "less0_k", "less1_q", "less1_k"), credit=1)
        x1_out = [pr.counter(f"p3_x1_out{k}", 16, credit=1) for k in range(2)]
        out = [pr.counter(f"p3_out{k}", 64, credit=1) for k in range(2)]

        def pairs_of_tiles(engine, body):
            with engine.Fori(0, B - 2) as b:
                body(b, 2)
            body(B - 2, 1)
            body(B - 1, 0)

        with nc.Block() as block:
            @block.sync
            def _(sp):
                for s in x1_out + out:
                    s.open(sp)

                def load(b, k):
                    tok, sem = bass.ds(b * S + k * TILE, TILE), tile_in[k].sem
                    sp.dma_start(o[k][:], pr.o1[:, tok].rearrange("(c p) t -> p c t", p=P)).then_inc(sem, 16)
                    flat = pr.rden1.rearrange("h d t -> (h d) t")
                    sp.dma_start(rden[k][:], flat[:, tok].rearrange("(c p) t -> p c t", p=P)).then_inc(sem, 16)
                    sp.dma_start(x[k][:], a["L0_attn_x"][bass.ds(b, 1), k * TILE:(k + 1) * TILE, :]
                                 .rearrange("b (n p) e -> p (b n) e", p=P)).then_inc(sem, 16)

                def load_mod(b, k):
                    sp.dma_start(mod[k][:], pr.mod_col[bass.ds(b, 1)].rearrange("b p c -> p (b c)")).then_inc(mod_in[k].sem, 16)

                def load_gate(b):
                    sp.dma_start(gate[:], pr.mod_row[bass.ds(b, 1), GA, :].broadcast_to([P, E])).then_inc(gate_in.sem, 16)

                def store_x1(b, k):
                    sp.wait_ge(x1_ready.sem, x1_ready.at(b * TPB + k, 1))
                    sp.dma_start(pr.x1[bass.ds(b * S + k * TILE, TILE), :].rearrange("(n p) e -> p n e", p=P),
                                 x1[k][:]).then_inc(x1_out[k].sem, 16)

                load_gate(0)
                sp.dma_start(wout[:], a["L0_attn_Wout"].rearrange("(k p) n -> p k n", p=P)).then_inc(loaded_out, 16)
                sp.dma_start(bout[:], a["L0_attn_bout"].partition_broadcast(P)).then_inc(loaded_out, 16)
                load(0, 0)
                load_mod(0, 0)
                sp.dma_start(wq_all[:], a["L0_ffn_q_w"].rearrange("(k p) n -> p k n", p=P)).then_inc(loaded, 16)
                sp.dma_start(wk[:], a["L0_ffn_k_w"].rearrange("(k p) n -> p k n", p=P)).then_inc(loaded, 16)
                sp.dma_start(wv[:], a["L0_ffn_v_w"].rearrange("(k p) n -> p k n", p=P)).then_inc(loaded, 16)
                sp.dma_start(kb[:], a["L0_ffn_k_b"].unsqueeze(1)).then_inc(loaded, 16)
                sp.dma_start(vb[:], a["L0_ffn_v_b"].partition_broadcast(P)).then_inc(loaded, 16)
                for h in range(H):
                    sp.dma_start(qb[h * D2:(h + 1) * D2, :],
                                 a["L0_ffn_q_b"][h * D1:h * D1 + D2].unsqueeze(1)).then_inc(loaded, 16)
                load(0, 1)
                load_mod(0, 1)
                sp.wait_ge(gated.sem, gated.at(0, 2))
                load_gate(1)
                store_x1(0, 0)
                sp.wait_ge(on_ready.sem, on_ready.at(0, 1))
                sp.wait_ge(xg_ready.sem, xg_ready.at(0, 1))
                load(1, 0)

                def pair(b, left):
                    for k in range(TPB):
                        n = b * TPB + k
                        tok = bass.ds(b * S + k * TILE, TILE)
                        sem = out[k].sem
                        if left > k:
                            sp.wait_ge(on_ready.sem, on_ready.at(n + 1, 1))
                            sp.wait_ge(xg_ready.sem, xg_ready.at(n + 1, 1))
                            load(b + 1 + k, 1 - k)
                        sp.wait_ge(gh_ready.sem, gh_ready.at(n, EC))
                        if left:
                            load_mod(b + 1, k)
                        sp.dma_start(pr.gh[:, tok].rearrange("(c p) t -> p c t", p=P), gh[k][:]).then_inc(sem, 16)
                        if k == 1 and left == 2:
                            sp.wait_ge(gated.sem, gated.at(b + 1, 2))
                            load_gate(b + 2)
                        if k == 0 or left:
                            store_x1(b + k, 1 - k)
                        sp.wait_ge(v_ready.sem, v_ready.at(n, 1))
                        sp.wait_ge(casts.sem, casts.after(n, "cast2_k"))
                        sp.dma_start(pr.v2[bass.ds(b, 1), :, :, k * BLK:(k + 1) * BLK].rearrange("b g p n j d -> p (b g) (n j d)"),
                                     v[k][:].rearrange("p g n j d -> p g (n j d)")).then_inc(sem, 16)
                        sp.dma_start(pr.q2[:, :, tok].rearrange("s p t -> p s t"), parts[k][0][:]).then_inc(sem, 16)
                        sp.dma_start(pr.k2[:, :, tok].rearrange("s p t -> p s t"), parts[k][1][:]).then_inc(sem, 16)

                pairs_of_tiles(sp, pair)
                for k in range(2):
                    sp.wait_ge(x1_out[k].sem, x1_out[k].at(B - 1, 16))
                    sp.wait_ge(out[k].sem, out[k].at(B - 1, 64))

            @block.gpsimd
            def _(pool):
                pool.memset(norm.power[:], -0.5).then_inc(filled, 1)
                for k in range(2):
                    pool.memset(v[k][:], 1.0).then_inc(filled, 1)
                pool.wait_ge(filled, 3)
                pool.wait_ge(loaded_out, 32)

                def scale(b):
                    pool.wait_ge(gate_in.sem, gate_in.at(b, 16))
                    pool.tensor_tensor(gwout[:], wout[:], gate[:].unsqueeze(1).broadcast_to([P, EC, E]),
                                       ALU.mult).then_inc(gated.sem, 1)
                    pool.tensor_tensor(gbias[:], bout[:], gate[:], ALU.mult).then_inc(gated.sem, 1)

                def with_bias(b, k):
                    pool.wait_ge(tile_in[k].sem, tile_in[k].at(b, 48))
                    pool.wait_ge(gated.sem, gated.at(b, 2))
                    pool.tensor_tensor(xg[:], x[k][:], gbias[:].unsqueeze(1).broadcast_to([P, BLK, E]),
                                       ALU.add).then_inc(xg_ready.sem, 1)

                scale(0)
                with_bias(0, 0)
                norm.pool(pool, 0)
                pool.wait_ge(x1_ready.sem, x1_ready.at(0, 1))
                with_bias(0, 1)

                def pair(b, left):
                    for k in range(TPB):
                        n = b * TPB + k
                        if k == 0 or left:
                            norm.pool(pool, n + 1)
                        if left:
                            if k == 0:
                                pool.wait_ge(x1_ready.sem, x1_ready.at(n + 1, 1))
                                pool.wait_ge(xg_ready.sem, xg_ready.at(n + 1, 1))
                                scale(b + 1)
                            pool.wait_ge(x1_ready.sem, x1_ready.at(n + 1, 1))
                            with_bias(b + 1, k)

                pairs_of_tiles(pool, pair)

            @block.scalar
            def _(act):
                norm.open(act, "act")
                casts.open(act)
                gh_ready.open(act)
                act.wait_ge(loaded, NLOAD)

                def modulate(b, k):
                    n = b * TPB + k
                    act.wait_ge(mod_in[k].sem, mod_in[k].at(b, 16))
                    act.wait_ge(gh_ready.sem, gh_ready.at(n - 1, EC))
                    norm.act(act, n, mod[k])

                def gate_h(b, k):
                    n = b * TPB + k
                    act.wait_ge(out[k].sem, out[k].at(b - 1, 64))
                    act.wait_ge(norm.h_ready.sem, norm.h_ready.at(n, EC))
                    for c in range(EC):
                        act.activation(gh[k][:, c, :], norm.hT[:, c, :], ACT.Identity,
                                       scale=mod[k][:, GB * EC + c:GB * EC + c + 1]).then_inc(gh_ready.sem, 1)

                modulate(0, 0)
                gate_h(0, 0)

                def pair(b, left):
                    for k in range(TPB):
                        n = b * TPB + k
                        more = k == 0 or left

                        def cast(part, c):
                            act.wait_ge(less.sem, less.after(n, f"less{part - 1}_{'qk'[c]}"))
                            act.copy(parts[k][c][:, part, :], rest[c][:]).then_inc(casts.sem, 1)

                        act.wait_ge(out[k].sem, out[k].at(b - 1, 64))
                        act.wait_ge(less.sem, less.after(n - 1, "less0_k"))
                        for c, (total, bias) in enumerate(((q_sum, qb), (k_sum, kb))):
                            act.wait_ge(total.sem, total.at(n, 1))
                            for to in (qk[c][:], parts[k][c][:, 0, :]):
                                act.activation(to, pr.bank[:, 4 + c, :], ACT.Identity, bias=bias[:, 0:1]).then_inc(casts.sem, 1)
                        cast(1, 0)
                        cast(1, 1)
                        if more:
                            modulate(b + k, 1 - k)
                        cast(2, 0)
                        cast(2, 1)
                        if more:
                            gate_h(b + k, 1 - k)

                pairs_of_tiles(act, pair)

            @block.vector
            def _(dve):
                v_ready.open(dve)
                less.open(dve)

                def divide(b, k):
                    n = b * TPB + k
                    dve.wait_ge(tile_in[k].sem, tile_in[k].at(b, 48))
                    dve.tensor_tensor(on[:], o[k][:], rden[k][:], ALU.mult).then_inc(on_ready.sem, 1)

                def residual(b, k):
                    n = b * TPB + k
                    dve.wait_ge(xg_ready.sem, xg_ready.at(n, 1))
                    dve.wait_ge(x1_out[k].sem, x1_out[k].at(b - 1, 16))
                    dve.wait_ge(out_sum.sem, out_sum.at(n, 1))
                    dve.tensor_tensor(x1[k][:], pr.bank[:, 2:4, :].rearrange("p a (n e) -> p (a n) e", e=E), xg[:],
                                      ALU.add).then_inc(x1_ready.sem, 1)
                    dve.wait_ge(x1_ready.sem, x1_ready.at(n, 1))
                    norm.statistics(dve, n, x1[k])

                divide(0, 0)
                residual(0, 0)
                divide(0, 1)
                norm.normalise(dve, 0, x1[0])
                dve.wait_ge(loaded, NLOAD)
                dve.wait_ge(filled, 3)
                dve.tensor_copy(wq[:], wq_all[:].rearrange("p k (h d) -> p k h d", d=D1)[:, :, :, 0:D2]).then_inc(picked, 1)

                def pair(b, left):
                    for k in range(TPB):
                        n = b * TPB + k
                        if k == 0 or left:
                            residual(b + k, 1 - k)
                            if left:
                                divide(b + 1, k)
                            norm.normalise(dve, n + 1, x1[1 - k])
                        for part in range(2):
                            for c in range(2):
                                if part == 0:
                                    dve.wait_ge(casts.sem, casts.after(n - 1, f"cast2_{'qk'[c]}"))
                                dve.wait_ge(casts.sem, casts.after(n, f"cast{part}_{'qk'[c]}"))
                                dve.tensor_tensor(rest[c][:], (rest if part else qk)[c][:], parts[k][c][:, part, :],
                                                  ALU.subtract).then_inc(less.sem, 1)
                        dve.wait_ge(out[k].sem, out[k].at(b - 1, 64))
                        dve.wait_ge(v_sum.sem, v_sum.at(n, 1))
                        for i in range(BLK):
                            op = dve.tensor_tensor(v[k][:, :, i, :, 0:D2],
                                                   pr.bank[:, 6, i * P:(i + 1) * P].rearrange("p (g j d) -> p g j d", g=UPB, j=HQ),
                                                   vb[:].rearrange("p (g j d) -> p g j d", g=UPB, j=HQ), ALU.add)
                        op.then_inc(v_ready.sem, 1)

                pairs_of_tiles(dve, pair)

            @block.tensor
            def _(pe):
                norm.open(pe, "pe")

                def project(b, k):
                    n = b * TPB + k
                    if k == 0:
                        pe.wait_ge(gated.sem, gated.at(b, 1))
                    pe.wait_ge(on_ready.sem, on_ready.at(n, 1))
                    for i in range(BLK):
                        to = pr.bank[:, 2 + i // 2, (i % 2) * E:(i % 2 + 1) * E]
                        for c in range(EC):
                            mm = pe.matmul(to, on[:, c, i * P:(i + 1) * P], gwout[:, c, :],
                                           start=(c == 0), stop=(c == EC - 1), skip_group_check=True)
                    mm.then_inc(out_sum.sem, 1)

                project(0, 0)
                pe.wait_ge(loaded, NLOAD)
                pe.wait_ge(picked, 1)

                def pair(b, left):
                    for k in range(TPB):
                        n = b * TPB + k
                        pe.wait_ge(norm.h_ready.sem, norm.h_ready.at(n - 1, EC))
                        norm.pe(pe, n)
                        if k == 0 or left:
                            project(b + k, 1 - k)
                        pe.wait_ge(norm.h_ready.sem, norm.h_ready.at(n, EC))
                        pe.wait_ge(casts.sem, casts.after(n - 1, "cast0_k"))
                        for i, (w, total) in enumerate(((wq[:].rearrange("p k h d -> p k (h d)"), q_sum), (wk[:], k_sum))):
                            for c in range(EC):
                                mm = pe.matmul(pr.bank[:, 4 + i, :], w[:, c, :], norm.hT[:, c, :],
                                               start=(c == 0), stop=(c == EC - 1))
                            mm.then_inc(total.sem, 1)
                        pe.wait_ge(v_ready.sem, v_ready.at(n - 1, 1))
                        for i in range(BLK):
                            for c in range(EC):
                                mm = pe.matmul(pr.bank[:, 6, i * P:(i + 1) * P], norm.hT[:, c, i * P:(i + 1) * P], wv[:, c, :],
                                               start=(c == 0), stop=(c == EC - 1), skip_group_check=True)
                        mm.then_inc(v_sum.sem, 1)

                pairs_of_tiles(pe, pair)


def route(pr):
    nc, a = pr.nc, pr.a
    NB = TILES * BLK
    with ExitStack() as ctx:
        def sb(name, shape, dt=F32):
            return ctx.enter_context(nc.sbuf_tensor(name, shape, dt))

        o = [sb(f"p5_o{k}", [P, TILE]) for k in range(2)]
        rden = [sb(f"p5_rden{k}", [P, TILE]) for k in range(2)]
        on = [sb(f"p5_on{k}", [P, TILE]) for k in range(2)]
        wo = sb("p5_wo", [P, E])
        ob = sb("p5_ob", [P, EC])
        wr = sb("p5_wr", [P, EC, NX])
        rb = sb("p5_rb", [P, NX])
        mla = [sb(f"p5_mla{k}", [P, EC, TILE]) for k in range(2)]
        part = [sb(f"p5_part{k}", [P, 2, EC, TILE], F32R) for k in range(2)]
        logit = sb("p5_logit", [P, NB, NX])
        prob = sb("p5_prob", [P, NB, NX])
        rank = sb("p5_rank", [P, NX])
        tmp = sb("p5_tmp", [P, NB, NX])
        first = sb("p5_first", [P, NB, NX])
        second = sb("p5_second", [P, NB, NX])
        top1 = sb("p5_top1", [P, NB])
        top2 = sb("p5_top2", [P, NB])
        best = sb("p5_best", [P, NB])
        total = sb("p5_total", [P, NB])
        comb = sb("p5_comb", [P, TILES, NX, BLK])
        combT = sb("p5_combT", [BLK * NX, TILES, P])

        loaded = pr.sem("p5_loaded")
        ranked = pr.sem("p5_ranked")
        tile_in = [pr.counter(f"p5_tile_in{k}", 32) for k in range(2)]
        on_ready = pr.counter("p5_on_ready", 1)
        mla_sum = pr.counter("p5_mla_sum", EC)
        mla_ready = pr.counter("p5_mla_ready", EC, credit=1)
        cut = pr.counter("p5_cut", 2, credit=2)
        logit_sum = pr.counter("p5_logit_sum", 1, credit=1)
        logit_ready = pr.counter("p5_logit_ready", 1, credit=1)
        stored = [pr.counter(f"p5_stored{k}", 32, credit=1) for k in range(2)]
        step = pr.sem("p5_step")
        exps = pr.sem("p5_exps")
        weighted = pr.sem("p5_weighted")
        turned = pr.sem("p5_turned")
        comb_ready = pr.sem("p5_comb_ready")
        comb_out = pr.sem("p5_comb_out")

        with nc.Block() as block:
            @block.sync
            def _(sp):
                for s in stored:
                    s.open(sp)
                sp.dma_start(wo[:], a["L0_ffn_o_w"][0:P, :]).then_inc(loaded, 16)
                sp.dma_start(wr[:], a["L0_ffn_router_w"].rearrange("(k p) n -> p k n", p=P)).then_inc(loaded, 16)
                sp.dma_start(rb[:], a["L0_ffn_router_b"].partition_broadcast(P)).then_inc(loaded, 16)
                for c in range(EC):
                    sp.dma_start(ob[:, c:c + 1], a["L0_ffn_o_b"][c * P:(c + 1) * P].unsqueeze(1)).then_inc(loaded, 16)

                def load(b, k):
                    tok, sem = bass.ds(b * S + k * TILE, TILE), tile_in[k].sem
                    sp.dma_start(o[k][:], pr.o2[:, tok]).then_inc(sem, 16)
                    sp.dma_start(rden[k][:], pr.rden2.rearrange("h d t -> (h d) t")[:, tok]).then_inc(sem, 16)

                load(0, 0)
                load(0, 1)

                def pair(b, last):
                    for k in range(TPB):
                        n = b * TPB + k
                        sp.wait_ge(on_ready.sem, on_ready.at(n, 1))
                        if not last:
                            load(b + 1, k)
                        sp.wait_ge(cut.sem, cut.at(n, 2))
                        for h in range(2):
                            sp.dma_start(pr.mla[h, :, bass.ds(b * S + k * TILE, TILE)].rearrange("(c p) t -> p c t", p=P),
                                         part[k][:, h].bitcast(F32)).then_inc(stored[k].sem, 16)

                in_pairs(sp, TILES, pair)
                for k in range(2):
                    sp.wait_ge(stored[k].sem, stored[k].at(B - 1, 32))
                sp.wait_ge(comb_ready, 1)
                sp.dma_start(pr.comb.rearrange("n e (b t) -> (e b) n t", b=BLK), combT[:]).then_inc(comb_out, 16)
                sp.wait_ge(comb_out, 16)

            @block.gpsimd
            def _(pool):
                for e in range(NX):
                    op = pool.memset(rank[:, e:e + 1], float(NX - e))
                op.then_inc(ranked, 1)

            @block.scalar
            def _(act):
                mla_ready.open(act)
                act.wait_ge(loaded, 80)

                def pair(b, last):
                    for k in range(TPB):
                        n = b * TPB + k
                        act.wait_ge(cut.sem, cut.at(n - 2, 2))
                        act.wait_ge(logit_sum.sem, logit_sum.at(n - 1, 1))
                        for c in range(EC):
                            act.wait_ge(mla_sum.sem, mla_sum.at(n, c + 1))
                            act.activation(mla[k][:, c, :], pr.bank[:, c, :], ACT.Identity,
                                           bias=ob[:, c:c + 1]).then_inc(mla_ready.sem, 1)

                in_pairs(act, TILES, pair)
                act.wait_ge(step, 2)
                act.activation(prob[:], logit[:], ACT.Exp).then_inc(exps, 1)

            @block.vector
            def _(dve):
                cut.open(dve)
                logit_ready.open(dve)
                dve.wait_ge(loaded, 80)

                def normalise(b, k):
                    dve.wait_ge(tile_in[k].sem, tile_in[k].at(b, 32))
                    dve.wait_ge(mla_ready.sem, mla_ready.at(b * TPB + k - 1, EC)) if not isinstance(b, int) or b or k else None
                    dve.tensor_tensor(on[k][:], o[k][:], rden[k][:], ALU.mult).then_inc(on_ready.sem, 1)

                normalise(0, 0)

                def pair(b, last):
                    for k in range(TPB):
                        n = b * TPB + k
                        if k == 0 or not last:
                            normalise(b + k, 1 - k)
                        dve.wait_ge(mla_ready.sem, mla_ready.at(n, EC))
                        dve.wait_ge(stored[k].sem, stored[k].at(b - 1, 32))
                        dve.tensor_copy(part[k][:, 0], mla[k][:]).then_inc(cut.sem, 1)
                        dve.wait_ge(cut.sem, cut.at(n, 1))
                        dve.tensor_tensor(part[k][:, 1], mla[k][:], part[k][:, 0].bitcast(F32), ALU.subtract).then_inc(cut.sem, 1)
                        dve.wait_ge(logit_sum.sem, logit_sum.at(n, 1))
                        dve.tensor_tensor(logit[:, bass.ds(n * BLK, BLK), :],
                                          pr.bank[:, 2, 0:BLK * NX].rearrange("p (b e) -> p b e", e=NX),
                                          rb[:].unsqueeze(1).broadcast_to([P, BLK, NX]), ALU.add).then_inc(logit_ready.sem, 1)

                in_pairs(dve, TILES, pair)
                dve.wait_ge(logit_ready.sem, logit_ready.at(TILES - 1, 1))
                dve.wait_ge(ranked, 1)

                def wide(t):
                    return t[:].unsqueeze(2).broadcast_to([P, NB, NX])

                dve.tensor_reduce(best[:], logit[:], AX.X, ALU.max).then_inc(step, 1)
                dve.wait_ge(step, 1)
                dve.tensor_tensor(logit[:], logit[:], wide(best), ALU.subtract).then_inc(step, 1)
                dve.wait_ge(exps, 1)
                dve.tensor_reduce(total[:], prob[:], AX.X, ALU.add).then_inc(step, 1)
                dve.wait_ge(step, 3)
                dve.reciprocal(total[:], total[:]).then_inc(step, 1)
                dve.wait_ge(step, 4)
                dve.tensor_tensor(prob[:], prob[:], wide(total), ALU.mult).then_inc(step, 1)
                at = 5
                for value, choice in ((top1, first), (top2, second)):
                    dve.wait_ge(step, at)
                    dve.tensor_reduce(value[:], prob[:], AX.X, ALU.max).then_inc(step, 1)
                    dve.wait_ge(step, at + 1)
                    dve.tensor_tensor(tmp[:], prob[:], wide(value), ALU.is_equal).then_inc(step, 1)
                    dve.wait_ge(step, at + 2)
                    dve.tensor_tensor(tmp[:], tmp[:], rank[:].unsqueeze(1).broadcast_to([P, NB, NX]), ALU.mult).then_inc(step, 1)
                    dve.wait_ge(step, at + 3)
                    dve.tensor_reduce(best[:], tmp[:], AX.X, ALU.max).then_inc(step, 1)
                    dve.wait_ge(step, at + 4)
                    dve.tensor_tensor(choice[:], tmp[:], wide(best), ALU.is_equal).then_inc(step, 1)
                    dve.wait_ge(step, at + 5)
                    dve.scalar_tensor_tensor(out=prob[:], in0=choice[:], scalar=-2.0, in1=prob[:],
                                             op0=ALU.mult, op1=ALU.add).then_inc(step, 1)
                    at += 6
                dve.wait_ge(step, at)
                dve.scalar_tensor_tensor(out=total[:], in0=top1[:], scalar=1e-8, in1=top2[:],
                                         op0=ALU.add, op1=ALU.add).then_inc(step, 1)
                dve.wait_ge(step, at + 1)
                dve.reciprocal(total[:], total[:]).then_inc(step, 1)
                dve.wait_ge(step, at + 2)
                dve.tensor_tensor(top1[:], top1[:], total[:], ALU.mult).then_inc(step, 1)
                dve.tensor_tensor(top2[:], top2[:], total[:], ALU.mult).then_inc(step, 1)
                dve.wait_ge(step, at + 4)
                dve.tensor_tensor(first[:], first[:], wide(top1), ALU.mult).then_inc(step, 1)
                dve.tensor_tensor(second[:], second[:], wide(top2), ALU.mult).then_inc(step, 1)
                dve.wait_ge(step, at + 6)
                dve.tensor_tensor(comb[:].rearrange("p n e b -> p n b e"),
                                  first[:].rearrange("p (n b) e -> p n b e", b=BLK),
                                  second[:].rearrange("p (n b) e -> p n b e", b=BLK), ALU.add).then_inc(weighted, 1)
                dve.wait_ge(turned, 1)
                dve.tensor_copy(combT[:], pr.bank[0:BLK * NX, 3:5, :].rearrange("q a (n t) -> q (a n) t", t=P)).then_inc(comb_ready, 1)

            @block.tensor
            def _(pe):
                logit_sum.open(pe)
                pe.wait_ge(loaded, 80)

                def pair(b, last):
                    for k in range(TPB):
                        n = b * TPB + k
                        pe.wait_ge(on_ready.sem, on_ready.at(n, 1))
                        pe.wait_ge(mla_ready.sem, mla_ready.at(n - 1, EC))
                        for c in range(EC):
                            pe.matmul(pr.bank[:, c, :], wo[:, c * P:(c + 1) * P], on[k][:], start=True,
                                      stop=True).then_inc(mla_sum.sem, 1)
                        pe.wait_ge(mla_ready.sem, mla_ready.at(n, EC))
                        pe.wait_ge(logit_ready.sem, logit_ready.at(n - 1, 1))
                        for i in range(BLK):
                            for c in range(EC):
                                mm = pe.matmul(pr.bank[:, 2, i * NX:(i + 1) * NX], mla[k][:, c, i * P:(i + 1) * P], wr[:, c, :],
                                               start=(c == 0), stop=(c == EC - 1), skip_group_check=True)
                        mm.then_inc(logit_sum.sem, 1)

                in_pairs(pe, TILES, pair)
                pe.wait_ge(weighted, 1)
                for n in range(TILES):
                    mm = pe.transpose(pr.bank[0:BLK * NX, 3 + n // 4, (n % 4) * P:(n % 4 + 1) * P],
                                      comb[:, n].rearrange("p e b -> p (e b)"), pr.ident[:])
                mm.then_inc(turned, 1)


def experts(pr):
    nc, a = pr.nc, pr.a
    COLS = 2 * FC * FC
    with ExitStack() as ctx:
        def sb(name, shape, dt=F32):
            return ctx.enter_context(nc.sbuf_tensor(name, shape, dt))

        x = [sb(f"p6_x{t}", [P, 2, EC, S], F32R) for t in range(2)]
        w = [[sb(f"p6_w{j}{k}", [P, EC * FF]) for j in (1, 2)] for k in range(2)]
        wp = [[sb(f"p6_wp{j}{k}", [P, 2, EC * FF], F32R) for j in (1, 2)] for k in range(2)]
        bias = sb("p6_bias", [P, NX * (FC + EC)])
        b1 = [sb(f"p6_b1{k}", [P, FC]) for k in range(2)]
        b2 = [sb(f"p6_b2{k}", [P, EC]) for k in range(2)]
        comb = [sb(f"p6_comb{k}", [P, TPB, TILE]) for k in range(2)]
        g = [sb(f"p6_g{f}", [P, S]) for f in range(2)]
        hid = [sb(f"p6_hid{f}", [P, 2, S], F32R) for f in range(FC)]
        z = [sb(f"p6_z{c}", [P, S]) for c in range(EC)]
        acc = sb("p6_acc", [P, EC, S])
        gh = sb("p6_gh", [P, EC, S])
        mod = sb("p6_mod", [P, NMOD * EC])
        x1 = sb("p6_resid", [P, S // P, E])
        y = sb("p6_y", [P, S // P, E])

        bank1 = [pr.bank[:, 2 * q:2 * q + 2, :] for q in range(2)]
        bank2 = [pr.bank[:, 4 + 2 * c:6 + 2 * c, :] for c in range(EC)]

        x_in = [pr.counter(f"p6_x_in{t}", 32) for t in range(2)]
        w_in = [pr.counter(f"p6_w_in{k}", 64) for k in range(2)]
        comb_in = [pr.counter(f"p6_comb_in{k}", 16) for k in range(2)]
        end_in = pr.counter("p6_end_in", 48)
        w_hi = pr.counter("p6_w_hi", 2, credit=1)
        w_lo = pr.counter("p6_w_lo", 2, credit=1)
        sum1 = pr.counter("p6_sum1", FC)
        gelu = pr.counter("p6_gelu", FC, credit=1)
        hi = pr.counter("p6_hi", FC)
        lo = pr.counter("p6_lo", FC, credit=1)
        sum2 = pr.counter("p6_sum2", FC, credit=2)
        weigh = pr.counter("p6_weigh", 2 * EC, credit=2)
        final = pr.counter("p6_final", EC + 1)
        turned = pr.counter("p6_turned", 2)
        done = pr.counter("p6_done", 2, credit=1)
        stored = pr.counter("p6_stored", 16, credit=1)

        def batches(engine, before, visit, end):
            with engine.Fori(0, B // 2) as i:
                for t in range(2):
                    b = i * 2 + t
                    before(b, i, t)
                    with engine.Fori(0, NX // 2) as j:
                        for k in range(2):
                            visit(i, b, j, k, b * NX + j * 2 + k, b * (NX // 2) + j, t)
                    end(b)

        with nc.Block() as block:
            @block.sync
            def _(sp):
                def before(b, i, t):
                    tok = bass.ds(b * S, S)
                    for h in range(2):
                        sp.dma_start(x[t][:, h].bitcast(F32), pr.mla[h, :, tok].rearrange("(c p) t -> p c t", p=P)).then_inc(x_in[t].sem, 16)

                def visit(i, b, j, k, v, pair, t):
                    e = j * 2 + k
                    sp.wait_ge(weigh.sem, weigh.at(v - 1, 0))
                    sp.dma_start(w[k][0][:], a["L0_ffn_w1"][bass.ds(e, 1)].rearrange("x (k p) n -> p (x k) n", p=P)).then_inc(w_in[k].sem, 16)
                    sp.dma_start(w[k][1][:], a["L0_ffn_w2"][bass.ds(e, 1)].rearrange("x (k p) n -> p (x k) n", p=P)).then_inc(w_in[k].sem, 16)
                    sp.dma_start(b1[k][:], pr.bias_col[:, bass.ds(e * FC, FC)]).then_inc(w_in[k].sem, 16)
                    sp.dma_start(b2[k][:], pr.bias_col[:, bass.ds(NX * FC + e * EC, EC)]).then_inc(w_in[k].sem, 16)
                    sp.dma_start(comb[k][:], pr.comb[bass.ds(b * TPB, TPB), bass.ds(e, 1), :]
                                 .rearrange("n e t -> e n t").broadcast_to([P, TPB, TILE])).then_inc(comb_in[k].sem, 16)

                batches(sp, before, visit, lambda b: None)

            @block.gpsimd
            def _(pool):
                w_lo.open(pool)

                def visit(i, b, j, k, v, pair, t):
                    for n in range(2):
                        pool.wait_ge(w_hi.sem, w_hi.at(v, n + 1))
                        pool.tensor_tensor(wp[k][n][:, 1], w[k][n][:], wp[k][n][:, 0].bitcast(F32), ALU.subtract).then_inc(w_lo.sem, 1)

                batches(pool, lambda b, i, t: None, visit, lambda b: None)

            @block.scalar
            def _(act):
                stored.open(act)
                w_hi.open(act)
                gelu.open(act)

                def high(v, j, k, pair):
                    act.wait_ge(w_in[k].sem, w_in[k].at(pair, 64))
                    act.wait_ge(sum2.sem, sum2.at(v - 2, FC))
                    for n in range(2):
                        act.copy(wp[k][n][:, 0], w[k][n][:]).then_inc(w_hi.sem, 1)

                def visit(i, b, j, k, v, pair, t):
                    high(v, j, k, pair)
                    for f in range(FC):
                        act.wait_ge(sum1.sem, sum1.at(v, f + 1))
                        act.wait_ge(lo.sem, lo.at(v, f - 1))
                        act.activation(g[f % 2][:], bank1[f % 2].rearrange("p a t -> p (a t)"), ACT.Gelu,
                                       bias=b1[k][:, f:f + 1]).then_inc(gelu.sem, 1)
                        act.wait_ge(sum2.sem, sum2.at(v - 1, f + 1))
                        act.wait_ge(gelu.sem, gelu.at(v, f + 1))
                        act.copy(hid[f][:, 0], g[f % 2][:]).then_inc(hi.sem, 1)

                def before(b, i, t):
                    act.wait_ge(done.sem, done.at(b - 1, 2))
                    tok = bass.ds(b * S, S)
                    act.dma_start(gh[:], pr.gh[:, tok].rearrange("(c p) t -> p c t", p=P)).then_inc(end_in.sem, 16)
                    act.dma_start(x1[:], pr.x1[tok, :].rearrange("(n p) e -> p n e", p=P)).then_inc(end_in.sem, 16)
                    act.dma_start(mod[:], pr.mod_col[bass.ds(b, 1)].rearrange("b p c -> p (b c)")).then_inc(end_in.sem, 16)

                def end(b):
                    act.wait_ge(done.sem, done.at(b, 2))
                    act.dma_start(a["out"][bass.ds(b, 1)].rearrange("b (n p) e -> p (b n) e", p=P), y[:]).then_inc(stored.sem, 16)

                batches(act, before, visit, end)
                act.wait_ge(stored.sem, stored.at(B - 1, 16))

            @block.vector
            def _(dve):
                lo.open(dve)
                weigh.open(dve)
                done.open(dve)

                def visit(i, b, j, k, v, pair, t):
                    for f in range(FC):
                        dve.wait_ge(hi.sem, hi.at(v, f + 1))
                        dve.tensor_tensor(hid[f][:, 1], g[f % 2][:], hid[f][:, 0].bitcast(F32), ALU.subtract).then_inc(lo.sem, 1)
                    dve.wait_ge(sum2.sem, sum2.at(v, FC))
                    dve.wait_ge(comb_in[k].sem, comb_in[k].at(pair, 16))
                    dve.wait_ge(weigh.sem, weigh.at(v - 1, 2 * EC))
                    dve.wait_ge(final.sem, final.at(b, 1))
                    weight = comb[k][:].rearrange("p n t -> p (n t)")
                    for c in range(EC):
                        dve.scalar_tensor_tensor(out=z[c][:], in0=bank2[c].rearrange("p a t -> p (a t)"), scalar=b2[k][:, c:c + 1],
                                                 in1=weight, op0=ALU.add, op1=ALU.mult).then_inc(weigh.sem, 1)
                    for c in range(EC):
                        dve.wait_ge(weigh.sem, weigh.at(v, c + 1))
                        dve.tensor_tensor(acc[:, c, :], acc[:, c, :], z[c][:], ALU.add).then_inc(weigh.sem, 1)

                def before(b, i, t):
                    dve.wait_ge(done.sem, done.at(b - 1, 2))
                    dve.memset(acc[:], 0.0).then_inc(final.sem, 1)

                def end(b):
                    dve.wait_ge(end_in.sem, end_in.at(b, 48))
                    dve.wait_ge(weigh.sem, weigh.at(b * NX + NX - 1, 2 * EC))
                    for c in range(EC):
                        dve.scalar_tensor_tensor(out=acc[:, c, :], in0=acc[:, c, :],
                                                 scalar=mod[:, GB3 * EC + c:GB3 * EC + c + 1],
                                                 in1=gh[:, c, :], op0=ALU.mult, op1=ALU.add).then_inc(final.sem, 1)
                    dve.wait_ge(stored.sem, stored.at(b - 1, 16))
                    for q in range(2):
                        dve.wait_ge(turned.sem, turned.at(b, q + 1))
                        n = S // P // 2
                        dve.tensor_tensor(y[:, q * n:(q + 1) * n, :], bank1[q].rearrange("p a (n e) -> p (a n) e", e=E),
                                          x1[:, q * n:(q + 1) * n, :], ALU.add).then_inc(done.sem, 1)

                batches(dve, before, visit, end)

            @block.tensor
            def _(pe):
                sum2.open(pe)

                def visit(i, b, j, k, v, pair, t):
                    w1 = wp[k][0][:].rearrange("p h (c f m) -> p h c f m", c=EC, f=FC)
                    w2 = wp[k][1][:].rearrange("p h (f c m) -> p h f c m", f=FC, c=EC)
                    products = ((0, 0), (0, 1), (1, 0))

                    def layer1(f):
                        pe.wait_ge(gelu.sem, gelu.at(v, f - 1))
                        for h in range(TPB):
                            for n, (pw, px) in enumerate(products):
                                if f == 0 and h == 0 and pw == 1:
                                    pe.wait_ge(w_lo.sem, w_lo.at(v, 1))
                                for c in range(EC):
                                    mm = pe.matmul(bank1[f % 2][:, h, :], w1[:, pw, c, f, :],
                                                   x[t][:, px, c, h * TILE:(h + 1) * TILE],
                                                   start=(n == 0 and c == 0), stop=(n == 2 and c == EC - 1))
                        mm.then_inc(sum1.sem, 1)

                    def layer2(f):
                        pe.wait_ge(hi.sem, hi.at(v, f + 1))
                        pe.wait_ge(lo.sem, lo.at(v, f + 1))
                        if f == 0:
                            pe.wait_ge(w_hi.sem, w_hi.at(v, 2))
                            pe.wait_ge(w_lo.sem, w_lo.at(v, 2))
                            pe.wait_ge(weigh.sem, weigh.at(v - 1, EC))
                        for c in range(EC):
                            for h in range(TPB):
                                for n, (pw, px) in enumerate(products):
                                    mm = pe.matmul(bank2[c][:, h, :], w2[:, pw, f, c, :],
                                                   hid[f][:, px, h * TILE:(h + 1) * TILE],
                                                   start=(f == 0 and n == 0), stop=(f == FC - 1 and n == 2),
                                                   skip_group_check=True)
                        mm.then_inc(sum2.sem, 1)

                    pe.wait_ge(x_in[t].sem, x_in[t].at(i, 32))
                    pe.wait_ge(done.sem, done.at(b - 1, 2))
                    pe.wait_ge(w_hi.sem, w_hi.at(v, 1))
                    layer1(0)
                    layer1(1)
                    layer1(2)
                    layer2(0)
                    layer1(3)
                    layer2(1)
                    layer2(2)
                    layer2(3)

                def end(b):
                    pe.wait_ge(final.sem, final.at(b, EC + 1))
                    for q in range(2):
                        pe.wait_ge(gelu.sem, gelu.at(b * NX + NX - 1, FC))
                        for n in range(S // P // 2):
                            for c in range(EC):
                                s = (q * S // P // 2 + n) * P
                                mm = pe.transpose(bank1[q].rearrange("p a (n e) -> p (a n) e", e=E)[:, n, c * P:(c + 1) * P],
                                                  acc[:, c, s:s + P], pr.ident[:])
                        mm.then_inc(turned.sem, 1)

                batches(pe, lambda b, i, t: None, visit, end)


def build(nc, a):
    with ExitStack() as ctx:
        pr = Program(nc, ctx, a)
        modulation(pr)
        from_x(pr)
        attention(pr, "a1", pr.q1, pr.k1, pr.v1, pr.o1, pr.den[0], pr.rden1, D1, SIX, True, D1 ** -0.5)
        between(pr)
        attention(pr, "a2", pr.q2, pr.k2, pr.v2, pr.o2, pr.den[1], pr.rden2, D2, NINE, False, D2 ** -0.5)
        route(pr)
        experts(pr)


_INS = ['L0_attn_x', 'L0_attn_Wqa', 'L0_attn_Wqb', 'L0_attn_Wkva', 'L0_attn_Wkvb', 'L0_attn_Wout', 'L0_attn_bout',
        'L0_ffn_q_w', 'L0_ffn_q_b', 'L0_ffn_k_w', 'L0_ffn_k_b', 'L0_ffn_v_w', 'L0_ffn_v_b', 'L0_ffn_o_w',
        'L0_ffn_o_b', 'L0_ffn_router_w', 'L0_ffn_router_b', 'L0_ffn_w1', 'L0_ffn_b1', 'L0_ffn_w2', 'L0_ffn_b2',
        'L0_c', 'L0_wmod']


def rope_tables():
    inv_freq = 1.0 / np.float32(10000.0) ** (np.arange(0, D1, 2, dtype=np.float32) / np.float32(D1))
    angle = np.outer(np.arange(S, dtype=np.float32), inv_freq.astype(np.float32)).astype(np.float32)
    rows = (np.arange(P) % D1) // 2
    return (np.ascontiguousarray(np.cos(angle).T[rows]).astype(np.float32),
            np.ascontiguousarray(np.sin(angle).T[rows]).astype(np.float32))


def kernel(**inputs):
    import concourse.bacc as bacc
    from concourse.bass_utils import run_bass_kernel_spmd

    nc = bacc.Bacc("TRN2", target_bir_lowering=False, num_devices=1)
    arrays = {f"in_{name}": np.ascontiguousarray(inputs[name]) for name in _INS}
    arrays["in_rope_cos"], arrays["in_rope_sin"] = rope_tables()
    a = {name[3:]: nc.dram_tensor(name, v.shape, mybir.dt.from_np(v.dtype), kind="ExternalInput").ap()
         for name, v in arrays.items()}
    a["out"] = nc.dram_tensor("out_0", (B, S, E), F32, kind="ExternalOutput").ap()
    build(nc, a)
    r = run_bass_kernel_spmd(nc, [arrays], core_ids=[0])
    return r.results[0]["out_0"]
```

```python
from contextlib import ExitStack

import numpy as np

import concourse.bass as bass
from concourse import mybir

F32 = mybir.dt.float32
F32R = mybir.dt.float32r
BF16 = mybir.dt.bfloat16
ALU = mybir.AluOpType
ACT = mybir.ActivationFunctionType
AX = mybir.AxisListType

P = 128
B, S, E = 4, 1024, 256
TOK = B * S
TILE = 512
TILES = TOK // TILE
TPB = S // TILE
BLK = TILE // P
EC = E // P
H, KVH = 16, 4
D1 = E // H
QL, KVL = 64, 32
D2 = 8
HQ = 4
UPB = H // HQ
NX, FF = 8, 512
FC = FF // P
EPS = 1e-5
FLOOR = 0.25
MASK = -1.0e30
LOW = -3.0e38
SA, CA, GA, SB, CB, GB, GB3 = range(7)
NMOD = 7


SIX = ((0, 0), (0, 1), (1, 0), (1, 1), (0, 2), (2, 0))
NINE = SIX + ((1, 2), (2, 1), (2, 2))


class Signal:

    def __init__(self, sem, per, credit=0):
        self.sem, self.per, self.credit = sem, per, credit

    def at(self, unit, steps):
        return (unit + self.credit) * self.per + steps

    def open(self, engine):
        engine.sem_inc(self.sem, self.credit * self.per)


class Steps(Signal):

    def __init__(self, sem, names, credit=0):
        super().__init__(sem, len(names), credit)
        self.names = names

    def after(self, unit, name):
        return self.at(unit, self.names.index(name) + 1)


def in_pairs(engine, units, body):
    with engine.Fori(0, units // 2 - 1) as i:
        body(i, False)
    body(units // 2 - 1, True)


class Place:

    def __init__(self, nc, *spans):
        self.nc, self.spans = nc, [list(span) for span in spans]

    def __call__(self, name, shape, dt):
        size = -(-int(np.prod(shape[1:])) * mybir.dt.size(dt) // 32) * 32
        span = [span for span in self.spans if span[1] - span[0] >= size][0]
        span[0] += size
        return self.nc.alloc_sbuf_tensor_at(name, shape, dt, offset=span[0] - size)

    def end(self):
        return self.spans[-1][0]


class Program:

    def __init__(self, nc, ctx, a):
        self.nc, self.ctx, self.a = nc, ctx, a
        self.sems = 0
        self.bank = ctx.enter_context(nc.psum_tensor("bank", [P, 8, 512], F32))
        self.ident = ctx.enter_context(nc.sbuf_tensor("ident", [P, P], F32))
        self.ident16 = ctx.enter_context(nc.sbuf_tensor("ident16", [P, P], BF16))
        self.mask_kq = ctx.enter_context(nc.sbuf_tensor("mask_kq", [P, P], BF16))
        self.mask_qk = ctx.enter_context(nc.sbuf_tensor("mask_qk", [P, P], BF16))

        def dram(name, shape, dt):
            return nc.dram_tensor(name, shape, dt, kind="Internal").ap()

        self.mod = ctx.enter_context(nc.sbuf_tensor("mod", [P, B, NMOD * EC], F32))
        self.bias = ctx.enter_context(nc.sbuf_tensor("bias", [P, NX * (FC + EC)], F32))

        self.mod_row = dram("mod_row", [B, NMOD, E], F32)
        self.qb = dram("qb", [H * D2], F32)
        self.minus = dram("minus", [2, HQ * S], BF16)
        self.q1 = dram("q1", [3, E, TOK], BF16)
        self.k1 = dram("k1", [3, KVH * D1, TOK], BF16)
        self.q2 = dram("q2", [3, H * D2, TOK], BF16)
        self.k2 = dram("k2", [3, H * D2, TOK], BF16)
        self.v1 = dram("v1", [B, KVH, P, S // P, D1 + 1], F32)
        self.v2 = dram("v2", [B, UPB, P, S // P, HQ, D2 + 1], F32)
        self.o1 = dram("o1", [H * D1, TOK], F32)
        self.o2 = dram("o2", [H * D2, TOK], F32)
        self.den = [dram(f"den{n}", [B, H, S], F32) for n in (1, 2)]
        self.rden1 = dram("rden1", [H, D1, TOK], F32)
        self.rden2 = dram("rden2", [H, D2, TOK], F32)
        self.x1 = dram("x1", [TOK, E], F32)
        self.gh = dram("gh", [E, TOK], F32)
        self.mla = dram("mla", [E, TOK], F32)
        self.comb = dram("comb", [TILES, NX, TILE], F32)

    def sem(self, name):
        self.sems += 1
        return self.ctx.enter_context(self.nc.semaphore(name))

    def mod_of(self, b, column):
        return self.mod[:, bass.ds(b, 1), column:column + 1].rearrange("p b c -> p (b c)")

    def counter(self, name, per, credit=0):
        return Signal(self.sem(name), per, credit)


    def steps(self, name, names, credit=0):
        return Steps(self.sem(name), names, credit)


def modulation(pr, place, block, start_dve, start_pe):
    nc, a = pr.nc, pr.a
    def sb(name, shape, dt=F32):
        return place(name, shape, dt)

    cT = sb("cT", [P, EC, B])
    sig = sb("sig", [P, EC, B])
    siluT = sb("siluT", [P, EC, B])
    wmod = sb("wmod", [P, EC, 6 * E])
    row = sb("row", [B, NMOD, E])
    sign = sb("sign", [B, 2, E])
    brow = sb("brow", [NX * (FC + EC), P])
    minus = sb("minus_ones", [P, 2 * HQ * S // P], BF16)

    loaded = pr.sem("m_loaded")
    made = pr.sem("m_made")
    neg_exp = pr.sem("m_neg_exp")
    silu = pr.sem("m_silu")
    summed = pr.sem("m_summed")
    rows = pr.sem("m_rows")
    turned = pr.sem("m_turned")
    cols = pr.cols = pr.sem("m_cols")
    stored = pr.stored = pr.sem("m_stored")
    negative = pr.sem("m_negative")
    raw = pr.bank[0:B, 5:8, :].rearrange("b n c -> b (n c)").rearrange("b (j e) -> b j e", e=E)

    @block.sync
    def _(sp):
        sp.dma_start(cT[:, 0, :], a["L0_c"][:, 0:P].rearrange("b p -> p b"),
                     allow_slow_non_contiguous=True).then_inc(loaded, 16)
        sp.dma_start(cT[:, 1, :], a["L0_c"][:, P:E].rearrange("b p -> p b"),
                     allow_slow_non_contiguous=True).then_inc(loaded, 16)
        sp.dma_start(wmod[:], a["L0_wmod"].rearrange("(k p) n -> p k n", p=P)).then_inc(loaded, 16)
        sp.dma_start(brow[0:NX * FC, :],
                     a["L0_ffn_b1"].rearrange("x (f p) -> (x f) p", p=P)).then_inc(loaded, 16)
        sp.dma_start(brow[NX * FC:NX * (FC + EC), :],
                     a["L0_ffn_b2"].rearrange("x (f p) -> (x f) p", p=P)).then_inc(loaded, 16)

    @block.gpsimd
    def _(pool):
        pool.memset(minus[:], -1.0).then_inc(negative, 1)
        for m in (pr.ident, pr.ident16, pr.mask_kq, pr.mask_qk):
            pool.memset(m[:], 0.0).then_inc(made, 1)
        pool.wait_ge(made, 4)
        for m in (pr.ident, pr.ident16):
            pool.affine_select(out=m[:], in_=m[:], compare_op=ALU.not_equal, fill=1.0, base=0,
                               pattern=[[-1, P]], channel_multiplier=1).then_inc(made, 1)
        pool.affine_select(out=pr.mask_kq[:], in_=pr.mask_kq[:], compare_op=ALU.is_ge, fill=MASK,
                           base=0, pattern=[[1, P]], channel_multiplier=-1).then_inc(made, 1)
        pool.affine_select(out=pr.mask_qk[:], in_=pr.mask_qk[:], compare_op=ALU.is_ge, fill=MASK,
                           base=0, pattern=[[-1, P]], channel_multiplier=1).then_inc(made, 1)

    @block.scalar
    def _(act):
        act.wait_ge(loaded, 80)
        act.activation(sig[:], cT[:], ACT.Exp, scale=-1.0).then_inc(neg_exp, 1)
        act.dma_start(pr.qb.rearrange("(h d) -> h d", d=D2),
                      a["L0_ffn_q_b"].rearrange("(h d) -> h d", d=D1)[:, 0:D2]).then_inc(stored, 16)
        act.wait_ge(negative, 1)
        act.dma_start(pr.minus.rearrange("r (p n) -> (r p) n", n=2 * HQ * S // P), minus[:]).then_inc(stored, 16)
        act.wait_ge(rows, 12)
        act.dma_start(pr.mod_row, row[:]).then_inc(stored, 16)

    @block.vector
    def _(dve):
        dve.wait_ge(neg_exp, 1)
        dve.tensor_scalar(sig[:], sig[:], 1.0, None, ALU.add).then_inc(silu, 1)
        dve.wait_ge(silu, 1)
        dve.reciprocal(sig[:], sig[:]).then_inc(silu, 1)
        dve.wait_ge(silu, 2)
        dve.tensor_tensor(siluT[:], cT[:], sig[:], ALU.mult).then_inc(silu, 1)
        start_dve(dve)
        dve.wait_ge(summed, 1)
        for j, f in ((SA, None), (SB, None), (CA, 1.0), (CB, 1.0)):
            if f is None:
                dve.tensor_copy(row[:, j, :], raw[:, j, :]).then_inc(rows, 1)
            else:
                dve.tensor_scalar(row[:, j, :], raw[:, j, :], f, None, ALU.add).then_inc(rows, 1)
        for n, j in enumerate((GA, GB)):
            dve.tensor_scalar(sign[:, n, :], raw[:, j, :], 0.0, 2.0, ALU.is_ge, ALU.mult).then_inc(rows, 1)
        dve.wait_ge(rows, 6)
        dve.tensor_scalar(sign[:], sign[:], -1.0, None, ALU.add).then_inc(rows, 1)
        dve.wait_ge(rows, 7)
        for n, j in enumerate((GA, GB)):
            dve.tensor_tensor(row[:, j, :], raw[:, j, :], sign[:, n, :], ALU.mult).then_inc(rows, 1)
        dve.wait_ge(rows, 9)
        for n, j in enumerate((GA, GB)):
            dve.scalar_tensor_tensor(out=row[:, j, :], in0=row[:, j, :], scalar=FLOOR,
                                     in1=sign[:, n, :], op0=ALU.max, op1=ALU.mult).then_inc(rows, 1)
        dve.wait_ge(rows, 11)
        dve.tensor_scalar(row[:, GB3, :], row[:, GB, :], 0.3, None, ALU.mult).then_inc(rows, 1)
        dve.wait_ge(turned, 1)
        dve.tensor_copy(pr.mod[:], pr.bank[:, 3, 0:NMOD * EC * B].rearrange("p (c b) -> p b c", b=B)).then_inc(cols, 1)
        dve.tensor_copy(pr.bias[:], pr.bank[:, 4, 0:NX * (FC + EC)]).then_inc(cols, 1)

    @block.tensor
    def _(pe):
        pe.wait_ge(silu, 3)
        for n in range(3):
            for k in range(EC):
                mm = pe.matmul(pr.bank[0:B, 5 + n, :], siluT[:, k, :], wmod[:, k, n * 512:(n + 1) * 512],
                               start=(k == 0), stop=(k == EC - 1))
        mm.then_inc(summed, 1)
        pe.wait_ge(made, 8)
        start_pe(pe)
        pe.wait_ge(rows, 12)
        flat = row[:].rearrange("b j e -> b (j e)")
        for c in range(NMOD * EC):
            pe.transpose(pr.bank[:, 3, c * B:(c + 1) * B], flat[:, c * P:(c + 1) * P], pr.ident[0:B, 0:B])
        n = NX * (FC + EC)
        pe.transpose(pr.bank[:, 4, 0:n], brow[:], pr.ident[0:n, 0:n]).then_inc(turned, 1)


class Norm:

    def __init__(self, pr, sb, name, shift, scale):
        self.pr, self.shift, self.scale = pr, shift, scale
        self.stats = sb(name + "_stats", [P, BLK, 6])
        self.mean = sb(name + "_mean", [P, BLK])
        self.diff = sb(name + "_diff", [P, BLK])
        self.var = sb(name + "_var", [P, BLK])
        self.rstd = sb(name + "_rstd", [P, BLK])
        self.power = sb(name + "_power", [P, BLK])
        self.xn = sb(name + "_xn", [P, BLK, E])
        self.hT = sb(name + "_hT", [P, EC, TILE])
        self.stat = pr.counter(name + "_stat", BLK + 6)
        self.var_ready = pr.counter(name + "_var_ready", 1)
        self.rstd_ready = pr.counter(name + "_rstd_ready", 1)
        self.xn_ready = pr.counter(name + "_xn_ready", 1)
        self.turned = pr.counter(name + "_turned", 1, credit=1)
        self.h_ready = pr.counter(name + "_h_ready", EC, credit=1)

    def open(self, engine, which):
        {"pe": self.turned, "act": self.h_ready}[which].open(engine)

    def statistics(self, dve, n, x):
        for b in range(BLK):
            dve.bn_stats(self.stats[:, b, :], x[:, b, :]).then_inc(self.stat.sem, 1)
        even, odd = (self.stats[:, :, 1], self.stats[:, :, 2]), (self.stats[:, :, 4], self.stats[:, :, 5])
        sem, at = self.stat.sem, self.stat.at
        dve.wait_ge(sem, at(n, BLK))
        dve.tensor_tensor(self.mean[:], even[0], odd[0], ALU.add).then_inc(sem, 1)
        dve.tensor_tensor(self.diff[:], even[0], odd[0], ALU.subtract).then_inc(sem, 1)
        dve.tensor_tensor(self.var[:], even[1], odd[1], ALU.add).then_inc(sem, 1)
        dve.wait_ge(sem, at(n, BLK + 3))
        dve.tensor_scalar(self.mean[:], self.mean[:], 0.5, None, ALU.mult).then_inc(sem, 1)
        dve.tensor_scalar(self.var[:], self.var[:], 1.0 / E, EPS, ALU.mult, ALU.add).then_inc(sem, 1)
        dve.scalar_tensor_tensor(out=self.diff[:], in0=self.diff[:], scalar=0.25, in1=self.diff[:],
                                 op0=ALU.mult, op1=ALU.mult).then_inc(sem, 1)
        dve.wait_ge(sem, at(n, BLK + 6))
        dve.tensor_tensor(self.var[:], self.var[:], self.diff[:], ALU.add).then_inc(self.var_ready.sem, 1)

    def normalise(self, dve, n, x):
        dve.wait_ge(self.turned.sem, self.turned.at(n - 1, 1))
        dve.wait_ge(self.rstd_ready.sem, self.rstd_ready.at(n, 1))
        for b in range(BLK):
            op = dve.tensor_scalar(self.xn[:, b, :], x[:, b, :], self.mean[:, b:b + 1], self.rstd[:, b:b + 1],
                                   ALU.subtract, ALU.mult)
        op.then_inc(self.xn_ready.sem, 1)

    def pool(self, pool, n):
        pool.wait_ge(self.var_ready.sem, self.var_ready.at(n, 1))
        pool.tensor_tensor(self.rstd[:], self.var[:], self.power[:], ALU.pow).then_inc(self.rstd_ready.sem, 1)

    def pe(self, pe, n):
        pe.wait_ge(self.xn_ready.sem, self.xn_ready.at(n, 1))
        for c in range(EC):
            for b in range(BLK):
                mm = pe.transpose(self.pr.bank[:, c, b * P:(b + 1) * P], self.xn[:, b, c * P:(c + 1) * P],
                                  self.pr.ident[:])
        mm.then_inc(self.turned.sem, 1)

    def act(self, act, n, b):
        act.wait_ge(self.turned.sem, self.turned.at(n, 1))
        for c in range(EC):
            sc, sh = self.scale * EC + c, self.shift * EC + c
            act.activation(self.hT[:, c, :], self.pr.bank[:, c, :], ACT.Identity,
                           bias=self.pr.mod_of(b, sh), scale=self.pr.mod_of(b, sc)).then_inc(self.h_ready.sem, 1)


def from_x(pr, place):
    nc, a = pr.nc, pr.a
    LAT = QL + KVL
    R = slice(QL, LAT)
    NK = KVH * D1
    ROWS = (P, P, NK)
    def sb(name, shape, dt=F32):
        return place(name, shape, dt)

    x = sb("p1_x", [P, 2, BLK, E])
    norm = Norm(pr, sb, "p1", SA, CA)
    wa = sb("p1_wa", [P, EC, LAT])
    wq = sb("p1_wq", [LAT, E])
    wq_turn = sb("p1_wq_turn", [LAT, E])
    wkv = sb("p1_wkv", [LAT, 2 * NK])
    wk = sb("p1_wk", [LAT, NK])
    wk_turn = sb("p1_wk_turn", [LAT, NK])
    wv = sb("p1_wv", [LAT, NK])
    cos = sb("p1_cos", [P, S])
    sin = sb("p1_sin", [P, S])
    lat = sb("p1_lat", [LAT, TILE])
    rotated = [sb(f"p1_rotated{c}", [ROWS[c], TILE]) for c in range(3)]
    rest = [sb(f"p1_rest{c}", [ROWS[c], TILE]) for c in range(3)]
    parts = [[sb(f"p1_part{k}{c}", [ROWS[c], 3, TILE], BF16) for c in range(3)] for k in range(2)]
    v = [sb(f"p1_v{k}", [P, KVH, BLK, D1 + 1]) for k in range(2)]
    sums = [pr.bank[0:ROWS[c], (3, 5, 3)[c], :] for c in range(3)]
    turns = [pr.bank[0:ROWS[c], (4, 6, 4)[c], :] for c in range(3)]

    loaded = pr.sem("p1_loaded")
    filled = pr.sem("p1_filled")
    weights = pr.sem("p1_weights")
    x_in = [pr.counter(f"p1_x_in{k}", 16) for k in range(2)]
    lat_sum = pr.counter("p1_lat_sum", 1)
    lat_ready = pr.counter("p1_lat_ready", 1)
    qk_sum = pr.counter("p1_qk_sum", 3)
    v_sum = pr.counter("p1_v_sum", 1)
    v_ready = pr.counter("p1_v_ready", 1, credit=1)
    steps = pr.steps("p1_steps", ("cos0", "sin0", "add0", "cos1", "sin1", "add1", "less0_0", "cos2", "sin2",
                                  "less0_1", "less1_0", "less1_1"), credit=1)
    steps_k = pr.steps("p1_steps_k", ("add2", "less0_2", "less1_2"), credit=1)
    casts = pr.steps("p1_casts", ("cast0_0", "cast0_1", "cast1_0", "cast1_1", "cast0_2", "cast2_0",
                                  "cast2_1", "cast1_2", "cast2_2"), credit=1)
    stored = [pr.counter(f"p1_stored{k}", 64, credit=1) for k in range(2)]

    def written(sp, b):
        for k in range(2):
            sp.wait_ge(stored[k].sem, stored[k].at(b, 64))

    def free(pe):
        pe.wait_ge(v_ready.sem, v_ready.at(TILES - 1, 1))
        pe.wait_ge(steps.sem, steps.after(TILES - 1, "sin2"))

    def start_dve(dve):
        dve.wait_ge(x_in[0].sem, x_in[0].at(0, 16))
        norm.statistics(dve, 0, x[:, 0])
        norm.normalise(dve, 0, x[:, 0])
        dve.wait_ge(loaded, 96)
        dve.wait_ge(filled, 5)
        dve.tensor_copy(wk[R, :], wkv[R, 0::2])
        dve.tensor_copy(wv[R, :], wkv[R, 1::2])
        for to, of in ((wq_turn[0:QL], wq[0:QL]), (wk_turn[R], wkv[R, 0::2])):
            dve.tensor_scalar(to[:, 0::2], of[:, 1::2], -1.0, None, ALU.mult)
            dve.tensor_copy(to[:, 1::2], of[:, 0::2]).then_inc(weights, 1)

    def start_pe(pe):
        norm.open(pe, "pe")
        norm.pe(pe, 0)

    def emit(block, preload_next):
        @block.sync
        def _(sp):
            stored[0].open(sp)
            stored[1].open(sp)

            def load(i, k):
                sp.dma_start(x[:, k], a["L0_attn_x"][bass.ds(i, 1), k * TILE:(k + 1) * TILE, :]
                             .rearrange("b (n p) e -> p (b n) e", p=P)).then_inc(x_in[k].sem, 16)

            load(0, 0)
            sp.dma_start(wkv[R, :], a["L0_attn_Wkvb"]).then_inc(loaded, 16)
            sp.dma_start(wa[:, :, 0:QL], a["L0_attn_Wqa"].rearrange("(k p) n -> p k n", p=P)).then_inc(loaded, 16)
            sp.dma_start(wa[:, :, QL:LAT], a["L0_attn_Wkva"].rearrange("(k p) n -> p k n", p=P)).then_inc(loaded, 16)
            sp.wait_ge(filled, 1)
            sp.dma_start(wq[0:QL, :], a["L0_attn_Wqb"]).then_inc(loaded, 16)
            sp.dma_start(cos[:], a["rope_cos"]).then_inc(loaded, 16)
            sp.dma_start(sin[:], a["rope_sin"]).then_inc(loaded, 16)
            load(0, 1)

            def pair(i, last):
                for k in range(TPB):
                    n = i * TPB + k
                    if not last:
                        sp.wait_ge(norm.h_ready.sem, norm.h_ready.at(n, EC))
                        load(i + 1, k)
                    tok = bass.ds(n * TILE, TILE)
                    sp.wait_ge(v_ready.sem, v_ready.at(n, 1))
                    sp.dma_start(pr.v1[bass.ds(i, 1), :, :, k * BLK:(k + 1) * BLK, :].rearrange("b g p n d -> p (b g) (n d)"),
                                 v[k][:].rearrange("p g n d -> p g (n d)")).then_inc(stored[k].sem, 16)
                    sp.wait_ge(casts.sem, casts.after(n, "cast2_1"))
                    for c in range(2):
                        sp.dma_start(pr.q1[:, c * P:(c + 1) * P, tok].rearrange("s p t -> p s t"),
                                     parts[k][c][:]).then_inc(stored[k].sem, 16)
                    sp.wait_ge(casts.sem, casts.after(n, "cast2_2"))
                    sp.dma_start(pr.k1[:, :, tok].rearrange("s p t -> p s t"), parts[k][2][:]).then_inc(stored[k].sem, 16)

            with sp.Fori(0, B - 1) as i:
                pair(i, False)
            preload_next(sp, written)
            pair(B - 1, True)

        @block.gpsimd
        def _(pool):
            steps_k.open(pool)
            pool.memset(wq[:], 0.0).then_inc(filled, 1)
            for t in (wq_turn, wk, wk_turn, wv):
                pool.memset(t[:], 0.0).then_inc(filled, 1)
            pool.memset(norm.power[:], -0.5).then_inc(filled, 1)
            for k in range(2):
                pool.memset(v[k][:], 1.0).then_inc(filled, 1)
            pool.wait_ge(filled, 8)
            norm.pool(pool, 0)

            def pair(i, last):
                for k in range(TPB):
                    n = i * TPB + k
                    if k == 0 or not last:
                        norm.pool(pool, n + 1)
                    pool.wait_ge(steps.sem, steps.after(n, "sin2"))
                    pool.tensor_tensor(rotated[2][:], rotated[2][:], rest[2][:], ALU.add).then_inc(steps_k.sem, 1)
                    pool.wait_ge(casts.sem, casts.after(n, "cast0_2"))
                    pool.tensor_tensor(rest[2][:], rotated[2][:], parts[k][2][:, 0, :], ALU.subtract).then_inc(steps_k.sem, 1)
                    pool.wait_ge(casts.sem, casts.after(n, "cast1_2"))
                    pool.tensor_tensor(rest[2][:], rest[2][:], parts[k][2][:, 1, :], ALU.subtract).then_inc(steps_k.sem, 1)

            in_pairs(pool, TILES, pair)

        @block.scalar
        def _(act):
            norm.open(act, "act")
            v_ready.open(act)
            casts.open(act)
            act.wait_ge(filled, 8)
            act.wait_ge(pr.cols, 2)

            def latents(n, b):
                norm.act(act, n, b)

            def copy_latents(n):
                act.wait_ge(lat_sum.sem, lat_sum.at(n, 1))
                act.copy(lat[:], pr.bank[0:LAT, 2, :]).then_inc(lat_ready.sem, 1)

            latents(0, 0)
            copy_latents(0)

            def pair(i, last):
                for k in range(TPB):
                    n = i * TPB + k
                    more = k == 0 or not last

                    def cast(part, c):
                        sig = steps_k if c == 2 else steps
                        act.wait_ge(sig.sem, sig.after(n, f"less{part - 1}_{c}" if part else f"add{c}"))
                        act.copy(parts[k][c][:, part, :], (rest if part else rotated)[c][:]).then_inc(casts.sem, 1)

                    act.wait_ge(stored[k].sem, stored[k].at(i - 1, 64))
                    cast(0, 0)
                    act.wait_ge(v_sum.sem, v_sum.at(n, 1))
                    act.copy(v[k][:, :, :, 0:D1].rearrange("p g n d -> p n g d"),
                             pr.bank[:, 7, 0:BLK * NK].rearrange("p (n g d) -> p n g d", n=BLK, g=KVH)).then_inc(v_ready.sem, 1)
                    if more:
                        latents(n + 1, i + k)
                    cast(0, 1)
                    cast(1, 0)
                    cast(1, 1)
                    if more:
                        copy_latents(n + 1)
                    cast(0, 2)
                    cast(2, 0)
                    cast(2, 1)
                    cast(1, 2)
                    cast(2, 2)

            in_pairs(act, TILES, pair)

        @block.vector
        def _(dve):
            steps.open(dve)

            def pair(i, last):
                for k in range(TPB):
                    n = i * TPB + k
                    more = k == 0 or not last
                    pos = slice(k * TILE, (k + 1) * TILE)

                    def rotate(c):
                        dve.wait_ge(casts.sem, casts.after(n - 1, f"cast2_{c}"))
                        dve.wait_ge(qk_sum.sem, qk_sum.at(n, c + 1))
                        dve.tensor_tensor(rotated[c][:], sums[c], cos[0:ROWS[c], pos], ALU.mult).then_inc(steps.sem, 1)
                        dve.tensor_tensor(rest[c][:], turns[c], sin[0:ROWS[c], pos], ALU.mult).then_inc(steps.sem, 1)

                    def add(c):
                        dve.wait_ge(steps.sem, steps.after(n, f"sin{c}"))
                        dve.tensor_tensor(rotated[c][:], rotated[c][:], rest[c][:], ALU.add).then_inc(steps.sem, 1)

                    def less(part, c):
                        dve.wait_ge(casts.sem, casts.after(n, f"cast{part}_{c}"))
                        dve.tensor_tensor(rest[c][:], (rest if part else rotated)[c][:], parts[k][c][:, part, :],
                                          ALU.subtract).then_inc(steps.sem, 1)

                    if more:
                        dve.wait_ge(x_in[1 - k].sem, x_in[1 - k].at(i + k, 16))
                        norm.statistics(dve, n + 1, x[:, 1 - k])
                    rotate(0)
                    add(0)
                    if more:
                        norm.normalise(dve, n + 1, x[:, 1 - k])
                    rotate(1)
                    add(1)
                    less(0, 0)
                    rotate(2)
                    less(0, 1)
                    less(1, 0)
                    less(1, 1)

            in_pairs(dve, TILES, pair)

        @block.tensor
        def _(pe):
            pe.wait_ge(weights, 2)
            pe.wait_ge(loaded, 96)

            def latents(n):
                for c in range(EC):
                    pe.wait_ge(norm.h_ready.sem, norm.h_ready.at(n, c + 1))
                    mm = pe.matmul(pr.bank[0:LAT, 2, :], wa[:, c, :], norm.hT[:, c, :],
                                   start=(c == 0), stop=(c == EC - 1))
                mm.then_inc(lat_sum.sem, 1)

            latents(0)

            def pair(i, last):
                for k in range(TPB):
                    n = i * TPB + k
                    pe.wait_ge(lat_ready.sem, lat_ready.at(n, 1))
                    pe.wait_ge(steps.sem, steps.after(n - 1, "sin2"))
                    for c in range(3):
                        cols = slice(0, NK) if c == 2 else slice(c * P, (c + 1) * P)
                        if c == 2:
                            pe.wait_ge(steps.sem, steps.after(n, "sin0"))
                        pe.matmul(sums[c], (wq, wq, wk)[c][:, cols], lat[:], start=True, stop=True)
                        pe.matmul(turns[c], (wq_turn, wq_turn, wk_turn)[c][:, cols], lat[:],
                                  start=True, stop=True).then_inc(qk_sum.sem, 1)
                    pe.wait_ge(v_ready.sem, v_ready.at(n - 1, 1))
                    for b in range(BLK):
                        mm = pe.matmul(pr.bank[:, 7, b * NK:(b + 1) * NK], lat[:, b * P:(b + 1) * P], wv[:],
                                       start=True, stop=True, skip_group_check=True)
                    mm.then_inc(v_sum.sem, 1)
                    if k == 0 or not last:
                        norm.pe(pe, n + 1)
                        latents(n + 1)

            in_pairs(pe, TILES, pair)

        def late(dve):
            pass

        return written, free, late

    return start_dve, start_pe, emit


def attention(pr, place, name, q, k, v, o, sums, rden, width, pairs, causal, scale):
    nc = pr.nc
    R = len(pairs) * width
    JK = 1 if causal else HQ
    KB, QB = S // P, S // P
    steps = [(t, kb) for t in range(TPB) for kb in range(KB) if not causal or kb * P < (t + 1) * TILE]
    L = len(steps)
    ends = [max(s for s in range(L) if steps[s][0] == t) for t in range(TPB)]
    looks = [(j, i, c) for j in range(HQ) for i in range(QB) for c in range(TPB)
             if not causal or c * TILE < (i + 1) * P]
    NL = len(looks)
    LPS = NL // L
    assert NL == LPS * L
    EARLY = 3
    AHEAD = EARLY * LPS
    TURN = -1
    uses = [0, 1, TURN] + list(range(2, NL))
    bank_of = {m: n % 3 for n, m in enumerate(uses)}
    if NL % 3 == 0:
        bank_of[NL - 1] = 1

    def before(m):
        n = uses.index(m)
        earlier = [w for w in uses[:n] if bank_of[w] == bank_of[m]]
        return (earlier[-1], False) if earlier else ([w for w in uses if bank_of[w] == bank_of[m]][-1], True)

    def sb(n, shape, dt=F32):
        return place(f"{name}_{n}", shape, dt)

    Q = [sb(f"Q{g}", [R + 2, HQ, S], BF16) for g in range(UPB)]
    K = [sb(f"K{g}", [R + 2, JK, S], BF16) for g in range(UPB)]
    V = [sb(f"V{g}", [P, JK, KB, width + 1] if causal else [P, KB, JK, width + 1]) for g in range(UPB)]
    prob = [sb(f"prob{n}", [P, HQ, TILE]) for n in range(2)]
    out = [sb(f"out{t}", [P, TILE]) for t in range(TPB)]
    peak = sb("peak", [P, HQ * QB, TPB])
    top = sb("top", [P, HQ * QB])
    top_hi = [sb(f"top_hi{g}", [HQ * QB, P], BF16) for g in range(UPB)]
    top_lo = [sb(f"top_lo{g}", [HQ * QB, P], BF16) for g in range(UPB)]
    den = sb("den", [P, HQ * S // P])
    rden_sq = sb("rden_sq", [P, HQ * S // P])
    scores = pr.bank[:, 0:4, :]
    acc = pr.bank[:, 4, :]
    look = pr.bank[:, 5:8, :]

    nload = 2 * len(pairs) + 1
    filled = pr.sem(name + "_filled")
    cleared = pr.sem(name + "_cleared")
    loaded = [pr.counter(f"{name}_loaded{g}", 16 * nload) for g in range(UPB)]
    shift_in = [pr.counter(f"{name}_shift_in{g}", 32, credit=1) for g in range(UPB)]
    qk_done = pr.counter(name + "_qk_done", 2 * L)
    exp_done = pr.counter(name + "_exp_done", 2 * L, credit=1)
    pv_done = pr.counter(name + "_pv_done", L, credit=1)
    taken = pr.counter(name + "_taken", TPB)
    stored = [pr.counter(f"{name}_stored{t}", 16 * (HQ + 1), credit=1 + t) for t in range(TPB)]
    den_in = pr.counter(name + "_den_in", 16, credit=1)
    den_done = pr.counter(name + "_den_done", 1)
    den_out = pr.counter(name + "_den_out", 16 * HQ, credit=2)
    look_done = pr.counter(name + "_look_done", NL)
    look_read = pr.counter(name + "_look_read", NL, credit=1)
    topped = pr.counter(name + "_topped", 1, credit=1)
    turned = pr.counter(name + "_turned", 1)
    rows_made = pr.counter(name + "_rows_made", 2, credit=1)

    def units(engine, body):
        with engine.Fori(0, B - 1) as b:
            for g in range(UPB):
                body(b, g, 2)
        for g in range(UPB):
            body(B - 1, g, min(2, UPB - 1 - g))

    def after(b, g):
        return (b, g + 1) if g < UPB - 1 else (b + 1, 0)

    def looks_of(b, g, s, more):
        if s < L - EARLY:
            return (*after(b, g), AHEAD + s * LPS, AHEAD + (s + 1) * LPS) if more else None
        first = (s - (L - EARLY)) * LPS
        return (*after(*after(b, g)), first, first + LPS) if more == 2 else None

    def load(sp, b, g):
        tok = bass.ds(b * S, S)
        sem = loaded[g].sem
        for n, (qi, ki) in enumerate(pairs):
            rows = slice(n * width, (n + 1) * width)
            for slot, of, part, heads in ((Q[g], q, qi, HQ), (K[g], k, ki, JK)):
                feats = of[part, g * heads * width:(g + 1) * heads * width, tok]
                sp.dma_start(slot[rows, :, :], feats.rearrange("(j d) t -> d j t", d=width)).then_inc(sem, 16)
        sp.dma_start(V[g][:].rearrange("p a b d -> p (a b d)"),
                     v[bass.ds(b, 1), g].rearrange("b p n d -> (b p) (n d)" if causal
                                                   else "b p n j d -> (b p) (n j d)")).then_inc(sem, 16)

    def preload(sp, written):
        for s in shift_in + stored + [den_in, den_out]:
            s.open(sp)
        written(sp, 0)
        load(sp, 0, 0)
        sp.wait_ge(pr.stored, 48)
        for g in range(UPB):
            sp.dma_start(K[g][R:R + 2, :, :].rearrange("r j t -> r (j t)"), pr.minus[:, 0:JK * S]).then_inc(filled, 16)
        for g in range(1, UPB):
            load(sp, 0, g)

    def invert(dve, u):
        dve.wait_ge(den_in.sem, den_in.at(u, 16))
        dve.wait_ge(den_out.sem, den_out.at(u - 1, 16 * HQ))
        dve.reciprocal(rden_sq[:], den[:]).then_inc(den_done.sem, 1)

    def out_written(sp, b):
        for n in range(TPB):
            sp.wait_ge(stored[n].sem, stored[n].at(b * UPB + UPB - 1, 16 * (HQ + 1)))
        sp.wait_ge(den_out.sem, den_out.at(b * UPB + UPB - 1, 16 * HQ))

    def out_free(pe):
        pe.wait_ge(taken.sem, taken.at(B * UPB - 1, TPB + 1))

    def late(dve):
        invert(dve, B * UPB - 1)

    def emit(block, written, free, preload_next, resume_next):
        @block.sync
        def _(sp):

            def shift(b, g):
                sp.wait_ge(rows_made.sem, rows_made.at(b * UPB + g, 2))
                for r, part in ((R, top_hi[g]), (R + 1, top_lo[g])):
                    sp.dma_start(Q[g][r:r + 1, :, :].rearrange("o j (i q) -> o (j i) q", q=P),
                                 part[:]).then_inc(shift_in[g].sem, 16)

            shift(0, 0)

            def unit(b, g, more):
                u = b * UPB + g
                if more:
                    shift(*after(b, g))
                for t in range(TPB):
                    sp.wait_ge(taken.sem, taken.at(u, t + 2))
                    tok = bass.ds(b * S + t * TILE, TILE)
                    for j in range(HQ):
                        f = (g * HQ + j) * width
                        sp.dma_start(o[f:f + width, tok], out[t][32 * j:32 * j + width, :]).then_inc(stored[t].sem, 16)
                    sp.dma_start(sums[bass.ds(b, 1), g * HQ:(g + 1) * HQ, t * TILE:(t + 1) * TILE]
                                 .rearrange("b h t -> (b h) t"), out[t][width::32, :]).then_inc(stored[t].sem, 16)
                if not more:
                    resume_next(sp)
                for t in range(TPB):
                    sp.wait_ge(stored[t].sem, stored[t].at(u, 16 * (HQ + 1)))
                sp.wait_ge(den_done.sem, den_done.at(u, 1))
                sp.dma_start(den[:], sums[bass.ds(b, 1), g * HQ:(g + 1) * HQ, :]
                             .rearrange("b h (s t) -> (b h s) t", t=HQ * S // P)).then_inc(den_in.sem, 16)
                if more and not isinstance(b, int):
                    if g == 0:
                        written(sp, b + 1)
                    load(sp, b + 1, g)
                if more == 1:
                    preload_next(sp, out_written)
                sp.wait_ge(den_done.sem, den_done.at(u + 1, 1))
                for j in range(HQ):
                    n = P // HQ
                    part = rden_sq[j * n:(j + 1) * n, :]
                    sp.dma_start(rden[g * HQ + j][:, bass.ds(b * S, S)].rearrange("d (s t) -> s d t", s=n),
                                 part.unsqueeze(1).broadcast_to([n, width, S // n])).then_inc(den_out.sem, 16)

            units(sp, unit)
            for t in range(TPB):
                sp.wait_ge(stored[t].sem, stored[t].at(B * UPB - 1, 16 * (HQ + 1)))
            sp.wait_ge(den_out.sem, den_out.at(B * UPB - 1, 16 * HQ))

        @block.scalar
        def _(act):
            exp_done.open(act)
            act.wait_ge(cleared, 3)

            def take(t, u):
                act.wait_ge(pv_done.sem, pv_done.at(u, ends[t] + 1))
                act.wait_ge(stored[t].sem, stored[t].at(u - 1, 16 * (HQ + 1)))
                act.copy(out[t][:], acc).then_inc(taken.sem, 1)

            def unit(b, g, more):
                u = b * UPB + g
                for s, (t, kb) in enumerate(steps):
                    off = max(0, kb * P - t * TILE) if causal else 0
                    act.wait_ge(pv_done.sem, pv_done.at(u, s - 1))
                    for n in range(2):
                        act.wait_ge(qk_done.sem, qk_done.at(u, 2 * s + n + 1))
                        act.activation(prob[s % 2][:, 2 * n:2 * n + 2, off:], scores[:, 2 * n:2 * n + 2, off:],
                                       ACT.Exp, scale=scale).then_inc(exp_done.sem, 1)
                    if s == 0:
                        take(1, u - 1)
                    if s == ends[0] + 1:
                        take(0, u)

            units(act, unit)
            take(1, B * UPB - 1)

        @block.vector
        def _(dve):
            look_read.open(dve)
            topped.open(dve)
            rows_made.open(dve)
            dve.memset(peak[:], LOW).then_inc(cleared, 1)
            dve.memset(den[:], 1.0).then_inc(cleared, 1)
            dve.memset(acc, 0.0).then_inc(cleared, 1)
            dve.wait_ge(cleared, 3)

            def peaks(b, g, first, last):
                u = b * UPB + g
                for m in range(first, last):
                    j, i, c = looks[m]
                    n = min(TILE, (i + 1) * P - c * TILE) if causal else TILE
                    dve.wait_ge(look_done.sem, look_done.at(u, m + 1))
                    if m == 0:
                        dve.wait_ge(topped.sem, topped.at(u - 1, 1))
                    dve.tensor_reduce(peak[:, j * QB + i, c:c + 1], look[:, bank_of[m], 0:n], AX.X,
                                      ALU.max).then_inc(look_read.sem, 1)

            def summits(b, g):
                u = b * UPB + g
                dve.wait_ge(look_read.sem, look_read.at(u, NL))
                dve.tensor_reduce(top[:], peak[:], AX.X, ALU.max).then_inc(topped.sem, 1)

            def rows(b, g):
                u = b * UPB + g
                dve.wait_ge(turned.sem, turned.at(u, 1))
                dve.wait_ge(shift_in[g].sem, shift_in[g].at(b - 1, 32))
                turned_top = look[0:HQ * QB, bank_of[TURN], 0:P]
                dve.tensor_copy(top_hi[g][:], turned_top).then_inc(rows_made.sem, 1)
                dve.wait_ge(rows_made.sem, rows_made.at(u, 1))
                dve.tensor_tensor(top_lo[g][:], turned_top, top_hi[g][:], ALU.subtract).then_inc(rows_made.sem, 1)

            peaks(0, 0, 0, NL)
            summits(0, 0)
            peaks(0, 1, 0, 2)
            rows(0, 0)
            peaks(0, 1, 2, AHEAD)

            def unit(b, g, more):
                for s in range(L):
                    at = looks_of(b, g, s, more)
                    if s == L - 5:
                        invert(dve, b * UPB + g - 1)
                    if at:
                        peaks(*at[:3], at[2] + 2)
                    if s == L - EARLY and more:
                        rows(*after(b, g))
                    if at:
                        peaks(*at[:2], at[2] + 2, at[3])
                    if s == L - EARLY - 1 and more:
                        summits(*after(b, g))

            units(dve, unit)

        @block.tensor
        def _(pe):
            pv_done.open(pe)
            pe.wait_ge(cleared, 3)
            free(pe)

            def look_for(b, g, first, last):
                u = b * UPB + g
                if first == 0:
                    pe.wait_ge(loaded[g].sem, loaded[g].at(b + 1, 0))
                for m in range(first, last):
                    j, i, c = looks[m]
                    n = min(TILE, (i + 1) * P - c * TILE) if causal else TILE
                    diag = causal and c == i * P // TILE
                    use, last = before(m)
                    v = u - 1 if last else u
                    if use == TURN:
                        pe.wait_ge(rows_made.sem, rows_made.at(u - 1, 2))
                    else:
                        pe.wait_ge(look_read.sem, look_read.at(v, use + 1))
                    mm = pe.matmul(look[:, bank_of[m], 0:n], Q[g][0:R, j, i * P:(i + 1) * P],
                                   K[g][0:R, j % JK, c * TILE:c * TILE + n], start=True, stop=not diag)
                    if diag:
                        mm = pe.matmul(look[:, bank_of[m], n - P:n], pr.ident16[:], pr.mask_qk[:], start=False, stop=True)
                    mm.then_inc(look_done.sem, 1)

            def turn(b, g):
                pe.wait_ge(topped.sem, topped.at(b * UPB + g, 1))
                pe.transpose(look[0:HQ * QB, bank_of[TURN], 0:P], top[:], pr.ident[:]).then_inc(turned.sem, 1)

            def score(b, g, s, n):
                u = b * UPB + g
                t, kb = steps[s]
                off = max(0, kb * P - t * TILE) if causal else 0
                diag = causal and kb * P >= t * TILE
                if s == 0 and n == 0:
                    pe.wait_ge(shift_in[g].sem, shift_in[g].at(b, 32))
                pe.wait_ge(exp_done.sem, exp_done.at(u, 2 * s - 2 + n + 1))
                for j in (2 * n, 2 * n + 1):
                    mm = pe.matmul(scores[:, j, off:], K[g][:, j % JK, kb * P:(kb + 1) * P],
                                   Q[g][:, j, t * TILE + off:(t + 1) * TILE], start=True, stop=not diag)
                    if diag:
                        mm = pe.matmul(scores[:, j, off:off + P], pr.ident16[:], pr.mask_kq[:], start=False, stop=True)
                mm.then_inc(qk_done.sem, 1)

            look_for(0, 0, 0, NL)
            look_for(0, 1, 0, 2)
            turn(0, 0)
            look_for(0, 1, 2, AHEAD)
            pe.wait_ge(filled, 16 * UPB)
            score(0, 0, 0, 0)
            score(0, 0, 0, 1)

            def unit(b, g, more):
                u = b * UPB + g
                for s, (t, kb) in enumerate(steps):
                    off = max(0, kb * P - t * TILE) if causal else 0
                    at = looks_of(b, g, s, more)
                    ahead = (b, g, s + 1) if s < L - 1 else (*after(b, g), 0)
                    n0, n1 = (2, 0) if s == L - EARLY else (1, 2)
                    if at:
                        look_for(*at[:3], at[2] + n0)
                    if s == L - EARLY and more:
                        turn(*after(b, g))
                    if s < L - 1 or more:
                        score(*ahead, 0)
                    if at:
                        look_for(*at[:2], at[2] + n0, at[2] + n0 + n1)
                    if s < L - 1 or more:
                        score(*ahead, 1)
                    if at:
                        look_for(*at[:2], at[2] + n0 + n1, at[3])
                    pe.wait_ge(exp_done.sem, exp_done.at(u, 2 * s + 2))
                    if s in (0, ends[0] + 1):
                        pe.wait_ge(taken.sem, taken.at(u, t + 1))
                    for j in range(HQ):
                        w = V[g][:, 0, kb, :] if causal else V[g][:, kb, j, :]
                        mm = pe.matmul(acc[32 * j:32 * j + width + 1, off:], w, prob[s % 2][:, j, off:],
                                       start=(kb == 0), stop=(s == ends[t]), skip_group_check=True)
                    mm.then_inc(pv_done.sem, 1)

            units(pe, unit)

        return out_written, out_free, late

    return preload, emit


def between(pr, place):
    nc, a = pr.nc, pr.a
    def sb(name, shape, dt=F32):
        return place(name, shape, dt)

    x = [sb(f"p3_x{k}", [P, BLK, E]) for k in range(2)]
    o = [sb(f"p3_o{k}", [P, EC, TILE]) for k in range(2)]
    rden = [sb(f"p3_rden{k}", [P, EC, TILE]) for k in range(2)]
    gate = sb("p3_gate", [P, E])
    norm = Norm(pr, sb, "p3", SB, CB)
    wout = sb("p3_wout", [P, EC, E])
    gwout = sb("p3_gwout", [P, EC, E])
    bout = sb("p3_bout", [P, E])
    gbias = sb("p3_gbias", [P, E])
    wq = sb("p3_wq", [P, EC, H, D2])
    wq_all = sb("p3_wq_all", [P, EC, E])
    wk = sb("p3_wk", [P, EC, P])
    wv = sb("p3_wv", [P, EC, P])
    qb = sb("p3_qb", [P, 1])
    kb = sb("p3_kb", [P, 1])
    vb = sb("p3_vb", [P, P])
    on = sb("p3_on", [P, EC, TILE])
    xg = sb("p3_xg", [P, BLK, E])
    x1 = [sb(f"p3_x1_{k}", [P, BLK, E]) for k in range(2)]
    gh = [sb(f"p3_gh{k}", [P, EC, TILE]) for k in range(2)]
    qk = [sb(f"p3_qk{c}", [P, TILE]) for c in range(2)]
    rest = [sb(f"p3_rest{c}", [P, TILE]) for c in range(2)]
    parts = [[sb(f"p3_part{k}{c}", [P, 3, TILE], BF16) for c in range(2)] for k in range(2)]
    v = [sb(f"p3_v{k}", [P, UPB, BLK, HQ, D2 + 1]) for k in range(2)]

    NLOAD = 16 * 6
    loaded_out = pr.sem("p3_loaded_out")
    loaded = pr.sem("p3_loaded")
    filled = pr.sem("p3_filled")
    picked = pr.sem("p3_picked")
    tile_in = [pr.counter(f"p3_tile_in{k}", 48) for k in range(2)]
    gate_in = pr.counter("p3_gate_in", 16)
    gated = pr.counter("p3_gated", 2)
    xg_ready = pr.counter("p3_xg_ready", 1)
    on_ready = pr.counter("p3_on_ready", 1)
    out_sum = pr.counter("p3_out_sum", 1)
    x1_ready = pr.counter("p3_x1_ready", 1)
    q_sum = pr.counter("p3_q_sum", 1)
    k_sum = pr.counter("p3_k_sum", 1)
    v_sum = pr.counter("p3_v_sum", 1)
    v_ready = pr.counter("p3_v_ready", 1, credit=1)
    gh_ready = pr.counter("p3_gh_ready", EC, credit=1)
    casts = pr.steps("p3_casts", ("q", "cast0_q", "k", "cast0_k", "cast1_q", "cast1_k", "cast2_q", "cast2_k"), credit=1)
    less = pr.steps("p3_less", ("less0_q", "less0_k", "less1_q", "less1_k"), credit=1)
    x1_out = [pr.counter(f"p3_x1_out{k}", 16, credit=1) for k in range(2)]
    out = [pr.counter(f"p3_out{k}", 64, credit=1) for k in range(2)]

    def pairs_of_tiles(engine, body):
        with engine.Fori(0, B - 2) as b:
            body(b, 2)
        body(B - 2, 1)
        body(B - 1, 0)

    def out_written(sp, b):
        for k in range(2):
            sp.wait_ge(x1_out[k].sem, x1_out[k].at(b, 16))
            sp.wait_ge(out[k].sem, out[k].at(b, 64))

    def out_free(pe):
        pe.wait_ge(v_ready.sem, v_ready.at(TILES - 1, 1))
        pe.wait_ge(casts.sem, casts.after(TILES - 1, "cast0_k"))

    def load(sp, b, k):
        tok, sem = bass.ds(b * S + k * TILE, TILE), tile_in[k].sem
        sp.dma_start(o[k][:], pr.o1[:, tok].rearrange("(c p) t -> p c t", p=P)).then_inc(sem, 16)
        flat = pr.rden1.rearrange("h d t -> (h d) t")
        sp.dma_start(rden[k][:], flat[:, tok].rearrange("(c p) t -> p c t", p=P)).then_inc(sem, 16)
        sp.dma_start(x[k][:], a["L0_attn_x"][bass.ds(b, 1), k * TILE:(k + 1) * TILE, :]
                     .rearrange("b (n p) e -> p (b n) e", p=P)).then_inc(sem, 16)

    def load_gate(sp, b):
        sp.dma_start(gate[:], pr.mod_row[bass.ds(b, 1), GA, :].broadcast_to([P, E])).then_inc(gate_in.sem, 16)

    def preload(sp, written):
        for s in x1_out + out:
            s.open(sp)
        written(sp, 0)
        load_gate(sp, 0)
        sp.dma_start(wout[:], a["L0_attn_Wout"].rearrange("(k p) n -> p k n", p=P)).then_inc(loaded_out, 16)
        sp.dma_start(bout[:], a["L0_attn_bout"].partition_broadcast(P)).then_inc(loaded_out, 16)
        load(sp, 0, 0)
        sp.dma_start(wq_all[:], a["L0_ffn_q_w"].rearrange("(k p) n -> p k n", p=P)).then_inc(loaded, 16)
        sp.dma_start(wk[:], a["L0_ffn_k_w"].rearrange("(k p) n -> p k n", p=P)).then_inc(loaded, 16)
        sp.dma_start(wv[:], a["L0_ffn_v_w"].rearrange("(k p) n -> p k n", p=P)).then_inc(loaded, 16)
        sp.dma_start(kb[:], a["L0_ffn_k_b"].unsqueeze(1)).then_inc(loaded, 16)
        sp.dma_start(vb[:], a["L0_ffn_v_b"].partition_broadcast(P)).then_inc(loaded, 16)
        sp.dma_start(qb[:], pr.qb.unsqueeze(1)).then_inc(loaded, 16)
        load(sp, 0, 1)

    def resume(sp):
        sp.wait_ge(gated.sem, gated.at(0, 2))
        load_gate(sp, 1)
        sp.wait_ge(on_ready.sem, on_ready.at(0, 1))
        sp.wait_ge(xg_ready.sem, xg_ready.at(0, 1))
        load(sp, 1, 0)

    def emit(block, written, free, late, preload_next):
        @block.sync
        def _(sp):
            def store_x1(b, k):
                sp.wait_ge(x1_ready.sem, x1_ready.at(b * TPB + k, 1))
                sp.dma_start(pr.x1[bass.ds(b * S + k * TILE, TILE), :].rearrange("(n p) e -> p n e", p=P),
                             x1[k][:]).then_inc(x1_out[k].sem, 16)

            store_x1(0, 0)

            def pair(b, left):
                for k in range(TPB):
                    n = b * TPB + k
                    tok = bass.ds(b * S + k * TILE, TILE)
                    sem = out[k].sem
                    if left > k:
                        sp.wait_ge(on_ready.sem, on_ready.at(n + 1, 1))
                        sp.wait_ge(xg_ready.sem, xg_ready.at(n + 1, 1))
                        load(sp, b + 1 + k, 1 - k)
                    if k == 1 and left == 2:
                        sp.wait_ge(gated.sem, gated.at(b + 1, 2))
                        load_gate(sp, b + 2)
                    if k == 0 or left:
                        store_x1(b + k, 1 - k)
                    sp.wait_ge(v_ready.sem, v_ready.at(n, 1))
                    sp.wait_ge(gh_ready.sem, gh_ready.at(n, EC))
                    sp.wait_ge(casts.sem, casts.after(n, "cast2_k"))
                    sp.dma_start(pr.v2[bass.ds(b, 1), :, :, k * BLK:(k + 1) * BLK].rearrange("b g p n j d -> p (b g) (n j d)"),
                                 v[k][:].rearrange("p g n j d -> p g (n j d)")).then_inc(sem, 16)
                    sp.dma_start(pr.gh[:, tok].rearrange("(c p) t -> p c t", p=P), gh[k][:]).then_inc(sem, 16)
                    sp.dma_start(pr.q2[:, :, tok].rearrange("s p t -> p s t"), parts[k][0][:]).then_inc(sem, 16)
                    sp.dma_start(pr.k2[:, :, tok].rearrange("s p t -> p s t"), parts[k][1][:]).then_inc(sem, 16)

            with sp.Fori(0, B - 2) as b:
                pair(b, 2)
            pair(B - 2, 1)
            preload_next(sp, out_written)
            pair(B - 1, 0)

        @block.gpsimd
        def _(pool):
            pool.wait_ge(loaded_out, 32)
            pool.memset(norm.power[:], -0.5).then_inc(filled, 1)
            for k in range(2):
                pool.memset(v[k][:], 1.0).then_inc(filled, 1)
            pool.wait_ge(filled, 3)

            def scale(b):
                pool.wait_ge(gate_in.sem, gate_in.at(b, 16))
                pool.tensor_tensor(gwout[:], wout[:], gate[:].unsqueeze(1).broadcast_to([P, EC, E]),
                                   ALU.mult).then_inc(gated.sem, 1)
                pool.tensor_tensor(gbias[:], bout[:], gate[:], ALU.mult).then_inc(gated.sem, 1)

            def with_bias(b, k):
                pool.wait_ge(tile_in[k].sem, tile_in[k].at(b, 48))
                pool.wait_ge(gated.sem, gated.at(b, 2))
                pool.tensor_tensor(xg[:], x[k][:], gbias[:].unsqueeze(1).broadcast_to([P, BLK, E]),
                                   ALU.add).then_inc(xg_ready.sem, 1)

            scale(0)
            with_bias(0, 0)
            norm.pool(pool, 0)
            pool.wait_ge(x1_ready.sem, x1_ready.at(0, 1))
            with_bias(0, 1)

            def pair(b, left):
                for k in range(TPB):
                    n = b * TPB + k
                    if k == 0 or left:
                        norm.pool(pool, n + 1)
                    if left:
                        if k == 0:
                            pool.wait_ge(x1_ready.sem, x1_ready.at(n + 1, 1))
                            pool.wait_ge(xg_ready.sem, xg_ready.at(n + 1, 1))
                            scale(b + 1)
                        pool.wait_ge(x1_ready.sem, x1_ready.at(n + 1, 1))
                        with_bias(b + 1, k)

            pairs_of_tiles(pool, pair)

        @block.scalar
        def _(act):
            norm.open(act, "act")
            casts.open(act)
            gh_ready.open(act)
            act.wait_ge(loaded, NLOAD)

            def modulate(b, k):
                n = b * TPB + k
                act.wait_ge(gh_ready.sem, gh_ready.at(n - 1, EC))
                norm.act(act, n, b)

            def gate_h(b, k):
                n = b * TPB + k
                act.wait_ge(out[k].sem, out[k].at(b - 1, 64))
                act.wait_ge(norm.h_ready.sem, norm.h_ready.at(n, EC))
                for c in range(EC):
                    act.activation(gh[k][:, c, :], norm.hT[:, c, :], ACT.Identity,
                                   scale=pr.mod_of(b, GB * EC + c)).then_inc(gh_ready.sem, 1)

            modulate(0, 0)
            gate_h(0, 0)

            def pair(b, left):
                for k in range(TPB):
                    n = b * TPB + k
                    more = k == 0 or left

                    def cast(part, c):
                        act.wait_ge(less.sem, less.after(n, f"less{part - 1}_{'qk'[c]}"))
                        act.copy(parts[k][c][:, part, :], rest[c][:]).then_inc(casts.sem, 1)

                    act.wait_ge(out[k].sem, out[k].at(b - 1, 64))
                    act.wait_ge(less.sem, less.after(n - 1, "less0_k"))
                    for c, (total, bias) in enumerate(((q_sum, qb), (k_sum, kb))):
                        act.wait_ge(total.sem, total.at(n, 1))
                        for to in (qk[c][:], parts[k][c][:, 0, :]):
                            act.activation(to, pr.bank[:, 4 + c, :], ACT.Identity, bias=bias[:, 0:1]).then_inc(casts.sem, 1)
                    cast(1, 0)
                    cast(1, 1)
                    if more:
                        modulate(b + k, 1 - k)
                    cast(2, 0)
                    cast(2, 1)
                    if more:
                        gate_h(b + k, 1 - k)

            pairs_of_tiles(act, pair)

        @block.vector
        def _(dve):
            v_ready.open(dve)
            less.open(dve)

            def divide(b, k):
                n = b * TPB + k
                dve.wait_ge(tile_in[k].sem, tile_in[k].at(b, 48))
                dve.tensor_tensor(on[:], o[k][:], rden[k][:], ALU.mult).then_inc(on_ready.sem, 1)

            def residual(b, k):
                n = b * TPB + k
                dve.wait_ge(xg_ready.sem, xg_ready.at(n, 1))
                dve.wait_ge(x1_out[k].sem, x1_out[k].at(b - 1, 16))
                dve.wait_ge(out_sum.sem, out_sum.at(n, 1))
                dve.tensor_tensor(x1[k][:], pr.bank[:, 2:4, :].rearrange("p a (n e) -> p (a n) e", e=E), xg[:],
                                  ALU.add).then_inc(x1_ready.sem, 1)
                dve.wait_ge(x1_ready.sem, x1_ready.at(n, 1))
                norm.statistics(dve, n, x1[k])

            divide(0, 0)
            residual(0, 0)
            divide(0, 1)
            norm.normalise(dve, 0, x1[0])
            late(dve)
            dve.wait_ge(loaded, NLOAD)
            dve.wait_ge(filled, 3)
            dve.tensor_copy(wq[:], wq_all[:].rearrange("p k (h d) -> p k h d", d=D1)[:, :, :, 0:D2]).then_inc(picked, 1)

            def pair(b, left):
                for k in range(TPB):
                    n = b * TPB + k
                    if k == 0 or left:
                        residual(b + k, 1 - k)
                        if left:
                            divide(b + 1, k)
                        norm.normalise(dve, n + 1, x1[1 - k])
                    for part in range(2):
                        for c in range(2):
                            if part == 0:
                                dve.wait_ge(casts.sem, casts.after(n - 1, f"cast2_{'qk'[c]}"))
                            dve.wait_ge(casts.sem, casts.after(n, f"cast{part}_{'qk'[c]}"))
                            dve.tensor_tensor(rest[c][:], (rest if part else qk)[c][:], parts[k][c][:, part, :],
                                              ALU.subtract).then_inc(less.sem, 1)
                    dve.wait_ge(out[k].sem, out[k].at(b - 1, 64))
                    dve.wait_ge(v_sum.sem, v_sum.at(n, 1))
                    for i in range(BLK):
                        op = dve.tensor_tensor(v[k][:, :, i, :, 0:D2],
                                               pr.bank[:, 6, i * P:(i + 1) * P].rearrange("p (g j d) -> p g j d", g=UPB, j=HQ),
                                               vb[:].rearrange("p (g j d) -> p g j d", g=UPB, j=HQ), ALU.add)
                    op.then_inc(v_ready.sem, 1)

            pairs_of_tiles(dve, pair)

        @block.tensor
        def _(pe):
            norm.open(pe, "pe")

            def project(b, k):
                n = b * TPB + k
                if k == 0:
                    pe.wait_ge(gated.sem, gated.at(b, 1))
                pe.wait_ge(on_ready.sem, on_ready.at(n, 1))
                for i in range(BLK):
                    to = pr.bank[:, 2 + i // 2, (i % 2) * E:(i % 2 + 1) * E]
                    for c in range(EC):
                        mm = pe.matmul(to, on[:, c, i * P:(i + 1) * P], gwout[:, c, :],
                                       start=(c == 0), stop=(c == EC - 1), skip_group_check=True)
                mm.then_inc(out_sum.sem, 1)

            free(pe)
            project(0, 0)
            pe.wait_ge(loaded, NLOAD)
            pe.wait_ge(picked, 1)

            def pair(b, left):
                for k in range(TPB):
                    n = b * TPB + k
                    pe.wait_ge(norm.h_ready.sem, norm.h_ready.at(n - 1, EC))
                    norm.pe(pe, n)
                    if k == 0 or left:
                        project(b + k, 1 - k)
                    pe.wait_ge(norm.h_ready.sem, norm.h_ready.at(n, EC))
                    pe.wait_ge(casts.sem, casts.after(n - 1, "cast0_k"))
                    for i, (w, total) in enumerate(((wq[:].rearrange("p k h d -> p k (h d)"), q_sum), (wk[:], k_sum))):
                        for c in range(EC):
                            mm = pe.matmul(pr.bank[:, 4 + i, :], w[:, c, :], norm.hT[:, c, :],
                                           start=(c == 0), stop=(c == EC - 1))
                        mm.then_inc(total.sem, 1)
                    pe.wait_ge(v_ready.sem, v_ready.at(n - 1, 1))
                    for i in range(BLK):
                        for c in range(EC):
                            mm = pe.matmul(pr.bank[:, 6, i * P:(i + 1) * P], norm.hT[:, c, i * P:(i + 1) * P], wv[:, c, :],
                                           start=(c == 0), stop=(c == EC - 1), skip_group_check=True)
                    mm.then_inc(v_sum.sem, 1)

            pairs_of_tiles(pe, pair)

        def out_late(dve):
            pass

        return out_written, out_free, out_late

    return preload, resume, emit


def route(pr, place):
    nc, a = pr.nc, pr.a
    NB = TILES * BLK
    def sb(name, shape, dt=F32):
        return place(name, shape, dt)

    o = [sb(f"p5_o{k}", [P, TILE]) for k in range(2)]
    rden = [sb(f"p5_rden{k}", [P, TILE]) for k in range(2)]
    on = [sb(f"p5_on{k}", [P, TILE]) for k in range(2)]
    wo = sb("p5_wo", [P, E])
    ob = sb("p5_ob", [P, EC])
    wr = sb("p5_wr", [P, EC, NX])
    rb = sb("p5_rb", [P, NX])
    mla = [sb(f"p5_mla{k}", [P, EC, TILE]) for k in range(2)]
    logit = sb("p5_logit", [P, NB, NX])
    prob = sb("p5_prob", [P, NB, NX])
    rank = sb("p5_rank", [P, NX])
    tmp = sb("p5_tmp", [P, NB, NX])
    first = sb("p5_first", [P, NB, NX])
    second = sb("p5_second", [P, NB, NX])
    top1 = sb("p5_top1", [P, NB])
    top2 = sb("p5_top2", [P, NB])
    best = sb("p5_best", [P, NB])
    total = sb("p5_total", [P, NB])
    comb = sb("p5_comb", [P, TILES, NX, BLK])
    combT = sb("p5_combT", [BLK * NX, TILES, P])
    sums = [pr.bank[:, 2 * k:2 * k + 2, :] for k in range(2)]
    logits = [pr.bank[:, 4 + k, 0:BLK * NX] for k in range(2)]

    loaded = pr.sem("p5_loaded")
    ranked = pr.sem("p5_ranked")
    tile_in = [pr.counter(f"p5_tile_in{k}", 32) for k in range(2)]
    on_ready = pr.counter("p5_on_ready", 1)
    mla_sum = pr.counter("p5_mla_sum", EC, credit=2)
    mla_ready = pr.counter("p5_mla_ready", EC, credit=2)
    logit_sum = pr.counter("p5_logit_sum", 1, credit=2)
    logit_ready = pr.counter("p5_logit_ready", 1, credit=2)
    stored = [pr.counter(f"p5_stored{k}", 16, credit=1) for k in range(2)]
    step = pr.sem("p5_step")
    exps = pr.sem("p5_exps")
    weighted = pr.sem("p5_weighted")
    turned = pr.sem("p5_turned")
    comb_ready = pr.sem("p5_comb_ready")
    comb_out = pr.sem("p5_comb_out")

    def mla_written(sp, b):
        for k in range(2):
            sp.wait_ge(stored[k].sem, stored[k].at(b, 16))

    def load(sp, b, k):
        tok, sem = bass.ds(b * S + k * TILE, TILE), tile_in[k].sem
        sp.dma_start(o[k][:], pr.o2[:, tok]).then_inc(sem, 16)
        sp.dma_start(rden[k][:], pr.rden2.rearrange("h d t -> (h d) t")[:, tok]).then_inc(sem, 16)

    def preload(sp, written):
        written(sp, 0)
        load(sp, 0, 0)
        for s in stored:
            s.open(sp)
        sp.dma_start(wo[:], a["L0_ffn_o_w"][0:P, :]).then_inc(loaded, 16)
        for c in range(EC):
            sp.dma_start(ob[:, c:c + 1], a["L0_ffn_o_b"][c * P:(c + 1) * P].unsqueeze(1)).then_inc(loaded, 16)
        sp.dma_start(wr[:], a["L0_ffn_router_w"].rearrange("(k p) n -> p k n", p=P)).then_inc(loaded, 16)
        sp.dma_start(rb[:], a["L0_ffn_router_b"].partition_broadcast(P)).then_inc(loaded, 16)
        load(sp, 0, 1)

    def resume(sp):
        for k in range(TPB):
            sp.wait_ge(on_ready.sem, on_ready.at(k, 1))
            load(sp, 1, k)

    def emit(block, written, free, late, preload_next, prepare):
        @block.sync
        def _(sp):
            def pair(b, left):
                for k in range(TPB):
                    n = b * TPB + k
                    if left > 1:
                        sp.wait_ge(on_ready.sem, on_ready.at(n + TPB, 1))
                        load(sp, b + 2, k)
                    sp.wait_ge(mla_ready.sem, mla_ready.at(n, EC))
                    sp.dma_start(pr.mla[:, bass.ds(b * S + k * TILE, TILE)].rearrange("(c p) t -> p c t", p=P),
                                 mla[k][:]).then_inc(stored[k].sem, 16)

            with sp.Fori(0, B - 2) as b:
                pair(b, 2)
            pair(B - 2, 1)
            preload_next(sp, mla_written)
            pair(B - 1, 0)
            for k in range(2):
                sp.wait_ge(stored[k].sem, stored[k].at(B - 1, 16))
            sp.wait_ge(comb_ready, 1)
            sp.dma_start(pr.comb.rearrange("n e (b t) -> (e b) n t", b=BLK), combT[:]).then_inc(comb_out, 16)
            sp.wait_ge(comb_out, 16)

        @block.gpsimd
        def _(pool):
            pool.wait_ge(loaded, 80)
            for e in range(NX):
                op = pool.memset(rank[:, e:e + 1], float(NX - e))
            op.then_inc(ranked, 1)

        @block.scalar
        def _(act):
            mla_ready.open(act)
            act.wait_ge(loaded, 80)

            def pair(b, last):
                for k in range(TPB):
                    n = b * TPB + k
                    act.wait_ge(logit_sum.sem, logit_sum.at(n - 2, 1))
                    act.wait_ge(stored[k].sem, stored[k].at(b - 1, 16))
                    for c in range(EC):
                        act.wait_ge(mla_sum.sem, mla_sum.at(n, c + 1))
                        act.activation(mla[k][:, c, :], sums[k][:, c, :], ACT.Identity,
                                       bias=ob[:, c:c + 1]).then_inc(mla_ready.sem, 1)

            with act.Fori(0, B - 1) as b:
                pair(b, False)
            pair(B - 1, True)
            prepare(act)
            act.wait_ge(step, 2)
            act.activation(prob[:], logit[:], ACT.Exp).then_inc(exps, 1)

        @block.vector
        def _(dve):
            logit_ready.open(dve)
            dve.wait_ge(loaded, 80)

            def divide(b, k):
                dve.wait_ge(tile_in[k].sem, tile_in[k].at(b, 32))
                dve.wait_ge(mla_sum.sem, mla_sum.at(b * TPB + k - 2, EC))
                dve.tensor_tensor(on[k][:], o[k][:], rden[k][:], ALU.mult).then_inc(on_ready.sem, 1)

            divide(0, 0)
            divide(0, 1)
            late(dve)

            def pair(b, last):
                for k in range(TPB):
                    n = b * TPB + k
                    if not last:
                        divide(b + 1, k)
                    dve.wait_ge(logit_sum.sem, logit_sum.at(n, 1))
                    dve.tensor_tensor(logit[:, bass.ds(n * BLK, BLK), :], logits[k].rearrange("p (b e) -> p b e", e=NX),
                                      rb[:].unsqueeze(1).broadcast_to([P, BLK, NX]), ALU.add).then_inc(logit_ready.sem, 1)

            in_pairs(dve, TILES, pair)
            dve.wait_ge(logit_ready.sem, logit_ready.at(TILES - 1, 1))
            dve.wait_ge(ranked, 1)

            def wide(t):
                return t[:].unsqueeze(2).broadcast_to([P, NB, NX])

            dve.tensor_reduce(best[:], logit[:], AX.X, ALU.max).then_inc(step, 1)
            dve.wait_ge(step, 1)
            dve.tensor_tensor(logit[:], logit[:], wide(best), ALU.subtract).then_inc(step, 1)
            dve.wait_ge(exps, 1)
            dve.tensor_reduce(total[:], prob[:], AX.X, ALU.add).then_inc(step, 1)
            dve.wait_ge(step, 3)
            dve.reciprocal(total[:], total[:]).then_inc(step, 1)
            dve.wait_ge(step, 4)
            dve.tensor_tensor(prob[:], prob[:], wide(total), ALU.mult).then_inc(step, 1)
            at = 5
            for value, choice in ((top1, first), (top2, second)):
                dve.wait_ge(step, at)
                dve.tensor_reduce(value[:], prob[:], AX.X, ALU.max).then_inc(step, 1)
                dve.wait_ge(step, at + 1)
                dve.tensor_tensor(tmp[:], prob[:], wide(value), ALU.is_equal).then_inc(step, 1)
                dve.wait_ge(step, at + 2)
                dve.tensor_tensor(tmp[:], tmp[:], rank[:].unsqueeze(1).broadcast_to([P, NB, NX]), ALU.mult).then_inc(step, 1)
                dve.wait_ge(step, at + 3)
                dve.tensor_reduce(best[:], tmp[:], AX.X, ALU.max).then_inc(step, 1)
                dve.wait_ge(step, at + 4)
                dve.tensor_tensor(choice[:], tmp[:], wide(best), ALU.is_equal).then_inc(step, 1)
                dve.wait_ge(step, at + 5)
                dve.scalar_tensor_tensor(out=prob[:], in0=choice[:], scalar=-2.0, in1=prob[:],
                                         op0=ALU.mult, op1=ALU.add).then_inc(step, 1)
                at += 6
            dve.wait_ge(step, at)
            dve.scalar_tensor_tensor(out=total[:], in0=top1[:], scalar=1e-8, in1=top2[:],
                                     op0=ALU.add, op1=ALU.add).then_inc(step, 1)
            dve.wait_ge(step, at + 1)
            dve.reciprocal(total[:], total[:]).then_inc(step, 1)
            dve.wait_ge(step, at + 2)
            dve.tensor_tensor(top1[:], top1[:], total[:], ALU.mult).then_inc(step, 1)
            dve.tensor_tensor(top2[:], top2[:], total[:], ALU.mult).then_inc(step, 1)
            dve.wait_ge(step, at + 4)
            dve.tensor_tensor(first[:], first[:], wide(top1), ALU.mult).then_inc(step, 1)
            dve.tensor_tensor(second[:], second[:], wide(top2), ALU.mult).then_inc(step, 1)
            dve.wait_ge(step, at + 6)
            dve.tensor_tensor(comb[:].rearrange("p n e b -> p n b e"),
                              first[:].rearrange("p (n b) e -> p n b e", b=BLK),
                              second[:].rearrange("p (n b) e -> p n b e", b=BLK), ALU.add).then_inc(weighted, 1)
            dve.wait_ge(turned, 1)
            dve.tensor_copy(combT[:], pr.bank[0:BLK * NX, 6:8, :].rearrange("q a (n t) -> q (a n) t", t=P)).then_inc(comb_ready, 1)

        @block.tensor
        def _(pe):
            mla_sum.open(pe)
            logit_sum.open(pe)
            pe.wait_ge(loaded, 80)

            def project(n, k):
                pe.wait_ge(on_ready.sem, on_ready.at(n, 1))
                pe.wait_ge(mla_ready.sem, mla_ready.at(n - 2, EC))
                for c in range(EC):
                    pe.matmul(sums[k][:, c, :], wo[:, c * P:(c + 1) * P], on[k][:], start=True,
                              stop=True).then_inc(mla_sum.sem, 1)

            free(pe)
            project(0, 0)

            def pair(b, last):
                for k in range(TPB):
                    n = b * TPB + k
                    if k == 0 or not last:
                        project(n + 1, 1 - k)
                    pe.wait_ge(mla_ready.sem, mla_ready.at(n, EC))
                    pe.wait_ge(logit_ready.sem, logit_ready.at(n - 2, 1))
                    for i in range(BLK):
                        for c in range(EC):
                            mm = pe.matmul(logits[k][:, i * NX:(i + 1) * NX], mla[k][:, c, i * P:(i + 1) * P], wr[:, c, :],
                                           start=(c == 0), stop=(c == EC - 1), skip_group_check=True)
                    mm.then_inc(logit_sum.sem, 1)

            in_pairs(pe, TILES, pair)
            pe.wait_ge(logit_ready.sem, logit_ready.at(TILES - 1, 1))

        def turn(pe):
            pe.wait_ge(weighted, 1)
            for n in range(TILES):
                mm = pe.transpose(pr.bank[0:BLK * NX, 6 + n // 4, (n % 4) * P:(n % 4 + 1) * P],
                                  comb[:, n].rearrange("p e b -> p (e b)"), pr.ident[:])
            mm.then_inc(turned, 1)

        def turn_read(pe):
            pe.wait_ge(comb_ready, 1)

        return turn, turn_read

    return preload, resume, emit


def experts(pr, place):
    nc, a = pr.nc, pr.a
    NB = S // P
    def sb(name, shape, dt=F32):
        return place(name, shape, dt)

    raw = sb("p6_raw", [P, EC, S])
    x = [sb(f"p6_x{t}", [P, 2, EC, S], F32R) for t in range(2)]
    w = [[sb(f"p6_w{j}{k}", [P, EC * FF]) for j in (1, 2)] for k in range(2)]
    wp = [[sb(f"p6_wp{j}{k}", [P, 2, EC * FF], F32R) for j in (1, 2)] for k in range(2)]
    comb = [sb(f"p6_comb{k}", [P, TPB, TILE]) for k in range(2)]
    g = [sb(f"p6_g{f}", [P, S]) for f in range(2)]
    hid = [sb(f"p6_hid{f}", [P, 2, S], F32R) for f in range(FC)]
    z = [sb(f"p6_z{c}", [P, S]) for c in range(EC)]
    acc = sb("p6_acc", [P, EC, S])
    gh = sb("p6_gh", [P, EC, S])
    x1 = sb("p6_resid", [P, NB, E])

    bank1 = [pr.bank[:, 2 * q:2 * q + 2, :] for q in range(2)]
    bank2 = [pr.bank[:, 4 + 2 * c:6 + 2 * c, :] for c in range(EC)]

    raw_in = pr.counter("p6_raw_in", 16)
    x_hi = pr.counter("p6_x_hi", EC)
    x_lo = pr.counter("p6_x_lo", EC)
    w_in = [pr.counter(f"p6_w_in{k}", 32) for k in range(2)]
    comb_in = [pr.counter(f"p6_comb_in{k}", 16) for k in range(2)]
    end_in = pr.counter("p6_end_in", 32)
    w_hi = pr.counter("p6_w_hi", 2)
    w_lo = pr.counter("p6_w_lo", 2)
    sum1 = pr.counter("p6_sum1", FC)
    gelu = pr.counter("p6_gelu", FC, credit=1)
    hi = pr.counter("p6_hi", FC)
    lo = pr.counter("p6_lo", FC, credit=1)
    sum2 = pr.counter("p6_sum2", FC, credit=2)
    weigh = pr.counter("p6_weigh", 2 * EC, credit=2)
    final = pr.counter("p6_final", TPB * EC)
    turned = pr.counter("p6_turned", 2)
    done = pr.counter("p6_done", 2)
    stored = pr.counter("p6_stored", 32)

    def visits(engine, visit):
        for b in range(B):
            for k in range(2):
                visit(b, 0, k, True)
            with engine.Fori(1, NX // 2) as j:
                for k in range(2):
                    visit(b, j, k, False)

    def load_raw(sp, b):
        sp.dma_start(raw[:], pr.mla[:, b * S:(b + 1) * S].rearrange("(c p) t -> p c t", p=P)).then_inc(raw_in.sem, 16)

    def load_weights(sp, e, k):
        for n, name in enumerate(("L0_ffn_w1", "L0_ffn_w2")):
            sp.dma_start(w[k][n][:], a[name][bass.ds(e, 1)].rearrange("x (k p) n -> p (x k) n", p=P)).then_inc(w_in[k].sem, 16)

    def preload(sp, written):
        written(sp, 0)
        load_raw(sp, 0)
        load_weights(sp, 0, 0)
        load_weights(sp, 1, 1)

    def cut(act, b, c):
        act.wait_ge(raw_in.sem, raw_in.at(b, 16))
        if b > 1:
            act.wait_ge(sum2.sem, sum2.at((b - 1) * NX - 1, FC))
        act.copy(x[b % 2][:, 0, c], raw[:, c]).then_inc(x_hi.sem, 1)

    def cut_weights(act, v, k, pair):
        act.wait_ge(w_in[k].sem, w_in[k].at(pair, 32))
        if not isinstance(v, int) or v > 1:
            act.wait_ge(sum2.sem, sum2.at(v - 2, FC))
        for n in range(2):
            act.copy(wp[k][n][:, 0], w[k][n][:]).then_inc(w_hi.sem, 1)

    def prepare(act):
        cut(act, 0, 0)
        cut(act, 0, 1)
        cut_weights(act, 0, 0, 0)

    def emit(block, turn_weights, turn_read):
        @block.sync
        def _(sp):
            def load_end(b):
                tok = slice(b * S, (b + 1) * S)
                sp.dma_start(gh[:], pr.gh[:, tok].rearrange("(c p) t -> p c t", p=P)).then_inc(end_in.sem, 16)
                sp.dma_start(x1[:], pr.x1[tok, :].rearrange("(n p) e -> p n e", p=P)).then_inc(end_in.sem, 16)

            def store(b):
                for q in range(2):
                    sp.wait_ge(done.sem, done.at(b, q + 1))
                    blocks = slice(q * NB // 2, (q + 1) * NB // 2)
                    sp.dma_start(a["out"][b].rearrange("(n p) e -> p n e", p=P)[:, blocks], x1[:, blocks]).then_inc(stored.sem, 16)
                sp.wait_ge(stored.sem, stored.at(b, 32))

            def visit(b, j, k, first):
                v, e = b * NX + j * 2 + k, j * 2 + k
                if not first or b > 0:
                    sp.wait_ge(weigh.sem, weigh.at(v - 1, 0))
                    load_weights(sp, e, k)
                sp.dma_start(comb[k][:], pr.comb[bass.ds(b * TPB, TPB), bass.ds(e, 1), :]
                             .rearrange("n e t -> e n t").broadcast_to([P, TPB, TILE])).then_inc(comb_in[k].sem, 16)
                if first and k == 0 and b < B - 1:
                    sp.wait_ge(x_hi.sem, x_hi.at(b, EC))
                    sp.wait_ge(x_lo.sem, x_lo.at(b, EC))
                    load_raw(sp, b + 1)
                if first and k == 1:
                    if b > 0:
                        sp.wait_ge(turned.sem, turned.at(b - 1, 2))
                        store(b - 1)
                    load_end(b)

            visits(sp, visit)
            store(B - 1)

        @block.gpsimd
        def _(pool):
            def cut(b, c):
                pool.wait_ge(x_hi.sem, x_hi.at(b, c + 1))
                pool.tensor_tensor(x[b % 2][:, 1, c], raw[:, c], x[b % 2][:, 0, c].bitcast(F32), ALU.subtract).then_inc(x_lo.sem, 1)

            cut(0, 0)
            cut(0, 1)

            def visit(b, j, k, first):
                v = b * NX + j * 2 + k
                for n in range(2):
                    pool.wait_ge(w_hi.sem, w_hi.at(v, n + 1))
                    pool.tensor_tensor(wp[k][n][:, 1], w[k][n][:], wp[k][n][:, 0].bitcast(F32), ALU.subtract).then_inc(w_lo.sem, 1)
                if first and b < B - 1:
                    cut(b + 1, k)

            visits(pool, visit)

        @block.scalar
        def _(act):
            gelu.open(act)

            def visit(b, j, k, first):
                v, pair = b * NX + j * 2 + k, b * (NX // 2) + j
                if not first or b + k > 0:
                    cut_weights(act, v, k, pair)
                for f in range(FC):
                    act.wait_ge(sum1.sem, sum1.at(v, f + 1))
                    if not first or b + k > 0 or f > 1:
                        act.wait_ge(lo.sem, lo.at(v, f - 1))
                    act.activation(g[f % 2][:], bank1[f % 2].rearrange("p a t -> p (a t)"), ACT.Gelu,
                                   bias=pr.bias[:, bass.ds((j * 2 + k) * FC + f, 1)]).then_inc(gelu.sem, 1)
                    act.wait_ge(sum2.sem, sum2.at(v - 1, f + 1))
                    act.wait_ge(gelu.sem, gelu.at(v, f + 1))
                    act.copy(hid[f][:, 0], g[f % 2][:]).then_inc(hi.sem, 1)
                if first and b < B - 1:
                    cut(act, b + 1, k)

            visits(act, visit)

        @block.vector
        def _(dve):
            lo.open(dve)
            weigh.open(dve)

            def combine(b):
                dve.wait_ge(end_in.sem, end_in.at(b, 32))
                dve.wait_ge(weigh.sem, weigh.at(b * NX + NX - 1, 2 * EC))
                for h in range(TPB):
                    tok = slice(h * TILE, (h + 1) * TILE)
                    for c in range(EC):
                        dve.scalar_tensor_tensor(out=gh[:, c, tok], in0=acc[:, c, tok],
                                                 scalar=pr.mod[:, b, GB3 * EC + c:GB3 * EC + c + 1],
                                                 in1=gh[:, c, tok], op0=ALU.mult, op1=ALU.add).then_inc(final.sem, 1)

            def finish(b):
                for q in range(2):
                    dve.wait_ge(turned.sem, turned.at(b, q + 1))
                    part = x1[:, q * NB // 2:(q + 1) * NB // 2, :]
                    dve.tensor_tensor(part, bank2[q].rearrange("p a (n e) -> p (a n) e", e=E), part,
                                      ALU.add).then_inc(done.sem, 1)

            def visit(b, j, k, first):
                v, pair = b * NX + j * 2 + k, b * (NX // 2) + j
                opening = first and k == 0
                if opening and b > 0:
                    combine(b - 1)
                for f in range(FC):
                    if opening and b > 0 and f == 2:
                        finish(b - 1)
                    dve.wait_ge(hi.sem, hi.at(v, f + 1))
                    dve.tensor_tensor(hid[f][:, 1], g[f % 2][:], hid[f][:, 0].bitcast(F32), ALU.subtract).then_inc(lo.sem, 1)
                dve.wait_ge(sum2.sem, sum2.at(v, FC))
                dve.wait_ge(comb_in[k].sem, comb_in[k].at(pair, 16))
                dve.wait_ge(weigh.sem, weigh.at(v - 1, 2 * EC))
                if opening and b > 0:
                    dve.wait_ge(final.sem, final.at(b - 1, TPB * EC))
                weight = comb[k][:].rearrange("p n t -> p (n t)")
                for c in range(EC):
                    dve.scalar_tensor_tensor(out=acc[:, c, :] if opening else z[c][:],
                                             in0=bank2[c].rearrange("p a t -> p (a t)"), scalar=pr.bias[:, bass.ds(NX * FC + (j * 2 + k) * EC + c, 1)],
                                             in1=weight, op0=ALU.add, op1=ALU.mult).then_inc(weigh.sem, 1)
                if opening:
                    dve.wait_ge(weigh.sem, weigh.at(v, EC))
                    dve.sem_inc(weigh.sem, EC)
                else:
                    for c in range(EC):
                        dve.wait_ge(weigh.sem, weigh.at(v, c + 1))
                        dve.tensor_tensor(acc[:, c, :], acc[:, c, :], z[c][:], ALU.add).then_inc(weigh.sem, 1)

            visits(dve, visit)
            combine(B - 1)
            finish(B - 1)

        @block.tensor
        def _(pe):
            sum2.open(pe)

            def turn(b):
                for q in range(2):
                    pe.wait_ge(final.sem, final.at(b, (q + 1) * EC))
                    for n in range(NB // 2):
                        for c in range(EC):
                            s = (q * NB // 2 + n) * P
                            mm = pe.transpose(bank2[q].rearrange("p a (n e) -> p (a n) e", e=E)[:, n, c * P:(c + 1) * P],
                                              gh[:, c, s:s + P], pr.ident[:])
                    mm.then_inc(turned.sem, 1)

            def visit(b, j, k, first):
                v, t = b * NX + j * 2 + k, b % 2
                opening = first and k == 0
                w1 = wp[k][0][:].rearrange("p h (c f m) -> p h c f m", c=EC, f=FC)
                w2 = wp[k][1][:].rearrange("p h (f c m) -> p h f c m", f=FC, c=EC)
                products = ((0, 0), (0, 1), (1, 0))

                def layer1(f):
                    pe.wait_ge(gelu.sem, gelu.at(v, f - 1))
                    for h in range(TPB):
                        for n, (pw, px) in enumerate(products):
                            if f == 0 and h == 0 and px == 1 and opening:
                                pe.wait_ge(x_lo.sem, x_lo.at(b, EC))
                            if f == 0 and h == 0 and pw == 1:
                                pe.wait_ge(w_lo.sem, w_lo.at(v, 1))
                            for c in range(EC):
                                mm = pe.matmul(bank1[f % 2][:, h, :], w1[:, pw, c, f, :],
                                               x[t][:, px, c, h * TILE:(h + 1) * TILE],
                                               start=(n == 0 and c == 0), stop=(n == 2 and c == EC - 1))
                    mm.then_inc(sum1.sem, 1)

                def layer2(f):
                    pe.wait_ge(hi.sem, hi.at(v, f + 1))
                    pe.wait_ge(lo.sem, lo.at(v, f + 1))
                    if f == 0:
                        pe.wait_ge(w_hi.sem, w_hi.at(v, 2))
                        pe.wait_ge(w_lo.sem, w_lo.at(v, 2))
                        pe.wait_ge(weigh.sem, weigh.at(v - 1, EC))
                    for c in range(EC):
                        for h in range(TPB):
                            for n, (pw, px) in enumerate(products):
                                mm = pe.matmul(bank2[c][:, h, :], w2[:, pw, f, c, :],
                                               hid[f][:, px, h * TILE:(h + 1) * TILE],
                                               start=(f == 0 and n == 0), stop=(f == FC - 1 and n == 2),
                                               skip_group_check=True)
                    mm.then_inc(sum2.sem, 1)

                if opening:
                    pe.wait_ge(x_hi.sem, x_hi.at(b, EC))
                pe.wait_ge(w_hi.sem, w_hi.at(v, 1))
                layer1(0)
                layer1(1)
                layer1(2)
                if opening:
                    if b > 0:
                        turn(b - 1)
                    else:
                        turn_weights(pe)
                    layer1(3)
                    if b > 0:
                        pe.wait_ge(done.sem, done.at(b - 1, 2))
                    else:
                        turn_read(pe)
                    layer2(0)
                else:
                    layer2(0)
                    layer1(3)
                layer2(1)
                layer2(2)
                layer2(3)

            visits(pe, visit)
            turn(B - 1)

    return preload, prepare, emit


def build(nc, a):
    with ExitStack() as ctx:
        pr = Program(nc, ctx, a)
        base, top = nc.sbuf_base, nc.sbuf_usable_end
        first = Place(nc, (base, top))
        a1_preload, a1 = attention(pr, first, "a1", pr.q1, pr.k1, pr.v1, pr.o1, pr.den[0], pr.rden1, D1, SIX, True, D1 ** -0.5)
        middle = first.end()
        p1_place, p3_place, p5_place = (Place(nc, (middle, top)) for _ in range(3))
        p3_preload, p3_resume, p3 = between(pr, p3_place)
        a2_preload, a2 = attention(pr, Place(nc, (base, middle), (p3_place.end(), top)), "a2", pr.q2, pr.k2, pr.v2, pr.o2,
                                   pr.den[1], pr.rden2, D2, NINE, False, D2 ** -0.5)
        p5_preload, p5_resume, p5 = route(pr, p5_place)
        p6_preload, p6_prepare, p6 = experts(pr, Place(nc, (base, middle), (p5_place.end(), top)))
        with nc.Block() as block:
            start_dve, start_pe, p1 = from_x(pr, p1_place)
            modulation(pr, p1_place, block, start_dve, start_pe)
            before = p1(block, a1_preload)
            before = a1(block, *before[:2], p3_preload, p3_resume)
            before = p3(block, *before, a2_preload)
            before = a2(block, *before[:2], p5_preload, p5_resume)
            before = p5(block, *before, p6_preload, p6_prepare)
            p6(block, *before)


_INS = ['L0_attn_x', 'L0_attn_Wqa', 'L0_attn_Wqb', 'L0_attn_Wkva', 'L0_attn_Wkvb', 'L0_attn_Wout', 'L0_attn_bout',
        'L0_ffn_q_w', 'L0_ffn_q_b', 'L0_ffn_k_w', 'L0_ffn_k_b', 'L0_ffn_v_w', 'L0_ffn_v_b', 'L0_ffn_o_w',
        'L0_ffn_o_b', 'L0_ffn_router_w', 'L0_ffn_router_b', 'L0_ffn_w1', 'L0_ffn_b1', 'L0_ffn_w2', 'L0_ffn_b2',
        'L0_c', 'L0_wmod']


def rope_tables():
    inv_freq = 1.0 / np.float32(10000.0) ** (np.arange(0, D1, 2, dtype=np.float32) / np.float32(D1))
    angle = np.outer(np.arange(S, dtype=np.float32), inv_freq.astype(np.float32)).astype(np.float32)
    rows = (np.arange(P) % D1) // 2
    return (np.ascontiguousarray(np.cos(angle).T[rows]).astype(np.float32),
            np.ascontiguousarray(np.sin(angle).T[rows]).astype(np.float32))


def kernel(**inputs):
    import concourse.bacc as bacc
    from concourse.bass_utils import run_bass_kernel_spmd

    nc = bacc.Bacc("TRN2", target_bir_lowering=False, num_devices=1)
    arrays = {f"in_{name}": np.ascontiguousarray(inputs[name]) for name in _INS}
    arrays["in_rope_cos"], arrays["in_rope_sin"] = rope_tables()
    a = {name[3:]: nc.dram_tensor(name, v.shape, mybir.dt.from_np(v.dtype), kind="ExternalInput").ap()
         for name, v in arrays.items()}
    a["out"] = nc.dram_tensor("out_0", (B, S, E), F32, kind="ExternalOutput").ap()
    build(nc, a)
    r = run_bass_kernel_spmd(nc, [arrays], core_ids=[0])
    return r.results[0]["out_0"]
```
